# Optimizing a Trainium2 kernel written in Bass

```python
import numpy as np
import jax
import jax.numpy as jnp

def _softmax(x, axis=-1):
    return jax.nn.softmax(x, axis=axis)

def _gelu(x):
    return jax.nn.gelu(x, approximate=True)

def _silu(x):
    return jax.nn.silu(x)

def _sigmoid(x):
    return jax.nn.sigmoid(x)

def _layernorm(x, axis=-1, eps=1e-05):
    m = jnp.mean(x, axis=axis, keepdims=True)
    v = jnp.var(x, axis=axis, keepdims=True)
    return (x - m) / jnp.sqrt(v + eps)

def _scatter_add(tgt, idx, src, axis=0):
    return tgt.at[idx].add(src)

def _segment_sum(src, seg, n):
    return jax.ops.segment_sum(src, seg, n)
kernel_name = 'mk_seq_preln_d1_jaxref_r8_cba4a3'

def setup_inputs(seed: int=0):
    np.random.seed(seed)
    _w = jnp.asarray

    def _L0_attn_setup():
        import jax, jax.numpy as jnp
        import numpy as np
        B, T, C, H = (2, 256, 128, 16)
        DH = C // H
        EPS = 1e-05

        def _rotary(t_len, d_head):
            inv_freq = 1.0 / 10000.0 ** (jnp.arange(0, d_head, 2, dtype=jnp.float32) / d_head)
            t = jnp.arange(t_len, dtype=jnp.float32)
            freqs = t[:, None] * inv_freq[None, :]
            emb = jnp.concatenate([freqs, freqs], axis=-1)
            return (jnp.cos(emb), jnp.sin(emb))

        def _apply_rope(x, cos, sin):
            d = x.shape[-1]
            x1, x2 = (x[..., :d // 2], x[..., d // 2:])
            x_rot = jnp.concatenate([-x2, x1], axis=-1)
            return x * cos + x_rot * sin

        def _decay_mask(t_len, n_head):
            gammas = 1.0 - 2.0 ** (-5.0 - jnp.arange(n_head, dtype=jnp.float32))
            n = jnp.arange(t_len)[:, None]
            m = jnp.arange(t_len)[None, :]
            dist = n - m
            decay = gammas[:, None, None] ** jnp.maximum(dist, 0).astype(jnp.float32)
            return jnp.where(dist[None] >= 0, decay, 0.0)
        key = jax.random.key(seed)
        ks = jax.random.split(key, 7)
        s = 1.0 / np.sqrt(C)
        return {'x': jax.random.normal(ks[0], (B, T, C), dtype=jnp.float32), 'Wq': jax.random.normal(ks[1], (C, C), dtype=jnp.float32) * s, 'Wk': jax.random.normal(ks[2], (C, C), dtype=jnp.float32) * s, 'Wv': jax.random.normal(ks[3], (C, C), dtype=jnp.float32) * s, 'Wo': jax.random.normal(ks[4], (C, C), dtype=jnp.float32) * s, 'gn_weight': jnp.ones((C,), dtype=jnp.float32), 'gn_bias': jnp.zeros((C,), dtype=jnp.float32)}
    _L0_attn_in = _L0_attn_setup()

    def _L0_ffn_setup():
        import jax, jax.numpy as jnp
        import numpy as np
        DIM = 128
        HEADS = 16
        HD = DIM // HEADS
        M = 32
        E = 4
        K = 2
        HID = 256
        MID = 256
        LB = 0.01
        EPS = 1.1920929e-07

        def _rms(x, w):
            return x * jax.lax.rsqrt(jnp.mean(x * x, axis=-1, keepdims=True) + EPS) * w

        def _gelu(x):
            return jax.nn.gelu(x, approximate=False)
        key = jax.random.key(seed)
        ks = jax.random.split(key, 20)
        d = DIM
        w = lambda k, s: jax.random.normal(k, s, jnp.float32) * 0.02
        return {'x': jax.random.normal(ks[0], (4, 128, d), jnp.float32), 'n1_w': jnp.ones((d,), jnp.float32), 'n2_w': jnp.ones((d,), jnp.float32), 'wq': w(ks[1], (d, d)), 'wk': w(ks[2], (d, d)), 'wv': w(ks[3], (d, d)), 'wo': w(ks[4], (d, d)), 'qn_w': jnp.ones((HD,), jnp.float32), 'kn_w': jnp.ones((HD,), jnp.float32), 'gate_w': w(ks[5], (E, d)), 'e0_up': w(ks[6], (HID, d)), 'e0_down': w(ks[7], (d, HID)), 'e1_w1': w(ks[8], (HID, d)), 'e1_w2': w(ks[9], (HID, d)), 'e1_down': w(ks[10], (d, HID)), 'e2_l1': w(ks[11], (MID, d)), 'e2_l2': w(ks[12], (HID, MID)), 'e2_l3': w(ks[13], (MID, HID)), 'e2_l4': w(ks[14], (d, MID)), 'e3_down': w(ks[15], (d, d)), 'e3_up': w(ks[16], (HID, d)), 'e3_out': w(ks[17], (d, HID))}
    _L0_ffn_in = _L0_ffn_setup()
    _d = {'L0_attn_x': _L0_attn_in['x'], 'L0_attn_Wq': _L0_attn_in['Wq'], 'L0_attn_Wk': _L0_attn_in['Wk'], 'L0_attn_Wv': _L0_attn_in['Wv'], 'L0_attn_Wo': _L0_attn_in['Wo'], 'L0_attn_gn_weight': _L0_attn_in['gn_weight'], 'L0_attn_gn_bias': _L0_attn_in['gn_bias'], 'L0_ffn_n1_w': _L0_ffn_in['n1_w'], 'L0_ffn_n2_w': _L0_ffn_in['n2_w'], 'L0_ffn_wq': _L0_ffn_in['wq'], 'L0_ffn_wk': _L0_ffn_in['wk'], 'L0_ffn_wv': _L0_ffn_in['wv'], 'L0_ffn_wo': _L0_ffn_in['wo'], 'L0_ffn_qn_w': _L0_ffn_in['qn_w'], 'L0_ffn_kn_w': _L0_ffn_in['kn_w'], 'L0_ffn_gate_w': _L0_ffn_in['gate_w'], 'L0_ffn_e0_up': _L0_ffn_in['e0_up'], 'L0_ffn_e0_down': _L0_ffn_in['e0_down'], 'L0_ffn_e1_w1': _L0_ffn_in['e1_w1'], 'L0_ffn_e1_w2': _L0_ffn_in['e1_w2'], 'L0_ffn_e1_down': _L0_ffn_in['e1_down'], 'L0_ffn_e2_l1': _L0_ffn_in['e2_l1'], 'L0_ffn_e2_l2': _L0_ffn_in['e2_l2'], 'L0_ffn_e2_l3': _L0_ffn_in['e2_l3'], 'L0_ffn_e2_l4': _L0_ffn_in['e2_l4'], 'L0_ffn_e3_down': _L0_ffn_in['e3_down'], 'L0_ffn_e3_up': _L0_ffn_in['e3_up'], 'L0_ffn_e3_out': _L0_ffn_in['e3_out']}
    _x0 = _d['L0_attn_x']
    _d['L0_attn_x'] = jax.random.normal(jax.random.fold_in(jax.random.key(seed), 1), (8, 512, 128), dtype=_x0.dtype)
    del _x0
    return _d

def reference(L0_attn_x, L0_attn_Wq, L0_attn_Wk, L0_attn_Wv, L0_attn_Wo, L0_attn_gn_weight, L0_attn_gn_bias, L0_ffn_n1_w, L0_ffn_n2_w, L0_ffn_wq, L0_ffn_wk, L0_ffn_wv, L0_ffn_wo, L0_ffn_qn_w, L0_ffn_kn_w, L0_ffn_gate_w, L0_ffn_e0_up, L0_ffn_e0_down, L0_ffn_e1_w1, L0_ffn_e1_w2, L0_ffn_e1_down, L0_ffn_e2_l1, L0_ffn_e2_l2, L0_ffn_e2_l3, L0_ffn_e2_l4, L0_ffn_e3_down, L0_ffn_e3_up, L0_ffn_e3_out):

    def _L0_attn_ref(x, Wq, Wk, Wv, Wo, gn_weight, gn_bias):
        import jax, jax.numpy as jnp
        import numpy as np
        B, T, C, H = (2, 256, 128, 16)
        DH = C // H
        EPS = 1e-05

        def _rotary(t_len, d_head):
            inv_freq = 1.0 / 10000.0 ** (jnp.arange(0, d_head, 2, dtype=jnp.float32) / d_head)
            t = jnp.arange(t_len, dtype=jnp.float32)
            freqs = t[:, None] * inv_freq[None, :]
            emb = jnp.concatenate([freqs, freqs], axis=-1)
            return (jnp.cos(emb), jnp.sin(emb))

        def _apply_rope(x, cos, sin):
            d = x.shape[-1]
            x1, x2 = (x[..., :d // 2], x[..., d // 2:])
            x_rot = jnp.concatenate([-x2, x1], axis=-1)
            return x * cos + x_rot * sin

        def _decay_mask(t_len, n_head):
            gammas = 1.0 - 2.0 ** (-5.0 - jnp.arange(n_head, dtype=jnp.float32))
            n = jnp.arange(t_len)[:, None]
            m = jnp.arange(t_len)[None, :]
            dist = n - m
            decay = gammas[:, None, None] ** jnp.maximum(dist, 0).astype(jnp.float32)
            return jnp.where(dist[None] >= 0, decay, 0.0)
        b, t, c = x.shape

        def proj(W):
            return jnp.einsum('btc,oc->bto', x, W).reshape(b, t, H, DH).transpose(0, 2, 1, 3)
        q, k, v = (proj(Wq), proj(Wk), proj(Wv))
        cos, sin = _rotary(t, DH)
        q = _apply_rope(q, cos, sin)
        k = _apply_rope(k, cos, sin)
        decay = _decay_mask(t, H)
        qk = jnp.einsum('bhtd,bhsd->bhts', q, k) * (1.0 / np.sqrt(DH))
        qk = qk * decay[None]
        out = jnp.einsum('bhts,bhsd->bhtd', qk, v)
        out = out.transpose(0, 2, 1, 3)
        mu = jnp.mean(out, axis=-1, keepdims=True)
        var = jnp.mean((out - mu) ** 2, axis=-1, keepdims=True)
        out = (out - mu) * jax.lax.rsqrt(var + EPS)
        out = out * gn_weight.reshape(H, DH) + gn_bias.reshape(H, DH)
        out = out.reshape(b, t, c)
        return jnp.einsum('btc,oc->bto', out, Wo)

    def _L0_ffn_ref(x, n1_w, n2_w, wq, wk, wv, wo, qn_w, kn_w, gate_w, e0_up, e0_down, e1_w1, e1_w2, e1_down, e2_l1, e2_l2, e2_l3, e2_l4, e3_down, e3_up, e3_out):
        import jax, jax.numpy as jnp
        import numpy as np
        DIM = 128
        HEADS = 16
        HD = DIM // HEADS
        M = 32
        E = 4
        K = 2
        HID = 256
        MID = 256
        LB = 0.01
        EPS = 1.1920929e-07

        def _rms(x, w):
            return x * jax.lax.rsqrt(jnp.mean(x * x, axis=-1, keepdims=True) + EPS) * w

        def _gelu(x):
            return jax.nn.gelu(x, approximate=False)
        B, T, C = x.shape
        h = _rms(x, n1_w)
        heads = lambda w_: (h @ w_.T).reshape(B, T, HEADS, HD).transpose(0, 2, 1, 3)
        q = _rms(heads(wq), qn_w)
        k = _rms(heads(wk), kn_w)
        v = heads(wv)
        scores = jnp.einsum('bhqd,bhkd->bhqk', q, k) * HD ** (-0.5)
        causal = jnp.tril(jnp.ones((T, T), bool))
        scores = jnp.where(causal[None, None], scores, -jnp.inf)
        attn = jax.nn.softmax(scores, axis=-1)
        ao = jnp.einsum('bhqk,bhkd->bhqd', attn, v).transpose(0, 2, 1, 3).reshape(B, T, C) @ wo.T
        ao = ao.at[:, :, :M].set(0.0)
        x = x + ao
        xf = _rms(x, n2_w).reshape(-1, C)
        N = xf.shape[0]
        logits = jnp.nan_to_num(xf @ gate_w.T)
        probs = jax.nn.softmax(logits, axis=-1)
        topv, topi = jax.lax.top_k(probs, K)
        topv = topv / (topv.sum(-1, keepdims=True) + 1e-08)
        wts = jnp.zeros((N, E), x.dtype).at[jnp.arange(N)[:, None], topi].add(topv)
        o0 = _gelu(xf @ e0_up.T) @ e0_down.T
        o1 = jax.nn.silu(xf @ e1_w1.T) * (xf @ e1_w2.T) @ e1_down.T
        o2 = _gelu(_gelu(_gelu(xf @ e2_l1.T) @ e2_l2.T) @ e2_l3.T) @ e2_l4.T
        o3 = _gelu(_gelu(xf @ e3_down.T) @ e3_up.T) @ e3_out.T
        moe = wts[:, 0:1] * o0 + wts[:, 1:2] * o1 + wts[:, 2:3] * o2 + wts[:, 3:4] * o3
        moe = moe.reshape(B, T, C).at[:, :, :M].set(0.0)
        return x + moe
    x = L0_attn_x
    x = x + _L0_attn_ref(_layernorm(x, axis=-1), L0_attn_Wq, L0_attn_Wk, L0_attn_Wv, L0_attn_Wo, L0_attn_gn_weight, L0_attn_gn_bias)
    x = x + _L0_ffn_ref(_layernorm(x, axis=-1), L0_ffn_n1_w, L0_ffn_n2_w, L0_ffn_wq, L0_ffn_wk, L0_ffn_wv, L0_ffn_wo, L0_ffn_qn_w, L0_ffn_kn_w, L0_ffn_gate_w, L0_ffn_e0_up, L0_ffn_e0_down, L0_ffn_e1_w1, L0_ffn_e1_w2, L0_ffn_e1_down, L0_ffn_e2_l1, L0_ffn_e2_l2, L0_ffn_e2_l3, L0_ffn_e2_l4, L0_ffn_e3_down, L0_ffn_e3_up, L0_ffn_e3_out)
    return x

_drawn_inputs = setup_inputs


def setup_inputs(seed=0):
    import zlib

    import numpy as np

    out = dict(_drawn_inputs(seed))
    spreads = {'L0_attn_gn_weight': (1.0, 0.2),
     'L0_attn_gn_bias': (0.0, 0.1),
     'L0_ffn_n1_w': (1.0, 0.6),
     'L0_ffn_n2_w': (1.0, 0.6),
     'L0_ffn_qn_w': (1.0, 0.6),
     'L0_ffn_kn_w': (1.0, 0.6)}
    factors = {'L0_ffn_wq': 8.0,
     'L0_ffn_wk': 8.0,
     'L0_ffn_wv': 8.0,
     'L0_ffn_wo': 8.0,
     'L0_ffn_gate_w': 8.0,
     'L0_ffn_e0_up': 8.0,
     'L0_ffn_e0_down': 8.0,
     'L0_ffn_e1_w1': 8.0,
     'L0_ffn_e1_w2': 8.0,
     'L0_ffn_e1_down': 8.0,
     'L0_ffn_e2_l1': 8.0,
     'L0_ffn_e2_l2': 8.0,
     'L0_ffn_e2_l3': 8.0,
     'L0_ffn_e2_l4': 8.0,
     'L0_ffn_e3_down': 8.0,
     'L0_ffn_e3_up': 8.0,
     'L0_ffn_e3_out': 8.0}
    for name, (base, spread) in spreads.items():
        noise = np.random.default_rng([zlib.crc32(name.encode()), seed]).standard_normal(out[name].shape)
        drawn = base * np.exp(spread * noise) if base else spread * noise
        out[name] = jnp.asarray(drawn.astype(out[name].dtype))
    for name, factor in factors.items():
        out[name] = (out[name] * factor).astype(out[name].dtype)
    return out
```

```python
import numpy as np
from contextlib import ExitStack

import concourse.bass as bass
from concourse import mybir

B, T, C = 8, 512, 128
H, D = 16, 8
NT = T // 128
G, J = 4, 4
SW = 32
SHIFT = 3 * D
M0 = 32
CM = C - M0
E = 4
HID = 256
EPS_LN, EPS_RMS = 1e-5, 1.1920929e-07
NEG = -1e30
FMAX = float(np.finfo(np.float32).max)
RSQRT_SEED = 0x5F3759DF

P_QKV1 = 0
P_STK1 = 2
P_SC1 = 6
P_N1 = 14
P_QKV2 = 16
P_STK2 = 18
P_MAX = 22
MAX_UNITS = [(qt, kt, gp) for qt in range(NT) for kt in range(qt + 1) for gp in range(2)]
P_SC2 = P_MAX + len(MAX_UNITS)
RUNS2 = [(g, kt) for g in range(G) for kt in range(NT)]
SC2_UNITS = [(i, qt, min(2, NT - qt)) for i, (g, kt) in enumerate(RUNS2) for qt in range(kt, NT, 2)]
P_N2 = P_SC2 + len(SC2_UNITS)
P_UNITS = P_N2 + 2
S_XN, S_QT, S_ST, S_CROSS, S_ON, S_WO1, S_H, S_MT, S_AO, S_WO2, S_XF, S_UNITS = 0, 1, 2, 5, 6, 7, 8, 9, 10, 11, 12, 13
O_AV1, O_AV2, O_UNITS = 0, 4, 8
X_GATE, X_L1, X_D3, X_L2, X_U3, X_L3, X_U0, X_E1, X_DN, X_UNITS = 0, 1, 3, 4, 6, 8, 10, 12, 16, 20

PARTS = 9
FRONT_STEPS, BACK_STEPS, N_CONSTS = 88, 28, 9


def tables():
    f = np.float32
    inv = (f(1.0) / f(10000.0) ** (np.arange(0, D, 2, dtype=f) / f(D))).astype(f)
    ang = (np.arange(T, dtype=f)[:, None] * inv[None, :]).astype(f)
    ang = np.concatenate([ang, ang], -1).astype(np.float64)
    gam = 1.0 - 2.0 ** (-5.0 - np.arange(H, dtype=np.float64))
    sign = np.where(np.arange(D) < D // 2, -1.0, 1.0)
    loc = np.arange(T) % 128
    dq = gam[None, :] ** loc[:, None] / np.sqrt(D)
    dk = gam[None, :] ** (-loc[:, None].astype(np.float64))
    cos, sin = np.cos(ang), np.sin(ang) * sign
    lay = lambda d, a: (d[:, :, None] * a[:, None, :]).reshape(T, C)
    cosd = np.concatenate([lay(dq, cos), lay(dk, cos)], 1).reshape(NT, 128, 2 * C).transpose(1, 0, 2)
    sind = np.concatenate([lay(dq, sin), lay(dk, sin)], 1).reshape(NT, 128, 2 * C).transpose(1, 0, 2)
    g128 = np.repeat(gam ** 128, D)
    same = np.arange(C)[:, None] // D == np.arange(C)[None, :] // D
    r = np.arange(128)
    return {
        "t_cos": np.ascontiguousarray(cosd.reshape(128, -1)).astype(f),
        "t_sin": np.ascontiguousarray(sind.reshape(128, -1)).astype(f),
        "t_state": (same * g128[:, None]).astype(f),
        "t_g128": g128[:, None].astype(f),
        "t_tri": (r[:, None] <= r[None, :]).astype(f),
        "t_neg": np.where(r[None, :] > r[:, None], NEG, 0.0).astype(f),
        "t_id": np.eye(128, dtype=f),
        "t_first": np.tile((np.arange(E)[None, :] < np.arange(E)[:, None]).astype(f).reshape(1, E * E), (128, 1)),
    }


def build(nc, A):
    f32, f32r, bf16, i32 = mybir.dt.float32, mybir.dt.float32r, mybir.dt.bfloat16, mybir.dt.int32
    ALU, ACT, AX = mybir.AluOpType, mybir.ActivationFunctionType, mybir.AxisListType
    ctx = ExitStack()
    with ctx:
        def sb(name, shape, dt=f32):
            return ctx.enter_context(nc.sbuf_tensor(name, shape, dt))

        def pb(name, shape):
            return ctx.enter_context(nc.psum_tensor(name, shape, f32))

        def sem(name):
            return ctx.enter_context(nc.semaphore(name))

        ww = {}
        for name, ap in A.items():
            if name.startswith(("w_", "t_")):
                ww[name] = sb("sb_" + name, list(ap.shape))
        w1, wo1, w2, wo2 = (ww[n] for n in ("w_qkv1", "w_o1", "w_qkv2", "w_o2"))
        ident, tri, neg32 = ww["t_id"], ww["t_tri"], ww["t_neg"]
        cos_t = ww["t_cos"][:].rearrange("p (t c) -> p t c", t=NT)
        sin_t = ww["t_sin"][:].rearrange("p (t c) -> p t c", t=NT)
        idb = sb("idb", [128, 128], bf16)
        negb = sb("negb", [128, J, 128], bf16)
        wqk = sb("wqk", [128, D])

        x = sb("x", [128, NT, C])
        nat = sb("nat", [128, NT, C])
        chT = sb("chT", [128, T])
        stats = sb("stats", [128, NT, 6])
        mv = sb("mv", [128, NT, 2])
        rs_v = sb("rs_v", [128, 128])
        rs_i = sb("rs_i", [128, 128], i32)
        rs_y = sb("rs_y", [128, 128])
        rs_t = sb("rs_t", [128, 128])
        qk = sb("qk", [128, 2, NT, C])
        v1 = sb("v1", [128, NT, C])
        v2 = sb("v2", [128, NT, H * (D + 1) + SW])
        v2h = v2[:, :, 0:H * (D + 1)].rearrange("p t (h s) -> p t h s", s=D + 1)
        stack = sb("stack", [128, 2, NT, H, SW], f32r)
        qs = sb("qs", [128, G, T], f32r)
        ks = sb("ks", [128, G, T], f32r)
        qx = sb("qx", [128, G, J, T], f32r)
        kx = sb("kx", [128, G, J, T], f32r)
        state = sb("state", [128, 3, C])
        state_in = sb("state_in", [128, C])
        cross = sb("cross", [128, T])
        p = sb("p", [128, 2, 4, T])
        p1 = p[:].rearrange("p a g (j n) -> p a g j n", j=J)
        p2 = p
        oT = sb("oT", [128, 4, T])
        o1 = sb("o1", [128, NT, C])
        sq = oT[:, 0:2, :].rearrange("p a (b c) -> p (a b) c", b=2)
        rot = oT[:, 2:4, :].rearrange("p a (b c) -> p (a b) c", b=2)
        rw = oT[:, 2, :].rearrange("p (t c) -> p t c", t=NT)
        red = sb("red", [128, 2, NT, H])
        x1 = sb("x1", [128, NT, C])
        z = sb("z", [128, NT, C])
        qT = z[:].rearrange("p t c -> p (t c)")
        mxp = sb("mxp", [128, NT, NT, H])
        mneg = sb("mneg", [128, NT, H])
        mT = sb("mT", [16, T], f32r)
        rcp = sb("rcp", [128, NT, H])
        xfT = sb("xfT", [128, T])
        gl = sb("gl", [128, 8, NT, E])
        mxm = sb("mxm", [128, NT, H])
        bsum = sb("bsum", [128, 3, NT])
        beats = sb("beats", [128, 3, NT, E, E])
        gsum = sb("gsum", [128, 4, NT])
        wts = sb("wts", [128, NT, E])
        hA = sb("hA", [128, 2, T])
        hB = sb("hB", [128, 2, T])
        h0 = sb("h0", [128, 2, T])
        h1 = sb("h1", [128, 2, T])
        h3a = sb("h3a", [128, T])
        h3 = sb("h3", [128, 2, T])
        sil = hB
        yout = sb("yout", [128, NT, C])

        pp = [pb(f"pair{i}", [128, 2, 512]) for i in range(2)]
        ps = pb("single", [128, 512])
        po = pb("outs", [128, 512])
        px = [pb(f"expert{i}", [128, 512]) for i in range(2)]

        waits_carried = {nc.vector: sem("waits_carried_dve"), nc.gpsimd: sem("waits_carried_pool")}
        gains = {}
        starts = {}

        def counted(name, gain):
            s = sem(name)
            gains[s] = gain
            return s

        loaded = sem("loaded")
        pool_made = sem("pool_made")
        consts_ready = sem("consts_ready")
        x_loaded = counted("x_loaded", 16)
        out_stored = counted("out_stored", 16)
        pair_filled = counted("pair_filled", P_UNITS)
        single_filled = counted("single_filled", S_UNITS)
        weighed = counted("weighed", NT + len(RUNS2))
        expert_filled = counted("expert_filled", X_UNITS)
        nat_ready = counted("nat_ready", 4)
        chT_ready = counted("chT_ready", 5)
        rotated = counted("rotated", 2)
        v_ready = counted("v_ready", 4)
        qk_ready = counted("qk_ready", 1)
        high_ready = counted("high_ready", 4)
        low_ready = counted("low_ready", 4)
        qT_ready = counted("qT_ready", 1)
        state_read = counted("state_read", 3)
        state_ready = counted("state_ready", 2)
        cross_ready = counted("cross_ready", 1)
        stack_a = counted("stack_a", 4)
        stack_b = counted("stack_b", 4)
        qx_ready = counted("qx_ready", 8 * 16)
        kx_ready = counted("kx_ready", 4 * 16)
        shift_ready = counted("shift_ready", 4 * 16)
        p1_ready = counted("p1_ready", 2 * NT)
        oT_ready = counted("oT_ready", 8)
        o1_copied = counted("o1_copied", 2)
        centred = counted("centred", 1)
        squared = counted("squared", 1)
        x1_ready = counted("x1_ready", 1)
        sq2_ready = counted("sq2_ready", 2)
        qkv2_read = counted("qkv2_read", 2)
        max_read = counted("max_read", len(MAX_UNITS))
        mneg_ready = counted("mneg_ready", 1)
        mT_ready = counted("mT_ready", 1)
        exp_done = counted("exp_done", len(SC2_UNITS))
        diag_done = counted("diag_done", len(RUNS2))
        n2_read = counted("n2_read", 2)
        y_ready = counted("y_ready", 1)
        ysq_ready = counted("ysq_ready", 1)
        base_ready = counted("base_ready", 1)
        logits_read = counted("logits_read", 1)
        logits_ready = counted("logits_ready", 1)
        gexp_ready = counted("gexp_ready", 1)
        h_ready = counted("h_ready", 13)
        h1_ready = counted("h1_ready", 2)
        down_read = counted("down_read", NT)
        starts[down_read] = NT
        front_step = counted("front_step", FRONT_STEPS)
        back_step = counted("back_step", BACK_STEPS)

        def count(s, b, n):
            return b * gains[s] + n + starts.get(s, 0)

        def first(b):
            return isinstance(b, int) and b == 0

        def apart(eng):
            eng.sem_inc(waits_carried[eng], 1)

        def heads(ap):
            return ap.rearrange("p t (h d) -> p (t h) d", d=D)

        def bc(ap, n):
            return ap.unsqueeze(len(ap.shape)).broadcast_to(list(ap.shape) + [n])

        pair_read = {}
        for m in range(2):
            pair_read[P_QKV1 + m] = [(v_ready, m + 1)]
            pair_read[P_N1 + m] = [(o1_copied, m + 1)]
            pair_read[P_QKV2 + m] = [(qkv2_read, m + 1)]
            pair_read[P_N2 + m] = [(n2_read, m + 1)]
            for layer, u in enumerate((P_STK1, P_STK2)):
                pair_read[u + 2 * m] = [(stack_a, 2 * layer + m + 1)]
                pair_read[u + 2 * m + 1] = [(stack_b, 2 * layer + m + 1)]
        for n in range(2 * NT):
            pair_read[P_SC1 + n] = [(p1_ready, n + 1)]
        for n in range(len(MAX_UNITS)):
            pair_read[P_MAX + n] = [(max_read, n + 1)]
        for n in range(len(SC2_UNITS)):
            pair_read[P_SC2 + n] = [(exp_done, n + 1)]
        single_read = {S_XN: (chT_ready, 1), S_QT: (qT_ready, 1), S_CROSS: (cross_ready, 1), S_ON: (chT_ready, 2),
                       S_WO1: (x1_ready, 1), S_H: (chT_ready, 3), S_MT: (mT_ready, 1), S_AO: (chT_ready, 4),
                       S_WO2: (y_ready, 1), S_XF: (chT_ready, 5)}
        for t in range(NT - 1):
            single_read[S_ST + t] = (state_read, t + 1)
        expert_read = {X_GATE: (logits_read, 1), X_D3: (h_ready, 3)}
        for m in range(2):
            for u, n in ((X_L1, 1), (X_L2, 4), (X_U3, 6), (X_L3, 8), (X_U0, 10)):
                expert_read[u + m] = (h_ready, n + m)
            expert_read[X_E1 + 2 * m] = (h_ready, 12 + m)
            expert_read[X_E1 + 2 * m + 1] = (h1_ready, m + 1)
        for t in range(NT):
            expert_read[X_DN + t] = (down_read, t + 1)

        def before(b, u, back, units):
            return (b, u - back) if u >= back else (b - 1, u - back + units)

        block = ctx.enter_context(nc.Block())

        def run(eng, front, back):
            front(0, lambda part: None)
            with eng.Fori(1, B) as b:
                front(b, lambda part: back(b - 1, part))
            for part in range(PARTS):
                back(B - 1, part)

        @block.tensor
        def _(pe):
            def pair(b, u):
                bb, prev = before(b, u, 2, P_UNITS)
                if not (isinstance(bb, int) and bb < 0):
                    for s, n in pair_read[prev]:
                        pe.wait_ge(s, count(s, bb, n))
                return pp[u % 2]

            def single(b, u):
                bb, prev = before(b, u, 1, S_UNITS)
                if not (isinstance(bb, int) and bb < 0):
                    pe.wait_ge(single_read[prev][0], count(single_read[prev][0], bb, single_read[prev][1]))

            def expert(b, u):
                bb, prev = before(b, u, 2, X_UNITS)
                pe.wait_ge(expert_read[prev][0], count(expert_read[prev][0], bb, expert_read[prev][1]))
                return px[u % 2]

            def channels_first(b, u):
                single(b, u)
                for t in range(NT):
                    last = nc.tensor.transpose(ps[:, t * 128:(t + 1) * 128], nat[:, t, :], ident[:])
                last.then_inc(single_filled, 1)

            def qkv(b, u, w):
                for m in range(2):
                    dst = pair(b, u + m)
                    for t in range(2 * m, 2 * m + 2):
                        last = nc.tensor.matmul(dst[:, t % 2, 0:3 * C], chT[:, t * 128:(t + 1) * 128], w[:],
                                                start=True, stop=True)
                    last.then_inc(pair_filled, 1)

            def stacks(b, u, layer):
                for s in range(2):
                    pe.wait_ge(high_ready, count(high_ready, b, 2 * layer + s + 1))
                    pe.wait_ge(low_ready, count(low_ready, b, 2 * layer + s + 1))
                    for gp in range(2):
                        dst = pair(b, u + 2 * s + gp)
                        for gg in range(2):
                            for t in range(NT):
                                src = stack[:, s, t, J * (2 * gp + gg):J * (2 * gp + gg) + J, :]
                                last = nc.tensor.transpose(dst[:, gg, t * 128:(t + 1) * 128],
                                                           src.rearrange("p j s -> p (j s)").bitcast(f32), ident[:])
                        last.then_inc(pair_filled, 1)

            def tokens_first(b, u, block_of):
                for m in range(2):
                    dst = pair(b, u + m)
                    for t in range(2 * m, 2 * m + 2):
                        for k in range(4):
                            last = nc.tensor.transpose(dst[:, t % 2, k * 128:(k + 1) * 128], block_of(t, k), ident[:])
                    last.then_inc(pair_filled, 1)

            def output(b, u, w, n):
                single(b, u)
                for t in range(NT):
                    last = nc.tensor.matmul(ps[:, t * n:(t + 1) * n], chT[:, t * 128:(t + 1) * 128], w[:],
                                            start=True, stop=True)
                last.then_inc(single_filled, 1)

            def front(b, ffn):
                pe.wait_ge(nat_ready, count(nat_ready, b, 1))
                channels_first(b, S_XN)
                ffn(0)
                pe.wait_ge(chT_ready, count(chT_ready, b, 1))
                qkv(b, P_QKV1, w1)
                ffn(1)
                single(b, S_QT)
                pe.wait_ge(qk_ready, count(qk_ready, b, 1))
                for t in range(NT):
                    last = nc.tensor.transpose(ps[:, t * 128:(t + 1) * 128], qk[:, 0, t, :], ident[:])
                last.then_inc(single_filled, 1)
                pe.wait_ge(v_ready, count(v_ready, b, 2))
                for t in range(NT - 1):
                    single(b, S_ST + t)
                    nc.tensor.matmul(ps[:, 0:C], qk[:, 1, t, :], v1[:, t, :], start=True, stop=True)\
                        .then_inc(single_filled, 1)
                stacks(b, P_STK1, 0)
                single(b, S_CROSS)
                pe.wait_ge(qT_ready, count(qT_ready, b, 1))
                pe.wait_ge(state_ready, count(state_ready, b, 2))
                for t in range(1, NT):
                    last = nc.tensor.matmul(ps[:, t * 128:(t + 1) * 128], state[:, t - 1, :],
                                            qT[:, t * 128:(t + 1) * 128], start=True, stop=True)
                last.then_inc(single_filled, 1)
                ffn(2)
                pe.wait_ge(stack_a, count(stack_a, b, 2))
                pe.wait_ge(stack_b, count(stack_b, b, 2))
                pe.wait_ge(qx_ready, count(qx_ready, b, 4 * 16))

                def scores(t):
                    for gp in range(2):
                        dst = pair(b, P_SC1 + 2 * t + gp)
                        for gg in range(2):
                            g = 2 * gp + gg
                            last = nc.tensor.matmul(dst[:, gg, :], ks[:, g, t * 128:(t + 1) * 128],
                                                    qx[:, g, :, t * 128:(t + 1) * 128], start=True, stop=True)
                        last.then_inc(pair_filled, 1)

                def weigh_retained(t):
                    if t or not first(b):
                        pe.wait_ge(oT_ready, count(oT_ready, b, t))
                    pe.wait_ge(p1_ready, count(p1_ready, b, 2 * t + 2))
                    for g in range(G):
                        last = nc.tensor.matmul(po[32 * g:32 * g + 32, :], v1[:, t, 32 * g:32 * g + 32],
                                                p1[:, t % 2, g, :, :], start=True, stop=True)
                    last.then_inc(weighed, 1)

                scores(0)
                for t in range(1, NT):
                    scores(t)
                    weigh_retained(t - 1)
                weigh_retained(NT - 1)
                ffn(3)
                pe.wait_ge(oT_ready, count(oT_ready, b, 4))
                tokens_first(b, P_N1, lambda t, k: oT[:, t, k * 128:(k + 1) * 128])
                ffn(4)
                pe.wait_ge(nat_ready, count(nat_ready, b, 2))
                channels_first(b, S_ON)
                pe.wait_ge(chT_ready, count(chT_ready, b, 2))
                output(b, S_WO1, wo1, C)
                ffn(5)
                pe.wait_ge(nat_ready, count(nat_ready, b, 3))
                channels_first(b, S_H)
                pe.wait_ge(chT_ready, count(chT_ready, b, 3))
                qkv(b, P_QKV2, w2)
                ffn(6)
                stacks(b, P_STK2, 1)
                ffn(7)
                pe.wait_ge(stack_a, count(stack_a, b, 4))
                pe.wait_ge(stack_b, count(stack_b, b, 4))
                pe.wait_ge(kx_ready, count(kx_ready, b, 4 * 16))
                for n, (qt, kt, gp) in enumerate(MAX_UNITS):
                    dst = pair(b, P_MAX + n)
                    for gg in range(2):
                        g = 2 * gp + gg
                        last = nc.tensor.matmul(dst[:, gg, :], qs[:, g, qt * 128:(qt + 1) * 128],
                                                kx[:, g, :, kt * 128:(kt + 1) * 128], start=True, stop=kt < qt)
                        if kt == qt:
                            last = nc.tensor.matmul(dst[:, gg, :], idb[:], negb[:, :, :], start=False, stop=True)
                    last.then_inc(pair_filled, 1)
                single(b, S_MT)
                pe.wait_ge(mneg_ready, count(mneg_ready, b, 1))
                for t in range(NT):
                    last = nc.tensor.transpose(ps[0:H, t * 128:(t + 1) * 128], mneg[:, t, :], ident[:])
                last.then_inc(single_filled, 1)
                ffn(8)
                pe.wait_ge(qx_ready, count(qx_ready, b, 8 * 16))
                pe.wait_ge(shift_ready, count(shift_ready, b, 4 * 16))
                pe.wait_ge(v_ready, count(v_ready, b, 4))

                def weigh(i):
                    g, kt = RUNS2[i]
                    if kt == 0:
                        pe.wait_ge(oT_ready, count(oT_ready, b, 4 + g))
                    pe.wait_ge(exp_done, count(exp_done, b, max(n for n, u in enumerate(SC2_UNITS) if u[0] == i) + 1))
                    pe.wait_ge(diag_done, count(diag_done, b, i + 1))
                    for j in range(J):
                        last = nc.tensor.matmul(po[32 * j:32 * j + 32, kt * 128:T], v2[:, kt, (D + 1) * (J * g + j):(D + 1) * (J * g + j) + SW],
                                                p2[:, i % 2, j, kt * 128:T], start=kt == 0, stop=kt == NT - 1,
                                                skip_group_check=True)
                    last.then_inc(weighed, 1)

                for n, (i, qt, m) in enumerate(SC2_UNITS):
                    g, kt = RUNS2[i]
                    dst = pair(b, P_SC2 + n)
                    for q in range(m):
                        last = nc.tensor.matmul(dst[:, q, :], ks[:, g, kt * 128:(kt + 1) * 128],
                                                qx[:, g, :, (qt + q) * 128:(qt + q + 1) * 128], start=True, stop=True)
                    last.then_inc(pair_filled, 1)
                    if qt == kt and i > 0:
                        weigh(i - 1)
                weigh(len(RUNS2) - 1)
                pe.wait_ge(oT_ready, count(oT_ready, b, 8))
                tokens_first(b, P_N2, lambda t, k: oT[:, k, t * 128:(t + 1) * 128])
                pe.wait_ge(n2_read, count(n2_read, b, 2))
                channels_first(b, S_AO)
                pe.wait_ge(chT_ready, count(chT_ready, b, 4))
                output(b, S_WO2, wo2, CM)
                pe.wait_ge(nat_ready, count(nat_ready, b, 4))
                channels_first(b, S_XF)

            def back(b, part):
                def up(u, w, src, blocks):
                    n = w.shape[-1] // blocks
                    for m in range(n // 128):
                        dst = expert(b, u + m)
                        for k in range(blocks):
                            last = nc.tensor.matmul(dst[:, :], w[:, k * n + m * 128:k * n + (m + 1) * 128],
                                                    src(k), start=k == 0, stop=k == blocks - 1)
                        last.then_inc(expert_filled, 1)

                if part == 0:
                    pe.wait_ge(chT_ready, count(chT_ready, b, 5))
                    dst = expert(b, X_GATE)
                    for t in range(NT):
                        last = nc.tensor.matmul(dst[:, t * E:(t + 1) * E], xfT[:, t * 128:(t + 1) * 128], ww["w_gate"][:],
                                                start=True, stop=True)
                    last.then_inc(expert_filled, 1)
                if part == 1:
                    up(X_L1, ww["w_l1"], lambda k: xfT[:, :], 1)
                    up(X_D3, ww["w_d3"], lambda k: xfT[:, :], 1)
                if part == 2:
                    pe.wait_ge(h_ready, count(h_ready, b, 2))
                    up(X_L2, ww["w_l2"], lambda k: hA[:, k, :], 2)
                if part == 3:
                    pe.wait_ge(h_ready, count(h_ready, b, 3))
                    up(X_U3, ww["w_u3"], lambda k: h3a[:, :], 1)
                if part == 4:
                    pe.wait_ge(h_ready, count(h_ready, b, 5))
                    up(X_L3, ww["w_l3"], lambda k: hB[:, k, :], 2)
                if part == 5:
                    up(X_U0, ww["w_u0"], lambda k: xfT[:, :], 1)
                if part in (6, 7):
                    m = part - 6
                    for n, w in enumerate(("w_g1", "w_u1")):
                        dst = expert(b, X_E1 + 2 * m + n)
                        nc.tensor.matmul(dst[:, :], ww[w][:, m * 128:(m + 1) * 128], xfT[:, :], start=True, stop=True)\
                            .then_inc(expert_filled, 1)
                if part == 8:
                    pe.wait_ge(h_ready, count(h_ready, b, 11))
                    pe.wait_ge(h1_ready, count(h1_ready, b, 2))
                    for t in range(NT):
                        dst = expert(b, X_DN + t)
                        for e, (h, w) in enumerate(((h0, "w_dn0"), (h1, "w_dn1"), (hA, "w_dn2"), (h3, "w_dn3"))):
                            for k in range(2):
                                last = nc.tensor.matmul(dst[:, e * CM:(e + 1) * CM], h[:, k, t * 128:(t + 1) * 128],
                                                        ww[w][:, k * CM:(k + 1) * CM], start=k == 0, stop=k == 1)
                        last.then_inc(expert_filled, 1)

            pe.wait_ge(loaded, 16 * len(ww))
            pe.wait_ge(consts_ready, N_CONSTS)
            run(pe, front, back)

        @block.scalar
        def _(act):
            A_ = nc.scalar.activation

            def pair(b, u):
                act.wait_ge(pair_filled, count(pair_filled, b, u + 1))
                return pp[u % 2]

            def high_parts(b, layer):
                for s in range(2):
                    src = qk[:, s].rearrange("p t (h d) -> p (t h) d", d=D)
                    dst = stack[:, s].rearrange("p t h s -> p (t h) s")
                    step = (1, 2)[s]
                    dst = dst.rearrange("p a (r d) -> p a r d", d=D)[:, :, 0:step + 1:step, :]
                    A_(dst, src.unsqueeze(2).broadcast_to([128, NT * H, 2, D]), ACT.Copy).then_inc(high_ready, 1)

            def stacks(b, u):
                for s, dst in enumerate((qs, ks)):
                    src = pair(b, u + 2 * s)
                    A_(dst[:, 0:2, :], src[:, :, :], ACT.Copy).then_inc(stack_a, 1)

            def front(b, ffn):
                act.wait_ge(single_filled, count(single_filled, b, S_XN + 1))
                A_(chT[:, :], ps[:, :], ACT.Copy).then_inc(chT_ready, 1)
                ffn(0)
                ffn(1)
                for m in range(2):
                    act.wait_ge(rotated, count(rotated, b, m + 1))
                    src = pp[(P_QKV1 + m) % 2]
                    A_(v1[:, 2 * m:2 * m + 2, :], src[:, :, 2 * C:3 * C], ACT.Copy).then_inc(v_ready, 1)
                act.wait_ge(qk_ready, count(qk_ready, b, 1))
                high_parts(b, 0)
                act.wait_ge(single_filled, count(single_filled, b, S_QT + 1))
                if not first(b):
                    act.wait_ge(base_ready, count(base_ready, b, 0))
                A_(qT[:, :], ps[:, :], ACT.Copy).then_inc(qT_ready, 1)
                stacks(b, P_STK1)
                act.wait_ge(single_filled, count(single_filled, b, S_CROSS + 1))
                A_(cross[:, 128:T], ps[:, 128:T], ACT.Copy).then_inc(cross_ready, 1)
                ffn(2)
                for m in range(2):
                    src = pair(b, P_N1 + m)
                    for t in range(2):
                        view = src[:, t, :].rearrange("p (j g k d) -> p j g k d", j=J, g=G, k=J)
                        for j in range(J):
                            i = A_(o1[:, 2 * m + t, :].rearrange("p (g j d) -> p g j d", g=G, j=J)[:, :, j, :],
                                   view[:, j, :, j, :], ACT.Copy)
                    i.then_inc(o1_copied, 1)
                ffn(3)
                act.wait_ge(centred, count(centred, b, 1))
                A_(sq[:, :, 0:C], o1[:, :, :], ACT.Square).then_inc(squared, 1)
                ffn(4)
                act.wait_ge(single_filled, count(single_filled, b, S_ON + 1))
                A_(chT[:, :], ps[:, :], ACT.Identity, scale=ww["w_gn"][:, 0:1], bias=ww["w_gn"][:, 1:2])\
                    .then_inc(chT_ready, 1)
                ffn(5)
                act.wait_ge(single_filled, count(single_filled, b, S_H + 1))
                A_(chT[:, :], ps[:, :], ACT.Copy, scale=ww["w_n12"][:, 0:1]).then_inc(chT_ready, 1)
                for m in range(2):
                    src = pair(b, P_QKV2 + m)
                    A_(sq[:, 2 * m:2 * m + 2, :], src[:, :, 0:2 * C], ACT.Square).then_inc(sq2_ready, 1)
                    A_(v2h[:, 2 * m:2 * m + 2, :, 0:D], src[:, :, 2 * C:3 * C].rearrange("p t (h d) -> p t h d", d=D),
                       ACT.Copy).then_inc(v_ready, 1)
                ffn(6)
                act.wait_ge(qkv2_read, count(qkv2_read, b, 2))
                high_parts(b, 1)
                stacks(b, P_STK2)
                ffn(7)
                act.wait_ge(single_filled, count(single_filled, b, S_MT + 1))
                A_(mT[:, :], ps[0:H, :], ACT.Copy).then_inc(mT_ready, 1)
                for n, (i, qt, m) in enumerate(SC2_UNITS):
                    src = pair(b, P_SC2 + n)
                    g, kt = RUNS2[i]
                    if qt == kt:
                        act.wait_ge(weighed, count(weighed, b, NT + i - 1))
                    dst = p2[:, i % 2, :, qt * 128:(qt + m) * 128].rearrange("p j (q n) -> p q j n", n=128)
                    A_(dst, src[:, 0:m, :].rearrange("p q (j n) -> p q j n", j=J), ACT.Exp, scale=float(D) ** -0.5)\
                        .then_inc(exp_done, 1)
                act.wait_ge(single_filled, count(single_filled, b, S_AO + 1))
                A_(chT[:, :], ps[:, :], ACT.Copy).then_inc(chT_ready, 1)
                act.wait_ge(y_ready, count(y_ready, b, 1))
                for t in range(NT):
                    i = A_(sq[:, t, 0:C], z[:, t, :], ACT.Square, accum_out=gsum[:, 0, t:t + 1])
                i.then_inc(ysq_ready, 1)
                act.wait_ge(single_filled, count(single_filled, b, S_XF + 1))
                A_(xfT[:, :], ps[:, :], ACT.Copy, scale=ww["w_n12"][:, 1:2]).then_inc(chT_ready, 1)

            def back(b, part):
                def hidden(u, dst, func):
                    act.wait_ge(expert_filled, count(expert_filled, b, u + 1))
                    A_(dst, px[u % 2][:, :], func).then_inc(h_ready, 1)

                if part == 0:
                    act.wait_ge(logits_ready, count(logits_ready, b, 1))
                    A_(gl[:, 3], gl[:, 2], ACT.Exp).then_inc(gexp_ready, 1)
                if part == 1:
                    hidden(X_L1, hA[:, 0, :], ACT.Gelu)
                    hidden(X_L1 + 1, hA[:, 1, :], ACT.Gelu)
                    hidden(X_D3, h3a[:, :], ACT.Gelu)
                if part == 2:
                    hidden(X_L2, hB[:, 0, :], ACT.Gelu)
                    hidden(X_L2 + 1, hB[:, 1, :], ACT.Gelu)
                if part == 3:
                    hidden(X_U3, h3[:, 0, :], ACT.Gelu)
                    hidden(X_U3 + 1, h3[:, 1, :], ACT.Gelu)
                if part == 4:
                    hidden(X_L3, hA[:, 0, :], ACT.Gelu)
                    hidden(X_L3 + 1, hA[:, 1, :], ACT.Gelu)
                if part == 5:
                    hidden(X_U0, h0[:, 0, :], ACT.Gelu)
                    hidden(X_U0 + 1, h0[:, 1, :], ACT.Gelu)
                if part == 6:
                    hidden(X_E1, sil[:, 0, :], ACT.Silu)
                if part == 7:
                    hidden(X_E1 + 2, sil[:, 1, :], ACT.Silu)

            act.wait_ge(loaded, 16 * len(ww))
            act.wait_ge(consts_ready, N_CONSTS)
            run(act, front, back)

        @block.vector
        def _(dve):
            V = nc.vector
            done = {}

            def step(b, ins, s=front_step):
                ins.then_inc(s, 1)
                done[s] = done.get(s, 0) + 1
                dve.wait_ge(s, count(s, b, done[s]))

            def pair(b, u):
                dve.wait_ge(pair_filled, count(pair_filled, b, u + 1))
                return pp[u % 2]

            def rsqrt(b, n):
                v, i, y, t = rs_v[:, 0:n], rs_i[:, 0:n], rs_y[:, 0:n], rs_t[:, 0:n]
                step(b, V.tensor_scalar(i, v.bitcast(i32), 1, None, ALU.logical_shift_right))
                step(b, V.tensor_scalar(y.bitcast(i32), i, -1, RSQRT_SEED, ALU.mult, ALU.add))
                for _ in range(3):
                    step(b, V.tensor_tensor(t, y, y, ALU.mult))
                    step(b, V.scalar_tensor_tensor(t, t, -0.5, v, ALU.mult, ALU.mult))
                    step(b, V.scalar_tensor_tensor(y, t, 1.5, y, ALU.add, ALU.mult))

            def moments(b, src):
                for t in range(NT):
                    i = V.bn_stats(stats[:, t, :], src[:, t, :])
                step(b, i)
                apart(dve)
                for t in range(NT):
                    i = V.bn_aggr(mv[:, t, :], stats[:, t, :])
                step(b, i)
                step(b, V.tensor_scalar(rs_v[:, 0:NT], mv[:, :, 1], EPS_LN, None, ALU.add))
                rsqrt(b, NT)

            def low_parts(b, layer):
                for s in range(2):
                    dve.wait_ge(high_ready, count(high_ready, b, 2 * layer + s + 1))
                    src = qk[:, s].rearrange("p t (h d) -> p (t h) d", d=D)
                    st = stack[:, s].rearrange("p t h s -> p (t h) s")
                    at = (2 * D, D)[s]
                    V.tensor_tensor(st[:, :, at:at + D], src, st[:, :, 0:D].bitcast(f32), ALU.subtract)\
                        .then_inc(low_ready, 1)

            def stacks(b, u):
                for s, dst in enumerate((qs, ks)):
                    src = pair(b, u + 2 * s + 1)
                    V.tensor_copy(dst[:, 2:4, :], src[:, :, :]).then_inc(stack_b, 1)

            def front(b, ffn):
                done[front_step] = 0
                dve.wait_ge(x_loaded, count(x_loaded, b, 16))
                moments(b, x)
                if not first(b):
                    dve.wait_ge(single_filled, count(single_filled, b, 0))
                for t in range(NT):
                    i = V.tensor_scalar(nat[:, t, :], x[:, t, :], mv[:, t, 0:1], rs_y[:, t:t + 1],
                                        ALU.subtract, ALU.mult)
                i.then_inc(nat_ready, 1)
                ffn(0)
                for m in range(2):
                    src = pair(b, P_QKV1 + m)[:, :, 0:2 * C]
                    tt = slice(2 * m, 2 * m + 2)
                    V.tensor_tensor(sq[:, tt, :], src, cos_t[:, tt, :], ALU.mult)
                    halves = lambda ap, k: ap.rearrange("p t (h d) -> p t h d", d=D)[:, :, :, 4 * k:4 * k + 4]
                    for k in range(2):
                        i = V.tensor_tensor(halves(rot[:, tt, :], k), halves(src, 1 - k), halves(sin_t[:, tt, :], k),
                                            ALU.mult)
                    i.then_inc(rotated, 1)
                dve.wait_ge(rotated, count(rotated, b, 2))
                V.tensor_tensor(qk[:].rearrange("p s t c -> p t s c"), sq.rearrange("p t (s c) -> p t s c", s=2),
                                rot.rearrange("p t (s c) -> p t s c", s=2), ALU.add).then_inc(qk_ready, 1)
                dve.wait_ge(qk_ready, count(qk_ready, b, 1))
                low_parts(b, 0)
                for t in range(NT - 1):
                    dve.wait_ge(single_filled, count(single_filled, b, S_ST + t + 1))
                    dst = state[:, 0, :] if t == 0 else state_in[:, :]
                    V.tensor_tensor(dst, ps[:, 0:C], ww["t_state"][:], ALU.mult).then_inc(state_read, 1)
                    dve.wait_ge(state_read, count(state_read, b, t + 1))
                    if t:
                        V.scalar_tensor_tensor(state[:, t, :], state[:, t - 1, :], ww["t_g128"][:, 0:1], state_in[:, :],
                                               ALU.mult, ALU.add).then_inc(state_ready, 1)
                        dve.wait_ge(state_ready, count(state_ready, b, t))
                stacks(b, P_STK1)
                ffn(1)

                def masked(t):
                    for gp in range(2):
                        src = pair(b, P_SC1 + 2 * t + gp)
                        if gp == 0 and (t >= 2 or not first(b)):
                            dve.wait_ge(weighed, count(weighed, b, t - 1))
                        dst = p1[:, t % 2, 2 * gp:2 * gp + 2].rearrange("p g j n -> p (g j) n")
                        V.tensor_tensor(dst, src[:].rearrange("p g (j n) -> p (g j) n", j=J),
                                        tri[:].unsqueeze(1).broadcast_to([128, 2 * J, 128]), ALU.mult)\
                            .then_inc(p1_ready, 1)

                def add_states(t):
                    dve.wait_ge(weighed, count(weighed, b, t + 1))
                    V.tensor_tensor(oT[:, t, :].rearrange("p (j n) -> p j n", j=J),
                                    po[:].rearrange("p (j n) -> p j n", j=J),
                                    cross[:, t * 128:(t + 1) * 128].unsqueeze(1).broadcast_to([128, J, 128]),
                                    ALU.add).then_inc(oT_ready, 1)

                dve.wait_ge(cross_ready, count(cross_ready, b, 1))
                masked(0)
                for t in range(1, NT):
                    masked(t)
                    add_states(t - 1)
                ffn(2)
                add_states(NT - 1)
                ffn(3)
                dve.wait_ge(o1_copied, count(o1_copied, b, 2))
                step(b, V.tensor_reduce(red[:, 0].rearrange("p t h -> p (t h)"), heads(o1[:]), AX.X, ALU.add))
                V.scalar_tensor_tensor(heads(o1[:]), bc(red[:, 0].rearrange("p t h -> p (t h)"), D), -1.0 / D,
                                       heads(o1[:]), ALU.mult, ALU.add).then_inc(centred, 1)
                dve.wait_ge(squared, count(squared, b, 1))
                step(b, V.tensor_reduce(red[:, 1], sq[:, :, 0:C].rearrange("p t (h d) -> p t h d", d=D), AX.X, ALU.add))
                step(b, V.tensor_scalar(rs_v[:, 0:NT * H], red[:, 1].rearrange("p t h -> p (t h)"), 1.0 / D, EPS_LN,
                                        ALU.mult, ALU.add))
                rsqrt(b, NT * H)
                V.tensor_tensor(heads(nat[:]), heads(o1[:]), bc(rs_y[:, 0:NT * H], D), ALU.mult).then_inc(nat_ready, 1)
                ffn(4)
                dve.wait_ge(single_filled, count(single_filled, b, S_WO1 + 1))
                V.tensor_tensor(x1[:], x[:], ps[:].rearrange("p (t c) -> p t c", t=NT), ALU.add).then_inc(x1_ready, 1)
                dve.wait_ge(x1_ready, count(x1_ready, b, 1))
                moments(b, x1)
                r1, r12 = gsum[:, 1, :], gsum[:, 2, :]
                step(b, V.tensor_copy(r1, rs_y[:, 0:NT]))
                step(b, V.tensor_tensor(rs_t[:, 0:NT], r1, r1, ALU.mult))
                step(b, V.tensor_tensor(rs_t[:, 0:NT], rs_t[:, 0:NT], mv[:, :, 1], ALU.mult))
                step(b, V.tensor_scalar(rs_v[:, 0:NT], rs_t[:, 0:NT], EPS_RMS, None, ALU.add))
                rsqrt(b, NT)
                step(b, V.tensor_tensor(r12, r1, rs_y[:, 0:NT], ALU.mult))
                for t in range(NT):
                    i = V.tensor_scalar(nat[:, t, :], x1[:, t, :], mv[:, t, 0:1], r12[:, t:t + 1],
                                        ALU.subtract, ALU.mult)
                i.then_inc(nat_ready, 1)
                for t in range(NT):
                    i = V.tensor_scalar(z[:, t, :], x1[:, t, :], mv[:, t, 0:1], r1[:, t:t + 1],
                                        ALU.subtract, ALU.mult)
                step(b, i)
                ffn(5)
                dve.wait_ge(sq2_ready, count(sq2_ready, b, 2))
                step(b, V.tensor_reduce(rs_t[:, :], sq.rearrange("p t (h d) -> p (t h) d", d=D), AX.X, ALU.add))
                step(b, V.tensor_scalar(rs_v[:, :], rs_t[:, :], 1.0 / D, EPS_RMS, ALU.mult, ALU.add))
                rsqrt(b, 2 * NT * H)
                ry = rs_y[:].rearrange("p (t s h) -> p t s h", t=NT, s=2)
                step(b, V.tensor_tensor(rw.rearrange("p t (h d) -> p t h d", d=D), bc(ry[:, :, 0, :], D),
                                        wqk[:].unsqueeze(1).unsqueeze(1).broadcast_to([128, NT, H, D]), ALU.mult))
                for m in range(2):
                    dve.wait_ge(v_ready, count(v_ready, b, 2 + m + 1))
                    src = pp[(P_QKV2 + m) % 2]
                    tt = slice(2 * m, 2 * m + 2)
                    V.tensor_tensor(qk[:, 0, tt, :], src[:, :, 0:C], rw[:, tt, :], ALU.mult)
                    V.tensor_tensor(qk[:, 1, tt, :].rearrange("p t (h d) -> p t h d", d=D),
                                    src[:, :, C:2 * C].rearrange("p t (h d) -> p t h d", d=D),
                                    bc(ry[:, tt, 1, :], D), ALU.mult).then_inc(qkv2_read, 1)
                dve.wait_ge(qkv2_read, count(qkv2_read, b, 2))
                ffn(6)
                low_parts(b, 1)
                stacks(b, P_STK2)
                ffn(7)
                for n, (qt, kt, gp) in enumerate(MAX_UNITS):
                    src = pair(b, P_MAX + n)
                    V.tensor_reduce(mxp[:, qt, kt, 2 * J * gp:2 * J * (gp + 1)],
                                    src[:].rearrange("p g (j n) -> p (g j) n", j=J), AX.X, ALU.max).then_inc(max_read, 1)
                dve.wait_ge(max_read, count(max_read, b, len(MAX_UNITS)))
                for qt in range(NT):
                    i = V.tensor_reduce(mxm[:, qt, :], mxp[:, qt, 0:qt + 1, :].rearrange("p k h -> p h k"), AX.X, ALU.max)
                step(b, i)
                V.tensor_scalar(mneg[:].rearrange("p t (j g) -> p t g j", g=G),
                                mxm[:].rearrange("p t (g j) -> p t g j", j=J), -1.0, None, ALU.mult).then_inc(mneg_ready, 1)
                ffn(8)
                for g in range(G):
                    dve.wait_ge(weighed, count(weighed, b, NT + NT * (g + 1)))
                    V.tensor_copy(oT[:, g, :], po[:]).then_inc(oT_ready, 1)
                for m in range(2):
                    src = pair(b, P_N2 + m)[:].rearrange("p t (h s) -> p (t h) s", s=SW)
                    tt = slice(2 * m, 2 * m + 2)
                    step(b, V.reciprocal(rcp[:, tt, :].rearrange("p t h -> p (t h)"), src[:, :, D]))
                    V.tensor_tensor(heads(nat[:, tt, :]), src[:, :, 0:D], bc(rcp[:, tt, :].rearrange("p t h -> p (t h)"), D),
                                    ALU.mult).then_inc(n2_read, 1)
                dve.wait_ge(single_filled, count(single_filled, b, S_WO2 + 1))
                V.tensor_tensor(z[:, :, M0:C], z[:, :, M0:C], ps[:, 0:NT * CM].rearrange("p (t c) -> p t c", t=NT),
                                ALU.add).then_inc(y_ready, 1)
                dve.wait_ge(ysq_ready, count(ysq_ready, b, 1))
                step(b, V.tensor_scalar(rs_v[:, 0:NT], gsum[:, 0, :], 1.0 / C, EPS_RMS, ALU.mult, ALU.add))
                rsqrt(b, NT)
                for t in range(NT):
                    i = V.tensor_scalar(nat[:, t, :], z[:, t, :], rs_y[:, t:t + 1], None, ALU.mult)
                i.then_inc(nat_ready, 1)
                assert done[front_step] == FRONT_STEPS, done

            def back(b, part):
                if part == 0:
                    done[back_step] = 0
                    go = lambda ins: step(b, ins, back_step)
                    dve.wait_ge(expert_filled, count(expert_filled, b, X_GATE + 1))
                    logits = px[X_GATE % 2][:, 0:NT * E].rearrange("p (t e) -> p t e", e=E)
                    V.tensor_scalar(gl[:, 0], logits, 0.0, FMAX, ALU.max, ALU.min)
                    V.tensor_scalar(gl[:, 1], logits, 0.0, -FMAX, ALU.min, ALU.max).then_inc(logits_read, 1)
                    dve.wait_ge(logits_read, count(logits_read, b, 1))
                    go(V.tensor_tensor(gl[:, 4], gl[:, 0], gl[:, 1], ALU.add))
                    go(V.tensor_reduce(bsum[:, 0, :], gl[:, 4], AX.X, ALU.max))
                    V.tensor_tensor(gl[:, 2], gl[:, 4], bc(bsum[:, 0, :], E), ALU.subtract).then_inc(logits_ready, 1)
                    dve.wait_ge(gexp_ready, count(gexp_ready, b, 1))
                    go(V.tensor_reduce(bsum[:, 1, :], gl[:, 3], AX.X, ALU.add))
                    go(V.reciprocal(bsum[:, 2, :], bsum[:, 1, :]))
                    go(V.tensor_tensor(gl[:, 5], gl[:, 3], bc(bsum[:, 2, :], E), ALU.mult))
                    pf = gl[:, 5].unsqueeze(2).broadcast_to([128, NT, E, E])
                    pe_ = bc(gl[:, 5], E)
                    V.tensor_tensor(beats[:, 0], pf, pe_, ALU.is_gt)
                    go(V.tensor_tensor(beats[:, 1], pf, pe_, ALU.is_ge))
                    go(V.tensor_tensor(beats[:, 2], beats[:, 1], beats[:, 0], ALU.subtract))
                    first = ww["t_first"][:].unsqueeze(1).broadcast_to([128, NT, E * E])
                    flat = lambda k: beats[:, k].rearrange("p t e f -> p t (e f)")
                    go(V.tensor_tensor(flat(1), flat(2), first, ALU.mult))
                    go(V.tensor_tensor(flat(2), flat(0), flat(1), ALU.add))
                    go(V.tensor_reduce(gl[:, 6], beats[:, 2], AX.X, ALU.add))
                    go(V.tensor_scalar(gl[:, 7], gl[:, 6], 1.5, None, ALU.is_lt))
                    go(V.tensor_tensor(gl[:, 6], gl[:, 7], gl[:, 5], ALU.mult))
                    go(V.tensor_reduce(bsum[:, 0, :], gl[:, 6], AX.X, ALU.add))
                    go(V.tensor_scalar(bsum[:, 1, :], bsum[:, 0, :], 1e-8, None, ALU.add))
                    go(V.reciprocal(bsum[:, 2, :], bsum[:, 1, :]))
                    go(V.tensor_tensor(wts[:], gl[:, 6], bc(bsum[:, 2, :], E), ALU.mult))
                if part in (6, 7):
                    m = part - 6
                    dve.wait_ge(expert_filled, count(expert_filled, b, X_E1 + 2 * m + 2))
                    dve.wait_ge(h_ready, count(h_ready, b, 12 + m))
                    V.tensor_tensor(h1[:, m, :], px[(X_E1 + 1) % 2][:], sil[:, m, :], ALU.mult).then_inc(h1_ready, 1)
                if part == 8:
                    dve.wait_ge(base_ready, count(base_ready, b, 1))
                    for t in range(NT):
                        dve.wait_ge(expert_filled, count(expert_filled, b, X_DN + t + 1))
                        for e in range(E):
                            i = V.scalar_tensor_tensor(yout[:, t, M0:C], px[(X_DN + t) % 2][:, e * CM:(e + 1) * CM],
                                                       wts[:, t, e:e + 1], yout[:, t, M0:C], ALU.mult, ALU.add)
                            if e < E - 1:
                                step(b, i, back_step)
                            else:
                                i.then_inc(down_read, 1)
                    assert done[back_step] == BACK_STEPS, done

            dve.wait_ge(loaded, 16 * len(ww))
            V.tensor_copy(idb[:], ident[:]).then_inc(consts_ready, 1)
            V.tensor_copy(negb[:], neg32[:].unsqueeze(1).broadcast_to([128, J, 128])).then_inc(consts_ready, 1)
            V.tensor_tensor(wqk[:], ww["w_qk"][:, 0:D], ww["w_qk"][:, D:2 * D], ALU.mult).then_inc(consts_ready, 1)
            V.memset(v2[:], 0.0).then_inc(consts_ready, 1)
            dve.wait_ge(consts_ready, N_CONSTS - 1)
            V.memset(v2h[:, :, :, D:D + 1], 1.0).then_inc(consts_ready, 1)
            V.memset(wts[:], 0.0).then_inc(down_read, NT)
            dve.wait_ge(consts_ready, N_CONSTS)
            run(dve, front, back)

        @block.gpsimd
        def _(pool):
            Q = nc.gpsimd

            def front(b, ffn):
                for i, (g, kt) in enumerate(RUNS2):
                    pool.wait_ge(exp_done, count(exp_done, b, min(n for n, u in enumerate(SC2_UNITS) if u[0] == i) + 1))
                    apart(pool)
                    blk = p2[:, i % 2, :, kt * 128:(kt + 1) * 128]
                    Q.affine_select(out=blk, in_=blk, compare_op=ALU.is_ge, fill=0.0, base=0,
                                    pattern=[[0, J], [1, 128]], channel_multiplier=-1).then_inc(diag_done, 1)
                pool.wait_ge(y_ready, count(y_ready, b, 1))
                if not first(b):
                    pool.wait_ge(out_stored, count(out_stored, b, 0))
                Q.tensor_tensor(yout[:], x1[:], z[:], ALU.add).then_inc(base_ready, 1)

            Q.memset(stack[:].bitcast(f32), 0.0).then_inc(pool_made, 1)
            pool.wait_ge(pool_made, 1)
            Q.memset(stack[:, 1, :, :, SHIFT:SHIFT + 1].bitcast(f32), 1.0).then_inc(consts_ready, 1)
            Q.memset(qx[:].bitcast(f32), 0.0).then_inc(consts_ready, 1)
            Q.memset(kx[:].bitcast(f32), 0.0).then_inc(consts_ready, 1)
            Q.memset(cross[:, 0:128], 0.0).then_inc(consts_ready, 1)
            run(pool, front, lambda b, part: None)

        @block.sync
        def _(sp):
            x_v = A["x"].rearrange("b (t p) c -> b p t c", p=128)
            out_v = A["out"].rearrange("b (t p) c -> b p t c", p=128)

            def expand(b, layer):
                sp.wait_ge(stack_a, count(stack_a, b, 2 * layer + 1))
                sp.wait_ge(stack_b, count(stack_b, b, 2 * layer + 1))
                for j in range(J):
                    sp.dma_start(qx[32 * j:32 * j + 32, :, j, :].bitcast(f32),
                                 qs[32 * j:32 * j + 32, :, :].bitcast(f32)).then_inc(qx_ready, 16)

            def store(b):
                sp.wait_ge(down_read, count(down_read, b, NT))
                sp.dma_start(out_v[b], yout[:]).then_inc(out_stored, 16)

            def front(b, ffn):
                if not first(b):
                    sp.wait_ge(x1_ready, count(x1_ready, b, 0))
                sp.dma_start(x[:], x_v[b]).then_inc(x_loaded, 16)
                expand(b, 0)
                sp.wait_ge(stack_a, count(stack_a, b, 4))
                sp.wait_ge(stack_b, count(stack_b, b, 4))
                for j in range(J):
                    sp.dma_start(kx[32 * j:32 * j + 32, :, j, :].bitcast(f32),
                                 ks[32 * j:32 * j + 32, :, :].bitcast(f32)).then_inc(kx_ready, 16)
                expand(b, 1)
                sp.wait_ge(mT_ready, count(mT_ready, b, 1))
                sp.wait_ge(qx_ready, count(qx_ready, b, 8 * 16))
                for j in range(J):
                    sp.dma_start(qx[32 * j + SHIFT:32 * j + SHIFT + 1, :, j, :].bitcast(f32),
                                 mT[4 * j:4 * j + 4, :].bitcast(f32))\
                        .then_inc(shift_ready, 16)
                ffn(8)

            def back(b, part):
                if part == 8:
                    store(b)

            for name, dst in ww.items():
                sp.dma_start(dst[:], A[name]).then_inc(loaded, 16)
            run(sp, front, back)
            sp.wait_ge(out_stored, 16 * B)
            


def kernel(**inputs):
    import numpy as _np
    import concourse.bacc as _bacc
    from concourse import mybir as _mybir
    from concourse.bass_utils import run_bass_kernel_spmd as _run

    I = {k: _np.asarray(v) for k, v in inputs.items()}
    a = lambda n: I["L0_attn_" + n]
    w = lambda n: I["L0_ffn_" + n]
    cat = _np.concatenate

    def blocks(m, n=None):
        m = m if n is None else m[:, n:]
        return m.reshape(-1, 128, m.shape[1]).transpose(1, 0, 2).reshape(128, -1)

    rows = lambda v: _np.broadcast_to(v[None, :], (128, v.shape[0]))
    arrays = {
        "x": a("x"),
        "w_qkv1": cat([a("Wq").T, a("Wk").T, a("Wv").T], 1),
        "w_o1": a("Wo").T,
        "w_gn": _np.stack([a("gn_weight"), a("gn_bias")], 1),
        "w_n12": _np.stack([w("n1_w"), w("n2_w")], 1),
        "w_qkv2": cat([w("wq").T, w("wk").T, w("wv").T], 1),
        "w_o2": w("wo").T[:, M0:],
        "w_qk": cat([rows(w("qn_w")), rows(w("kn_w"))], 1),
        "w_gate": w("gate_w").T,
        "w_u0": w("e0_up").T, "w_dn0": blocks(w("e0_down").T, M0),
        "w_g1": w("e1_w1").T, "w_u1": w("e1_w2").T, "w_dn1": blocks(w("e1_down").T, M0),
        "w_l1": w("e2_l1").T, "w_l2": blocks(w("e2_l2").T), "w_l3": blocks(w("e2_l3").T),
        "w_dn2": blocks(w("e2_l4").T, M0),
        "w_d3": w("e3_down").T, "w_u3": w("e3_up").T, "w_dn3": blocks(w("e3_out").T, M0),
    }
    arrays.update(tables())
    nc = _bacc.Bacc("TRN2", target_bir_lowering=False, num_devices=1)
    A, send = {}, {}
    for name, v in arrays.items():
        v = _np.ascontiguousarray(v)
        send[name + "_dram"] = v
        A[name] = nc.dram_tensor(name + "_dram", v.shape, _mybir.dt.from_np(v.dtype), kind="ExternalInput").ap()
    A["out"] = nc.dram_tensor("out_dram", (B, T, C), _mybir.dt.float32, kind="ExternalOutput").ap()
    build(nc, A)
    r = _run(nc, [send], core_ids=[0])
    return r.results[0]["out_dram"]
```

```python
import numpy as np
from contextlib import ExitStack

import concourse.bass as bass
from concourse import mybir

B, T, C = 8, 512, 128
H, D = 16, 8
NT = T // 128
G, J = 4, 4
SW = 32
SHIFT = 3 * D
M0 = 32
CM = C - M0
E = 4
HID = 256
EPS_LN, EPS_RMS = 1e-5, 1.1920929e-07
NEG = -1e30
FMAX = float(np.finfo(np.float32).max)
RSQRT_SEED = 0x5F3759DF

U_SC1 = 0
U_N1 = U_SC1 + NT * G
U_QKV2 = U_N1 + NT
U_STK2 = U_QKV2 + NT
U_AB = U_STK2 + 2 * G
MAX_UNITS = [(qt, kt) for qt in range(NT) for kt in range(qt + 1)]
EXP_UNITS = [(kt, qt) for kt in range(NT) for qt in range(kt, NT)]
NU = len(MAX_UNITS)
by = lambda kind, g: [(kind, g, n) for n in range(NU)]
mixed = lambda a, b: [u for two in zip(a, b) for u in two]
AHEAD = 10
MAXIMA = [u for g in range(G) for u in by("max", g)]
EXPS = [u for g in range(G) for u in by("exp", g)]
ORDER = MAXIMA[:NU + AHEAD] + mixed(EXPS, MAXIMA[NU + AHEAD:]) + EXPS[(G - 1) * NU - AHEAD:]
PLACE = {u: i for i, u in enumerate(ORDER)}
MT_AT = {PLACE["max", g, NU - 1] + 3: g for g in range(G)}
WEIGH_AT = {}
for g in range(G):
    for kt in range(NT):
        after = NU * g + EXP_UNITS.index((kt, NT - 1)) + (2, 2, 1, 2)[kt]
        WEIGH_AT.setdefault(PLACE[EXPS[min(after, G * NU - 1)]], []).append((g, kt))
OT_AT = {PLACE["exp", g + 1, 3]: g for g in range(G - 1)}
SIDE_AT = {4 + 5 * part: part for part in range(15)}
U_N2 = U_AB + len(ORDER)
RING_UNITS = U_N2 + NT
S_ON, S_WO1, S_H, S_MT, S_AO, S_WO2, S_XF, S_UNITS = 0, 1, 2, 3, 7, 8, 9, 10
L_XN, L_QKV, L_QT, L_ST, L_STK, L_CROSS, L_UNITS = 0, 1, 5, 6, 9, 17, 18
X_GATE, X_E1, X_L1, X_D3, X_L2, X_U3, X_L3, X_U0, X_DN, X_UNITS = 0, 1, 5, 7, 8, 10, 12, 14, 16, 20

RET = 15
LEAD_PARTS, FFN_PARTS = RET + 2, 12
FRONT_STEPS, TAIL_STEPS, BACK_STEPS, N_CONSTS = 58, 20, 28, 9


def tables():
    f = np.float32
    inv = (f(1.0) / f(10000.0) ** (np.arange(0, D, 2, dtype=f) / f(D))).astype(f)
    ang = (np.arange(T, dtype=f)[:, None] * inv[None, :]).astype(f)
    ang = np.concatenate([ang, ang], -1).astype(np.float64)
    gam = 1.0 - 2.0 ** (-5.0 - np.arange(H, dtype=np.float64))
    sign = np.where(np.arange(D) < D // 2, -1.0, 1.0)
    loc = np.arange(T) % 128
    dq = gam[None, :] ** loc[:, None] / np.sqrt(D)
    dk = gam[None, :] ** (-loc[:, None].astype(np.float64))
    cos, sin = np.cos(ang), np.sin(ang) * sign
    lay = lambda d, a: (d[:, :, None] * a[:, None, :]).reshape(T, C)
    cosd = np.concatenate([lay(dq, cos), lay(dk, cos)], 1).reshape(NT, 128, 2 * C).transpose(1, 0, 2)
    sind = np.concatenate([lay(dq, sin), lay(dk, sin)], 1).reshape(NT, 128, 2 * C).transpose(1, 0, 2)
    g128 = np.repeat(gam ** 128, D)
    same = np.arange(C)[:, None] // D == np.arange(C)[None, :] // D
    r = np.arange(128)
    return {
        "t_cos": np.ascontiguousarray(cosd.reshape(128, -1)).astype(f),
        "t_sin": np.ascontiguousarray(sind.reshape(128, -1)).astype(f),
        "t_state": (same * g128[:, None]).astype(f),
        "t_g128": g128[:, None].astype(f),
        "t_tri": (r[:, None] <= r[None, :]).astype(f),
        "t_neg": np.where(r[None, :] > r[:, None], NEG, 0.0).astype(f),
        "t_id": np.eye(128, dtype=f),
        "t_first": np.tile((np.arange(E)[None, :] < np.arange(E)[:, None]).astype(f).reshape(1, E * E), (128, 1)),
    }


def build(nc, A):
    f32, f32r, bf16, i32 = mybir.dt.float32, mybir.dt.float32r, mybir.dt.bfloat16, mybir.dt.int32
    ALU, ACT, AX = mybir.AluOpType, mybir.ActivationFunctionType, mybir.AxisListType
    ctx = ExitStack()
    with ctx:
        def sb(name, shape, dt=f32):
            return ctx.enter_context(nc.sbuf_tensor(name, shape, dt))

        def pb(name, shape):
            return ctx.enter_context(nc.psum_tensor(name, shape, f32))

        def sem(name):
            return ctx.enter_context(nc.semaphore(name))

        ww = {}
        for name, ap in A.items():
            if name.startswith(("w_", "t_")):
                ww[name] = sb("sb_" + name, list(ap.shape))
        w1, wo1, w2, wo2 = (ww[n] for n in ("w_qkv1", "w_o1", "w_qkv2", "w_o2"))
        ident, tri, neg32 = ww["t_id"], ww["t_tri"], ww["t_neg"]
        cos_t = ww["t_cos"][:].rearrange("p (t c) -> p t c", t=NT)
        sin_t = ww["t_sin"][:].rearrange("p (t c) -> p t c", t=NT)
        idb = sb("idb", [128, 128], bf16)
        negb = sb("negb", [128, J, 128], bf16)
        negkb = sb("negkb", [128, J, 128], bf16)
        wqk = sb("wqk", [128, D])

        x = sb("x", [128, NT, C])
        nat = sb("nat", [128, NT, C])
        chT = sb("chT", [128, T])
        stats = sb("stats", [128, NT, 6])
        mv = sb("mv", [128, NT, 2])
        rs_v = sb("rs_v", [128, 128])
        rs_i = sb("rs_i", [128, 128], i32)
        rs_y = sb("rs_y", [128, 128])
        rs_t = sb("rs_t", [128, 128])
        qk = sb("qk", [128, 2, NT, C])
        v1 = sb("v1", [128, NT, C])
        v2 = sb("v2", [128, NT, H * (D + 1) + SW])
        v2h = v2[:, :, 0:H * (D + 1)].rearrange("p t (h s) -> p t h s", s=D + 1)
        stack = sb("stack", [128, 2, NT, H, SW], f32r)
        qs1 = sb("qs1", [128, G, T], f32r)
        ks1 = sb("ks1", [128, G, T], f32r)
        qs = sb("qs", [128, G, T], f32r)
        ks = sb("ks", [128, G, T], f32r)
        qx = sb("qx", [128, G, J, T], f32r)
        kx = sb("kx", [128, 2, J, T], f32r)
        state = sb("state", [128, 3, C])
        state_in = sb("state_in", [128, C])
        cross = sb("cross", [128, T])
        p = sb("p", [128, 2, 4, T])
        p1 = p[:].rearrange("p a g (j n) -> p a g j n", j=J)

        def p2(kt):
            return p[:, kt % 2, :, 0:128] if kt == NT - 1 else p[:, kt % 2, :, kt * 128:T]

        oT = sb("oT", [128, 4, T])
        o1 = sb("o1", [128, NT, C])
        sq = oT[:, 0:2, :].rearrange("p a (b c) -> p (a b) c", b=2)
        rw = oT[:, 2, :].rearrange("p (t c) -> p t c", t=NT)
        red = sb("red", [128, 2, NT, H])
        x1 = sb("x1", [128, NT, C])
        z = sb("z", [128, NT, C])
        mxp = sb("mxp", [128, NT, J, NT])
        mneg = sb("mneg", [128, G, NT, J])
        mT = sb("mT", [J, 2, T], f32r)
        rcp = sb("rcp", [128, NT, H])
        xfT = sb("xfT", [128, T])
        gl = sb("gl", [128, 8, NT, E])
        mxm = sb("mxm", [128, NT, J])
        bsum = sb("bsum", [128, 3, NT])
        beats = sb("beats", [128, 3, NT, E, E])
        gsum = sb("gsum", [128, 4, NT])
        wts = sb("wts", [128, NT, E])
        hA = sb("hA", [128, 2, T])
        hB = sb("hB", [128, 2, T])
        h0 = sb("h0", [128, 2, T])
        h1 = sb("h1", [128, 2, T])
        h3a = h0[:, 0, :]
        h3 = sb("h3", [128, 2, T])
        sil = hB
        halved = lambda ap: ap[:].rearrange("p a (b c) -> p (a b) c", b=2)
        raw, cosp, sinp = halved(h1), halved(hA), halved(hB)
        qT = h0[:, 0, :]
        yout = sb("yout", [128, NT, C])

        pr = [pb(f"ring{i}", [128, 512]) for i in range(4)]
        ps = pb("single", [128, 512])
        po = pb("outs", [128, 512])
        px = [pb(f"side{i}", [128, 512]) for i in range(2)]

        waits_carried = {nc.vector: sem("waits_carried_dve"), nc.gpsimd: sem("waits_carried_pool"), nc.sync: sem("waits_carried_sp")}
        gains = {}
        starts = {}

        def counted(name, gain):
            s = sem(name)
            gains[s] = gain
            return s

        loaded = sem("loaded")
        pool_made = sem("pool_made")
        consts_ready = sem("consts_ready")
        x_loaded = counted("x_loaded", 16)
        out_stored = counted("out_stored", 16)
        starts[out_stored] = 16
        ring_filled = counted("ring_filled", RING_UNITS)
        single_filled = counted("single_filled", S_UNITS)
        lead_filled = counted("lead_filled", L_UNITS)
        expert_filled = counted("expert_filled", X_UNITS)
        weighed = counted("weighed", NT + G * NT)
        xn_ready = counted("xn_ready", 1)
        xnT_ready = counted("xnT_ready", 1)
        nat_ready = counted("nat_ready", 2)
        chT_ready = counted("chT_ready", 2)
        v_ready = counted("v_ready", 2 * NT)
        sin_ready = counted("sin_ready", 2)
        cos_ready = counted("cos_ready", 1)
        qk_ready = counted("qk_ready", 1)
        high_ready = counted("high_ready", 4)
        low_ready = counted("low_ready", 4)
        qT_ready = counted("qT_ready", 1)
        state_read = counted("state_read", 3)
        state_ready = counted("state_ready", 2)
        cross_ready = counted("cross_ready", 1)
        stack_a = counted("stack_a", 2 * G)
        stack_b = counted("stack_b", 2 * G)
        qx_ready = counted("qx_ready", 12 * 16)
        kx_ready = [counted(f"kx_ready{i}", 2 * J * 16) for i in range(2)]
        shift_ready = [counted(f"shift_ready{i}", 2 * J * 16) for i in range(2)]
        p1_ready = counted("p1_ready", 2 * NT)
        p1_copied = counted("p1_copied", 2 * NT)
        p1_masked = counted("p1_masked", 2 * NT)
        oT_ready = counted("oT_ready", 8)
        o1_copied = counted("o1_copied", NT)
        centred = counted("centred", 1)
        squared = counted("squared", 1)
        x1_ready = counted("x1_ready", 1)
        qkv2_read = counted("qkv2_read", NT)
        k2_ready = counted("k2_ready", 1)
        max_read = counted("max_read", G * NU)
        mneg_ready = counted("mneg_ready", G)
        mT_ready = counted("mT_ready", G)
        exp_done = counted("exp_done", G * NU)
        n2_read = counted("n2_read", NT)
        aoT_ready = counted("aoT_ready", 1)
        y_ready = counted("y_ready", 1)
        ysq_ready = counted("ysq_ready", 1)
        xf_ready = counted("xf_ready", 1)
        xfT_ready = counted("xfT_ready", 1)
        base_ready = counted("base_ready", 1)
        logits_read = counted("logits_read", 1)
        logits_ready = counted("logits_ready", 1)
        gexp_ready = counted("gexp_ready", 1)
        h_ready = counted("h_ready", 13)
        h1_ready = counted("h1_ready", 2)
        down_read = counted("down_read", NT)
        starts[down_read] = NT
        front_step = counted("front_step", FRONT_STEPS)
        tail_step = counted("tail_step", TAIL_STEPS)
        back_step = counted("back_step", BACK_STEPS)

        def count(s, b, n):
            return b * gains[s] + n + starts.get(s, 0)

        def first(b):
            return isinstance(b, int) and b == 0

        def apart(eng):
            eng.sem_inc(waits_carried[eng], 1)

        def heads(ap):
            return ap.rearrange("p t (h d) -> p (t h) d", d=D)

        def bc(ap, n):
            return ap.unsqueeze(len(ap.shape)).broadcast_to(list(ap.shape) + [n])

        def turn(layer, s):
            return s if layer == 0 else 1 - s

        def stack_read(layer, s, g):
            return (stack_a, stack_b)[g % 2], G * layer + 2 * turn(layer, s) + g // 2 + 1

        ring_read = {}
        for n in range(NT * G):
            ring_read[U_SC1 + n] = ((p1_ready, p1_copied)[n % 2], n // 2 + 1)
        for t in range(NT):
            ring_read[U_N1 + t] = (o1_copied, t + 1)
            ring_read[U_QKV2 + t] = (qkv2_read, t + 1)
            ring_read[U_N2 + t] = (n2_read, t + 1)
        for n in range(2 * G):
            ring_read[U_STK2 + n] = stack_read(1, 1 - n // G, n % G)
        for at, (kind, g, n) in enumerate(ORDER):
            ring_read[U_AB + at] = ({"max": max_read, "exp": exp_done}[kind], NU * g + n + 1)
        single_read = {S_ON: (chT_ready, 1), S_WO1: (x1_ready, 1), S_H: (chT_ready, 2), S_AO: (aoT_ready, 1),
                       S_WO2: (y_ready, 1), S_XF: (xfT_ready, 1)}
        for g in range(G):
            single_read[S_MT + g] = (mT_ready, g + 1)
        lead_read = {L_XN: (xnT_ready, 1), L_QT: (qT_ready, 1), L_CROSS: (cross_ready, 1)}
        for t in range(NT):
            lead_read[L_QKV + t] = (v_ready, t + 1)
        for t in range(NT - 1):
            lead_read[L_ST + t] = (state_read, t + 1)
        for n in range(2 * G):
            lead_read[L_STK + n] = stack_read(0, n // G, n % G)
        expert_read = {X_GATE: (logits_read, 1), X_D3: (h_ready, 5)}
        for m in range(2):
            for u, n in ((X_L1, 3), (X_L2, 6), (X_U3, 8), (X_L3, 10), (X_U0, 12)):
                expert_read[u + m] = (h_ready, n + m)
            expert_read[X_E1 + 2 * m] = (h_ready, 1 + m)
            expert_read[X_E1 + 2 * m + 1] = (h1_ready, m + 1)
        for t in range(NT):
            expert_read[X_DN + t] = (down_read, t + 1)

        def before(b, u, back, units):
            return (b, u - back) if u >= back else (b - 1, u - back + units)

        block = ctx.enter_context(nc.Block())

        def run(eng, lead, front, attend, ffn):
            for part in range(LEAD_PARTS):
                lead(0, part)
            front(0, lambda part: None)
            with eng.Fori(1, B) as b:
                attend(b - 1, lambda part: lead(b, part))
                front(b, lambda part: ffn(b - 1, part))
            attend(B - 1, lambda part: None)
            for part in range(FFN_PARTS):
                ffn(B - 1, part)

        def beside(at, side):
            if at in SIDE_AT:
                side(SIDE_AT[at])

        @block.tensor
        def _(pe):
            def ring(b, u):
                bb, prev = before(b, u, 4, RING_UNITS)
                if not (isinstance(bb, int) and bb < 0):
                    pe.wait_ge(ring_read[prev][0], count(ring_read[prev][0], bb, ring_read[prev][1]))
                return pr[u % 4]

            def single(b, u):
                bb, prev = before(b, u, 1, S_UNITS)
                if not (isinstance(bb, int) and bb < 0):
                    pe.wait_ge(single_read[prev][0], count(single_read[prev][0], bb, single_read[prev][1]))

            def leading(b, u):
                if u >= 2:
                    pe.wait_ge(lead_read[u - 2][0], count(lead_read[u - 2][0], b, lead_read[u - 2][1]))
                elif not first(b):
                    pe.wait_ge(down_read, count(down_read, b - 2, NT - 1 + u))
                return px[u % 2]

            def expert(b, u):
                if u >= 2:
                    pe.wait_ge(expert_read[u - 2][0], count(expert_read[u - 2][0], b, expert_read[u - 2][1]))
                elif isinstance(b, int):
                    pe.wait_ge(down_read, count(down_read, b - 1, NT - 1 + u))
                else:
                    read, n = lead_read[L_UNITS - 2 + u]
                    pe.wait_ge(read, count(read, b + 1, n))
                return px[u % 2]

            def transposed(dst, src):
                for t in range(NT):
                    last = nc.tensor.transpose(dst[:, t * 128:(t + 1) * 128], src(t), ident[:])
                return last

            def stacked(dst, s, g):
                return transposed(dst, lambda t: stack[:, s, t, J * g:J * g + J, :]
                                  .rearrange("p j s -> p (j s)").bitcast(f32))

            def scores(b, t):
                for g in range(G):
                    dst = ring(b, U_SC1 + G * t + g)
                    nc.tensor.matmul(dst[:, :], ks1[:, g, t * 128:(t + 1) * 128],
                                     qx[:, g, :, t * 128:(t + 1) * 128], start=True, stop=True)\
                        .then_inc(ring_filled, 1)

            def weigh_retained(b, t):
                if t or not first(b):
                    pe.wait_ge(oT_ready, count(oT_ready, b, t))
                pe.wait_ge(p1_ready, count(p1_ready, b, 2 * (t + 1)))
                pe.wait_ge(p1_masked, count(p1_masked, b, 2 * (t + 1)))
                for g in range(G):
                    last = nc.tensor.matmul(po[32 * g:32 * g + 32, :], v1[:, t, 32 * g:32 * g + 32],
                                            p1[:, t % 2, g, :, :], start=True, stop=True)
                last.then_inc(weighed, 1)

            def lead(b, part):
                if part == 2:
                    pe.wait_ge(xn_ready, count(xn_ready, b, 1))
                    transposed(leading(b, L_XN), lambda t: nat[:, t, :]).then_inc(lead_filled, 1)
                if part in (3, 4):
                    pe.wait_ge(xnT_ready, count(xnT_ready, b, 1))
                    for t in (0, 1) if part == 3 else (2, 3):
                        dst = leading(b, L_QKV + t)
                        nc.tensor.matmul(dst[:, 0:3 * C], chT[:, t * 128:(t + 1) * 128], w1[:], start=True, stop=True)\
                            .then_inc(lead_filled, 1)
                if part == 7:
                    pe.wait_ge(qk_ready, count(qk_ready, b, 1))
                    transposed(leading(b, L_QT), lambda t: qk[:, 0, t, :]).then_inc(lead_filled, 1)
                if part in (7, 8, 9):
                        t = part - 7
                        dst = leading(b, L_ST + t)
                        nc.tensor.matmul(dst[:, 0:C], qk[:, 1, t, :], v1[:, t, :], start=True, stop=True)\
                            .then_inc(lead_filled, 1)
                if part in (10, 11, 12, 13):
                    s, g0 = (part - 10) // 2, 2 * ((part - 10) % 2)
                    pe.wait_ge(high_ready, count(high_ready, b, s + 1))
                    pe.wait_ge(low_ready, count(low_ready, b, s + 1))
                    for g in (g0, g0 + 1):
                        stacked(leading(b, L_STK + G * s + g), s, g).then_inc(lead_filled, 1)
                if part == 14:
                    dst = leading(b, L_CROSS)
                    pe.wait_ge(qT_ready, count(qT_ready, b, 1))
                    pe.wait_ge(state_ready, count(state_ready, b, 2))
                    for t in range(1, NT):
                        last = nc.tensor.matmul(dst[:, t * 128:(t + 1) * 128], state[:, t - 1, :],
                                                qT[:, t * 128:(t + 1) * 128], start=True, stop=True)
                    last.then_inc(lead_filled, 1)
                if part == RET:
                    pe.wait_ge(stack_a, count(stack_a, b, G))
                    pe.wait_ge(stack_b, count(stack_b, b, G))
                    pe.wait_ge(qx_ready, count(qx_ready, b, 8 * 16))
                    scores(b, 0)
                if part == RET + 1:
                    scores(b, 1)
                    weigh_retained(b, 0)

            def output(b, u, w, n):
                single(b, u)
                for t in range(NT):
                    last = nc.tensor.matmul(ps[:, t * n:(t + 1) * n], chT[:, t * 128:(t + 1) * 128], w[:],
                                            start=True, stop=True)
                last.then_inc(single_filled, 1)

            def front(b, side):
                side(0)
                scores(b, 2)
                weigh_retained(b, 1)
                side(1)
                scores(b, 3)
                weigh_retained(b, 2)
                side(2)
                weigh_retained(b, 3)
                side(3)
                for t in range(NT):
                    pe.wait_ge(oT_ready, count(oT_ready, b, t + 1))
                    transposed(ring(b, U_N1 + t), lambda k: oT[:, t, k * 128:(k + 1) * 128]).then_inc(ring_filled, 1)
                side(4)
                side(5)
                single(b, S_ON)
                pe.wait_ge(nat_ready, count(nat_ready, b, 1))
                transposed(ps, lambda t: nat[:, t, :]).then_inc(single_filled, 1)
                pe.wait_ge(chT_ready, count(chT_ready, b, 1))
                output(b, S_WO1, wo1, C)
                side(6)
                side(7)
                single(b, S_H)
                pe.wait_ge(nat_ready, count(nat_ready, b, 2))
                transposed(ps, lambda t: nat[:, t, :]).then_inc(single_filled, 1)
                pe.wait_ge(chT_ready, count(chT_ready, b, 2))
                for t in range(NT):
                    dst = ring(b, U_QKV2 + t)
                    nc.tensor.matmul(dst[:, 0:3 * C], chT[:, t * 128:(t + 1) * 128], w2[:], start=True, stop=True)\
                        .then_inc(ring_filled, 1)
                side(8)
                side(9)
                for n in range(2 * G):
                    s, g = 1 - n // G, n % G
                    pe.wait_ge(high_ready, count(high_ready, b, 2 + turn(1, s) + 1))
                    pe.wait_ge(low_ready, count(low_ready, b, 2 + turn(1, s) + 1))
                    stacked(ring(b, U_STK2 + n), s, g).then_inc(ring_filled, 1)
                side(10)
                side(11)

            def attend(b, side):
                def weigh(g, kt):
                    if kt == 0:
                        pe.wait_ge(oT_ready, count(oT_ready, b, 4 + g))
                    pe.wait_ge(exp_done, count(exp_done, b, NU * g + EXP_UNITS.index((kt, NT - 1)) + 1))
                    for j in range(J):
                        h = (D + 1) * (J * g + j)
                        last = nc.tensor.matmul(po[32 * j:32 * j + 32, kt * 128:T], v2[:, kt, h:h + SW],
                                                p2(kt)[:, j, :], start=kt == 0, stop=kt == NT - 1,
                                                skip_group_check=True)
                    last.then_inc(weighed, 1)

                pe.wait_ge(stack_a, count(stack_a, b, 2 * G))
                pe.wait_ge(stack_b, count(stack_b, b, 2 * G))
                pe.wait_ge(v_ready, count(v_ready, b, 2 * NT))
                for at, (kind, g, n) in enumerate(ORDER):
                    if kind == "max":
                        qt, kt = MAX_UNITS[n]
                        if n == 0:
                            pe.wait_ge(kx_ready[g % 2], count(kx_ready[g % 2], b, (g // 2 + 1) * J * 16))
                        dst = ring(b, U_AB + at)
                        last = nc.tensor.matmul(dst[:, :], qs[:, g, qt * 128:(qt + 1) * 128],
                                                kx[:, g % 2, :, kt * 128:(kt + 1) * 128], start=True, stop=kt < qt)
                        if kt == qt:
                            last = nc.tensor.matmul(dst[:, :], idb[:], negb[:, :, :], start=False, stop=True)
                        last.then_inc(ring_filled, 1)
                    else:
                        kt, qt = EXP_UNITS[n]
                        if n == 0:
                            if g == 0:
                                pe.wait_ge(qx_ready, count(qx_ready, b, 12 * 16))
                            pe.wait_ge(shift_ready[g % 2], count(shift_ready[g % 2], b, (g // 2 + 1) * J * 16))
                        dst = ring(b, U_AB + at)
                        last = nc.tensor.matmul(dst[:, :], ks[:, g, kt * 128:(kt + 1) * 128],
                                                qx[:, g, :, qt * 128:(qt + 1) * 128], start=True, stop=kt < qt)
                        if kt == qt:
                            last = nc.tensor.matmul(dst[:, :], idb[:], negkb[:, :, :], start=False, stop=True)
                        last.then_inc(ring_filled, 1)
                    if at in MT_AT:
                        gm = MT_AT[at]
                        single(b, S_MT + gm)
                        pe.wait_ge(mneg_ready, count(mneg_ready, b, gm + 1))
                        transposed(ps[0:J, :], lambda t: mneg[:, gm, t, :]).then_inc(single_filled, 1)
                    for g_kt in WEIGH_AT.get(at, []):
                        weigh(*g_kt)
                    beside(at, side)
                for t in range(NT):
                    if t == 0:
                        pe.wait_ge(oT_ready, count(oT_ready, b, 8))
                    transposed(ring(b, U_N2 + t), lambda k: oT[:, k, t * 128:(t + 1) * 128]).then_inc(ring_filled, 1)
                single(b, S_AO)
                pe.wait_ge(n2_read, count(n2_read, b, NT))
                transposed(ps, lambda t: nat[:, t, :]).then_inc(single_filled, 1)
                side(RET)
                pe.wait_ge(aoT_ready, count(aoT_ready, b, 1))
                output(b, S_WO2, wo2, CM)
                side(RET + 1)
                single(b, S_XF)
                pe.wait_ge(xf_ready, count(xf_ready, b, 1))
                transposed(ps, lambda t: nat[:, t, :]).then_inc(single_filled, 1)

            def back(b, part):
                def up(u, w, src, blocks):
                    n = w.shape[-1] // blocks
                    for m in range(n // 128):
                        dst = expert(b, u + m)
                        for k in range(blocks):
                            last = nc.tensor.matmul(dst[:, :], w[:, k * n + m * 128:k * n + (m + 1) * 128],
                                                    src(k), start=k == 0, stop=k == blocks - 1)
                        last.then_inc(expert_filled, 1)

                if part == 0:
                    pe.wait_ge(xfT_ready, count(xfT_ready, b, 1))
                    dst = expert(b, X_GATE)
                    for t in range(NT):
                        last = nc.tensor.matmul(dst[:, t * E:(t + 1) * E], xfT[:, t * 128:(t + 1) * 128], ww["w_gate"][:],
                                                start=True, stop=True)
                    last.then_inc(expert_filled, 1)
                if part in (1, 2):
                    m = part - 1
                    for n, w in enumerate(("w_g1", "w_u1")):
                        dst = expert(b, X_E1 + 2 * m + n)
                        nc.tensor.matmul(dst[:, :], ww[w][:, m * 128:(m + 1) * 128], xfT[:, :], start=True, stop=True)\
                            .then_inc(expert_filled, 1)
                if part == 3:
                    up(X_L1, ww["w_l1"], lambda k: xfT[:, :], 1)
                    up(X_D3, ww["w_d3"], lambda k: xfT[:, :], 1)
                if part == 4:
                    pe.wait_ge(h_ready, count(h_ready, b, 4))
                    up(X_L2, ww["w_l2"], lambda k: hA[:, k, :], 2)
                if part == 5:
                    pe.wait_ge(h_ready, count(h_ready, b, 5))
                    up(X_U3, ww["w_u3"], lambda k: h3a, 1)
                if part == 6:
                    pe.wait_ge(h_ready, count(h_ready, b, 7))
                    up(X_L3, ww["w_l3"], lambda k: hB[:, k, :], 2)
                if part == 7:
                    up(X_U0, ww["w_u0"], lambda k: xfT[:, :], 1)
                if part >= 8:
                    pe.wait_ge(h_ready, count(h_ready, b, 13))
                    pe.wait_ge(h1_ready, count(h1_ready, b, 2))
                    for t in (part - 8,):
                        dst = expert(b, X_DN + t)
                        for e, (h, w) in enumerate(((h0, "w_dn0"), (h1, "w_dn1"), (hA, "w_dn2"), (h3, "w_dn3"))):
                            for k in range(2):
                                last = nc.tensor.matmul(dst[:, e * CM:(e + 1) * CM], h[:, k, t * 128:(t + 1) * 128],
                                                        ww[w][:, k * CM:(k + 1) * CM], start=k == 0, stop=k == 1)
                        last.then_inc(expert_filled, 1)

            pe.wait_ge(loaded, 16 * len(ww))
            pe.wait_ge(consts_ready, N_CONSTS)
            run(pe, lead, front, attend, back)

        @block.scalar
        def _(act):
            A_ = nc.scalar.activation
            x_v = A["x"].rearrange("b (t p) c -> b p t c", p=128)

            def high_parts(b, layer, s):
                src = qk[:, s].rearrange("p t (h d) -> p (t h) d", d=D)
                dst = stack[:, s].rearrange("p t h s -> p (t h) s")
                step = (1, 2)[s]
                dst = dst.rearrange("p a (r d) -> p a r d", d=D)[:, :, 0:step + 1:step, :]
                A_(dst, src.unsqueeze(2).broadcast_to([128, NT * H, 2, D]), ACT.Copy).then_inc(high_ready, 1)

            def unmasked(b, t):
                for g in (1, 3):
                    act.wait_ge(ring_filled, count(ring_filled, b, U_SC1 + G * t + g + 1))
                    if g == 1 and (t >= 2 or not first(b)):
                        act.wait_ge(weighed, count(weighed, b, t - 1))
                    A_(p1[:, t % 2, g], pr[(U_SC1 + G * t + g) % 4][:, :].rearrange("p (j n) -> p j n", j=J), ACT.Copy)\
                        .then_inc(p1_copied, 1)

            def lead(b, part):
                if part == 0:
                    if not first(b):
                        act.wait_ge(x1_ready, count(x1_ready, b, 0))
                    act.dma_start(x[:], x_v[b]).then_inc(x_loaded, 16)
                if part == 2:
                    act.wait_ge(lead_filled, count(lead_filled, b, L_XN + 1))
                    A_(chT[:, :], px[L_XN % 2][:, :], ACT.Copy).then_inc(xnT_ready, 1)
                if part in (3, 4):
                    if part == 3 and not first(b):
                        act.wait_ge(down_read, count(down_read, b - 2, NT))
                    for t in (0, 1) if part == 3 else (2, 3):
                        act.wait_ge(lead_filled, count(lead_filled, b, L_QKV + t + 1))
                        src = px[(L_QKV + t) % 2]
                        A_(raw[:, t, :], src[:, 0:2 * C], ACT.Copy)
                        A_(v1[:, t, :], src[:, 2 * C:3 * C], ACT.Copy).then_inc(v_ready, 1)
                if part == 7:
                    act.wait_ge(qk_ready, count(qk_ready, b, 1))
                    high_parts(b, 0, 0)
                    act.wait_ge(lead_filled, count(lead_filled, b, L_QT + 1))
                    A_(qT, px[L_QT % 2][:, :], ACT.Copy).then_inc(qT_ready, 1)
                if part == 8:
                    high_parts(b, 0, 1)
                if part in (10, 11, 12, 13):
                    s, g = (part - 10) // 2, 2 * ((part - 10) % 2)
                    u = L_STK + G * s + g
                    act.wait_ge(lead_filled, count(lead_filled, b, u + 1))
                    A_((qs1, ks1)[s][:, g, :], px[u % 2][:, :], ACT.Copy).then_inc(stack_a, 1)
                if part == 14:
                    act.wait_ge(lead_filled, count(lead_filled, b, L_CROSS + 1))
                    A_(cross[:, 128:T], px[L_CROSS % 2][:, 128:T], ACT.Copy).then_inc(cross_ready, 1)
                if part >= RET:
                    unmasked(b, part - RET)

            def front(b, side):
                side(0)
                unmasked(b, 2)
                side(1)
                unmasked(b, 3)
                side(2)
                side(3)
                for t in range(NT):
                    act.wait_ge(ring_filled, count(ring_filled, b, U_N1 + t + 1))
                    src = pr[(U_N1 + t) % 4][:, :]
                    view = bass.AP(tensor=src.tensor, offset=src.offset, ap=[list(src.ap[0]), [SW, G], [128 + D, J], [1, D]])
                    A_(o1[:, t, :].rearrange("p (g j d) -> p g j d", g=G, j=J), view, ACT.Copy).then_inc(o1_copied, 1)
                act.wait_ge(centred, count(centred, b, 1))
                A_(sq[:, :, 0:C], o1[:, :, :], ACT.Square).then_inc(squared, 1)
                side(4)
                side(5)
                act.wait_ge(single_filled, count(single_filled, b, S_ON + 1))
                A_(chT[:, :], ps[:, :], ACT.Identity, scale=ww["w_gn"][:, 0:1], bias=ww["w_gn"][:, 1:2])\
                    .then_inc(chT_ready, 1)
                side(6)
                side(7)
                act.wait_ge(single_filled, count(single_filled, b, S_H + 1))
                A_(chT[:, :], ps[:, :], ACT.Copy, scale=ww["w_n12"][:, 0:1]).then_inc(chT_ready, 1)
                for t in range(NT):
                    act.wait_ge(ring_filled, count(ring_filled, b, U_QKV2 + t + 1))
                    src = pr[(U_QKV2 + t) % 4]
                    A_(sq[:, t, :], src[:, 0:2 * C], ACT.Square)
                    A_(v2h[:, t, :, 0:D], src[:, 2 * C:3 * C].rearrange("p (h d) -> p h d", d=D),
                       ACT.Copy).then_inc(v_ready, 1)
                act.wait_ge(k2_ready, count(k2_ready, b, 1))
                high_parts(b, 1, 1)
                act.wait_ge(qkv2_read, count(qkv2_read, b, NT))
                high_parts(b, 1, 0)
                for n, dst in enumerate((ks, qs)):
                    for g in (0, 2):
                        u = U_STK2 + G * n + g
                        act.wait_ge(ring_filled, count(ring_filled, b, u + 1))
                        A_(dst[:, g, :], pr[u % 4][:, :], ACT.Copy).then_inc(stack_a, 1)

            def attend(b, side):
                for at, (kind, g, n) in enumerate(ORDER):
                    if kind == "exp":
                        kt, qt = EXP_UNITS[n]
                        act.wait_ge(ring_filled, count(ring_filled, b, U_AB + at + 1))
                        if qt == kt:
                            act.wait_ge(weighed, count(weighed, b, NT + (NT * g - 1, max(NT * g - 2, 0), NT * g + 1, NT * g)[kt]))
                        A_(p2(kt)[:, :, (qt - kt) * 128:(qt - kt + 1) * 128],
                           pr[(U_AB + at) % 4][:, :].rearrange("p (j n) -> p j n", j=J), ACT.Exp, scale=float(D) ** -0.5)\
                            .then_inc(exp_done, 1)
                    if at in MT_AT:
                        gm = MT_AT[at]
                        act.wait_ge(single_filled, count(single_filled, b, S_MT + gm + 1))
                        if gm >= 2:
                            act.wait_ge(shift_ready[gm % 2], count(shift_ready[gm % 2], b, J * 16))
                        A_(mT[:, gm % 2, :], ps[0:J, :], ACT.Copy).then_inc(mT_ready, 1)
                    beside(at, side)
                act.wait_ge(single_filled, count(single_filled, b, S_AO + 1))
                A_(chT[:, :], ps[:, :], ACT.Copy).then_inc(aoT_ready, 1)
                side(RET)
                act.wait_ge(down_read, count(down_read, b, 0))
                act.wait_ge(y_ready, count(y_ready, b, 1))
                for t in range(NT):
                    i = A_(cosp[:, t, 0:C], z[:, t, :], ACT.Square, accum_out=gsum[:, 0, t:t + 1])
                i.then_inc(ysq_ready, 1)
                act.wait_ge(single_filled, count(single_filled, b, S_XF + 1))
                A_(xfT[:, :], ps[:, :], ACT.Copy, scale=ww["w_n12"][:, 1:2]).then_inc(xfT_ready, 1)
                side(RET + 1)

            def back(b, part):
                def hidden(u, dst, func):
                    act.wait_ge(expert_filled, count(expert_filled, b, u + 1))
                    A_(dst, px[u % 2][:, :], func).then_inc(h_ready, 1)

                if part == 0:
                    act.wait_ge(logits_ready, count(logits_ready, b, 1))
                    A_(gl[:, 3], gl[:, 2], ACT.Exp).then_inc(gexp_ready, 1)
                if part in (1, 2):
                    hidden(X_E1 + 2 * (part - 1), sil[:, part - 1, :], ACT.Silu)
                if part == 3:
                    hidden(X_L1, hA[:, 0, :], ACT.Gelu)
                    hidden(X_L1 + 1, hA[:, 1, :], ACT.Gelu)
                    hidden(X_D3, h3a, ACT.Gelu)
                if part == 4:
                    act.wait_ge(h1_ready, count(h1_ready, b, 2))
                    hidden(X_L2, hB[:, 0, :], ACT.Gelu)
                    hidden(X_L2 + 1, hB[:, 1, :], ACT.Gelu)
                if part == 5:
                    hidden(X_U3, h3[:, 0, :], ACT.Gelu)
                    hidden(X_U3 + 1, h3[:, 1, :], ACT.Gelu)
                if part == 6:
                    hidden(X_L3, hA[:, 0, :], ACT.Gelu)
                    hidden(X_L3 + 1, hA[:, 1, :], ACT.Gelu)
                if part == 7:
                    hidden(X_U0, h0[:, 0, :], ACT.Gelu)
                    hidden(X_U0 + 1, h0[:, 1, :], ACT.Gelu)

            act.wait_ge(loaded, 16 * len(ww))
            act.wait_ge(consts_ready, N_CONSTS)
            run(act, lead, front, attend, back)

        @block.vector
        def _(dve):
            V = nc.vector
            done = {}

            def step(b, ins, s=front_step):
                ins.then_inc(s, 1)
                done[s] = done.get(s, 0) + 1
                dve.wait_ge(s, count(s, b, done[s]))

            def ring(b, u):
                dve.wait_ge(ring_filled, count(ring_filled, b, u + 1))
                return pr[u % 4]

            def rsqrt(b, n, s=front_step):
                v, i, y, t = rs_v[:, 0:n], rs_i[:, 0:n], rs_y[:, 0:n], rs_t[:, 0:n]
                step(b, V.tensor_scalar(i, v.bitcast(i32), 1, None, ALU.logical_shift_right), s)
                step(b, V.tensor_scalar(y.bitcast(i32), i, -1, RSQRT_SEED, ALU.mult, ALU.add), s)
                for _ in range(3):
                    step(b, V.tensor_tensor(t, y, y, ALU.mult), s)
                    step(b, V.scalar_tensor_tensor(t, t, -0.5, v, ALU.mult, ALU.mult), s)
                    step(b, V.scalar_tensor_tensor(y, t, 1.5, y, ALU.add, ALU.mult), s)

            def moments(b, src):
                for t in range(NT):
                    i = V.bn_stats(stats[:, t, :], src[:, t, :])
                step(b, i)
                apart(dve)
                for t in range(NT):
                    i = V.bn_aggr(mv[:, t, :], stats[:, t, :])
                step(b, i)
                step(b, V.tensor_scalar(rs_v[:, 0:NT], mv[:, :, 1], EPS_LN, None, ALU.add))

            def low_parts(b, layer, s):
                dve.wait_ge(high_ready, count(high_ready, b, 2 * layer + turn(layer, s) + 1))
                src = qk[:, s].rearrange("p t (h d) -> p (t h) d", d=D)
                st = stack[:, s].rearrange("p t h s -> p (t h) s")
                at = (2 * D, D)[s]
                V.tensor_tensor(st[:, :, at:at + D], src, st[:, :, 0:D].bitcast(f32), ALU.subtract)\
                    .then_inc(low_ready, 1)

            def lead(b, part):
                if part == 0:
                    done[front_step] = 0
                    dve.wait_ge(x_loaded, count(x_loaded, b, 16))
                    moments(b, x)
                if part == 1:
                    rsqrt(b, NT)
                    for t in range(NT):
                        i = V.tensor_scalar(nat[:, t, :], x[:, t, :], mv[:, t, 0:1], rs_y[:, t:t + 1],
                                            ALU.subtract, ALU.mult)
                    i.then_inc(xn_ready, 1)
                if part in (4, 5):
                    m = part - 4
                    dve.wait_ge(v_ready, count(v_ready, b, 2 * m + 2))
                    tt = slice(2 * m, 2 * m + 2)
                    halves = lambda ap, k: ap.rearrange("p t (h d) -> p t h d", d=D)[:, :, :, 4 * k:4 * k + 4]
                    for k in range(2):
                        i = V.tensor_tensor(halves(sinp[:, tt, :], k), halves(raw[:, tt, :], 1 - k),
                                            halves(sin_t[:, tt, :], k), ALU.mult)
                    i.then_inc(sin_ready, 1)
                if part in (7, 8, 9):
                    t = part - 7
                    dve.wait_ge(lead_filled, count(lead_filled, b, L_ST + t + 1))
                    if t == 2:
                        dve.wait_ge(state_ready, count(state_ready, b, 1))
                    dst = state[:, 0, :] if t == 0 else state_in[:, :]
                    V.tensor_tensor(dst, px[(L_ST + t) % 2][:, 0:C], ww["t_state"][:], ALU.mult).then_inc(state_read, 1)
                    if t:
                        dve.wait_ge(state_read, count(state_read, b, t + 1))
                        V.scalar_tensor_tensor(state[:, t, :], state[:, t - 1, :], ww["t_g128"][:, 0:1],
                                               state_in[:, :], ALU.mult, ALU.add).then_inc(state_ready, 1)
                if part in (10, 11, 12, 13):
                    s, g = (part - 10) // 2, 2 * ((part - 10) % 2) + 1
                    u = L_STK + G * s + g
                    dve.wait_ge(lead_filled, count(lead_filled, b, u + 1))
                    V.tensor_copy((qs1, ks1)[s][:, g, :], px[u % 2][:, :]).then_inc(stack_b, 1)
                if part == RET:
                    dve.wait_ge(cross_ready, count(cross_ready, b, 1))
                    masked(b, 0)
                if part == RET + 1:
                    masked(b, 1)
                    add_states(b, 0)

            def masked(b, t):
                for g in (0, 2):
                    src = ring(b, U_SC1 + G * t + g)
                    if g == 0 and (t >= 2 or not first(b)):
                        dve.wait_ge(weighed, count(weighed, b, t - 1))
                    V.tensor_tensor(p1[:, t % 2, g], src[:].rearrange("p (j n) -> p j n", j=J),
                                    tri[:].unsqueeze(1).broadcast_to([128, J, 128]), ALU.mult)\
                        .then_inc(p1_ready, 1)

            def add_states(b, t):
                dve.wait_ge(weighed, count(weighed, b, t + 1))
                V.tensor_tensor(oT[:, t, :].rearrange("p (j n) -> p j n", j=J),
                                po[:].rearrange("p (j n) -> p j n", j=J),
                                cross[:, t * 128:(t + 1) * 128].unsqueeze(1).broadcast_to([128, J, 128]),
                                ALU.add).then_inc(oT_ready, 1)

            def front(b, side):
                side(0)
                masked(b, 2)
                add_states(b, 1)
                side(1)
                masked(b, 3)
                add_states(b, 2)
                side(2)
                add_states(b, 3)
                side(3)
                dve.wait_ge(o1_copied, count(o1_copied, b, NT))
                step(b, V.tensor_reduce(red[:, 0].rearrange("p t h -> p (t h)"), heads(o1[:]), AX.X, ALU.add))
                V.scalar_tensor_tensor(heads(o1[:]), bc(red[:, 0].rearrange("p t h -> p (t h)"), D), -1.0 / D,
                                       heads(o1[:]), ALU.mult, ALU.add).then_inc(centred, 1)
                dve.wait_ge(squared, count(squared, b, 1))
                step(b, V.tensor_reduce(red[:, 1], sq[:, :, 0:C].rearrange("p t (h d) -> p t h d", d=D), AX.X, ALU.add))
                step(b, V.tensor_scalar(rs_v[:, 0:NT * H], red[:, 1].rearrange("p t h -> p (t h)"), 1.0 / D, EPS_LN,
                                        ALU.mult, ALU.add))
                rsqrt(b, NT * H)
                V.tensor_tensor(heads(nat[:]), heads(o1[:]), bc(rs_y[:, 0:NT * H], D), ALU.mult).then_inc(nat_ready, 1)
                side(4)
                side(5)
                if not first(b):
                    dve.wait_ge(base_ready, count(base_ready, b, 0))
                dve.wait_ge(single_filled, count(single_filled, b, S_WO1 + 1))
                V.tensor_tensor(x1[:], x[:], ps[:].rearrange("p (t c) -> p t c", t=NT), ALU.add).then_inc(x1_ready, 1)
                dve.wait_ge(x1_ready, count(x1_ready, b, 1))
                moments(b, x1)
                step(b, V.scalar_tensor_tensor(rs_v[:, NT:2 * NT], rs_v[:, 0:NT], EPS_RMS, mv[:, :, 1],
                                               ALU.mult, ALU.add))
                rsqrt(b, 2 * NT)
                r1, r12 = rs_y[:, 0:NT], rs_y[:, NT:2 * NT]
                for t in range(NT):
                    i = V.tensor_scalar(nat[:, t, :], x1[:, t, :], mv[:, t, 0:1], r12[:, t:t + 1],
                                        ALU.subtract, ALU.mult)
                i.then_inc(nat_ready, 1)
                for t in range(NT):
                    i = V.tensor_scalar(z[:, t, :], x1[:, t, :], mv[:, t, 0:1], r1[:, t:t + 1],
                                        ALU.subtract, ALU.mult)
                step(b, i)
                side(6)
                side(7)
                dve.wait_ge(v_ready, count(v_ready, b, 2 * NT))
                step(b, V.tensor_reduce(rs_t[:, :], sq.rearrange("p t (h d) -> p (t h) d", d=D), AX.X, ALU.add))
                step(b, V.tensor_scalar(rs_v[:, :], rs_t[:, :], 1.0 / D, EPS_RMS, ALU.mult, ALU.add))
                rsqrt(b, 2 * NT * H)
                ry = rs_y[:].rearrange("p (t s h) -> p t s h", t=NT, s=2)
                for t in range(NT):
                    i = V.tensor_tensor(qk[:, 1, t, :].rearrange("p (h d) -> p h d", d=D),
                                        pr[(U_QKV2 + t) % 4][:, C:2 * C].rearrange("p (h d) -> p h d", d=D),
                                        bc(ry[:, t, 1, :], D), ALU.mult)
                i.then_inc(k2_ready, 1)
                step(b, V.tensor_tensor(rw.rearrange("p t (h d) -> p t h d", d=D), bc(ry[:, :, 0, :], D),
                                        wqk[:].unsqueeze(1).unsqueeze(1).broadcast_to([128, NT, H, D]), ALU.mult))
                for t in range(NT):
                    V.tensor_tensor(qk[:, 0, t, :], pr[(U_QKV2 + t) % 4][:, 0:C], rw[:, t, :], ALU.mult)\
                        .then_inc(qkv2_read, 1)
                dve.wait_ge(k2_ready, count(k2_ready, b, 1))
                low_parts(b, 1, 1)
                dve.wait_ge(qkv2_read, count(qkv2_read, b, NT))
                low_parts(b, 1, 0)
                for n, dst in enumerate((ks, qs)):
                    for g in (1, 3):
                        V.tensor_copy(dst[:, g, :], ring(b, U_STK2 + G * n + g)[:, :]).then_inc(stack_b, 1)
                side(8)
                side(9)
                side(10)
                side(11)
                assert done[front_step] == FRONT_STEPS, done

            def attend(b, side):
                done[tail_step] = 0
                go = lambda ins: step(b, ins, tail_step)

                def take_output(g):
                    dve.wait_ge(weighed, count(weighed, b, NT + NT * (g + 1)))
                    V.tensor_copy(oT[:, g, :], po[:]).then_inc(oT_ready, 1)

                for at, (kind, g, n) in enumerate(ORDER):
                    if kind == "max":
                        qt, kt = MAX_UNITS[n]
                        V.tensor_reduce(mxp[:, qt, :, kt], ring(b, U_AB + at)[:].rearrange("p (j n) -> p j n", j=J),
                                        AX.X, ALU.max).then_inc(max_read, 1)
                        if n == NU - 1:
                            dve.wait_ge(max_read, count(max_read, b, NU * (g + 1)))
                            go(V.tensor_reduce(mxm[:].rearrange("p t j -> p (t j)"), mxp[:].rearrange("p t j k -> p (t j) k"),
                                               AX.X, ALU.max))
                            V.tensor_scalar(mneg[:, g], mxm[:], -1.0, None, ALU.mult).then_inc(mneg_ready, 1)
                    if at in OT_AT:
                        take_output(OT_AT[at])
                    beside(at, side)
                take_output(G - 1)
                for t in range(NT):
                    src = ring(b, U_N2 + t)[:].rearrange("p (h s) -> p h s", s=SW)
                    go(V.reciprocal(rcp[:, t, :], src[:, :, D]))
                    V.tensor_tensor(nat[:, t, :].rearrange("p (h d) -> p h d", d=D), src[:, :, 0:D], bc(rcp[:, t, :], D),
                                    ALU.mult).then_inc(n2_read, 1)
                side(RET)
                dve.wait_ge(single_filled, count(single_filled, b, S_WO2 + 1))
                V.tensor_tensor(z[:, :, M0:C], z[:, :, M0:C], ps[:, 0:NT * CM].rearrange("p (t c) -> p t c", t=NT),
                                ALU.add).then_inc(y_ready, 1)
                dve.wait_ge(ysq_ready, count(ysq_ready, b, 1))
                go(V.tensor_scalar(rs_v[:, 0:NT], gsum[:, 0, :], 1.0 / C, EPS_RMS, ALU.mult, ALU.add))
                rsqrt(b, NT, tail_step)
                for t in range(NT):
                    i = V.tensor_scalar(nat[:, t, :], z[:, t, :], rs_y[:, t:t + 1], None, ALU.mult)
                i.then_inc(xf_ready, 1)
                side(RET + 1)
                assert done[tail_step] == TAIL_STEPS, done

            def back(b, part):
                go = lambda ins: step(b, ins, back_step)
                if part == 0:
                    done[back_step] = 0
                    dve.wait_ge(expert_filled, count(expert_filled, b, X_GATE + 1))
                    logits = px[X_GATE % 2][:, 0:NT * E].rearrange("p (t e) -> p t e", e=E)
                    V.tensor_scalar(gl[:, 0], logits, 0.0, FMAX, ALU.max, ALU.min)
                    V.tensor_scalar(gl[:, 1], logits, 0.0, -FMAX, ALU.min, ALU.max).then_inc(logits_read, 1)
                    dve.wait_ge(logits_read, count(logits_read, b, 1))
                    go(V.tensor_tensor(gl[:, 4], gl[:, 0], gl[:, 1], ALU.add))
                    go(V.tensor_reduce(bsum[:, 0, :], gl[:, 4], AX.X, ALU.max))
                    V.tensor_tensor(gl[:, 2], gl[:, 4], bc(bsum[:, 0, :], E), ALU.subtract).then_inc(logits_ready, 1)
                if part == 3:
                    dve.wait_ge(gexp_ready, count(gexp_ready, b, 1))
                    go(V.tensor_reduce(bsum[:, 1, :], gl[:, 3], AX.X, ALU.add))
                    go(V.reciprocal(bsum[:, 2, :], bsum[:, 1, :]))
                    go(V.tensor_tensor(gl[:, 5], gl[:, 3], bc(bsum[:, 2, :], E), ALU.mult))
                    pf = gl[:, 5].unsqueeze(2).broadcast_to([128, NT, E, E])
                    pe_ = bc(gl[:, 5], E)
                    V.tensor_tensor(beats[:, 0], pf, pe_, ALU.is_gt)
                    go(V.tensor_tensor(beats[:, 1], pf, pe_, ALU.is_ge))
                    go(V.tensor_tensor(beats[:, 2], beats[:, 1], beats[:, 0], ALU.subtract))
                    first = ww["t_first"][:].unsqueeze(1).broadcast_to([128, NT, E * E])
                    flat = lambda k: beats[:, k].rearrange("p t e f -> p t (e f)")
                    go(V.tensor_tensor(flat(1), flat(2), first, ALU.mult))
                    go(V.tensor_tensor(flat(2), flat(0), flat(1), ALU.add))
                    go(V.tensor_reduce(gl[:, 6], beats[:, 2], AX.X, ALU.add))
                    go(V.tensor_scalar(gl[:, 7], gl[:, 6], 1.5, None, ALU.is_lt))
                    go(V.tensor_tensor(gl[:, 6], gl[:, 7], gl[:, 5], ALU.mult))
                    go(V.tensor_reduce(bsum[:, 0, :], gl[:, 6], AX.X, ALU.add))
                    go(V.tensor_scalar(bsum[:, 1, :], bsum[:, 0, :], 1e-8, None, ALU.add))
                    go(V.reciprocal(bsum[:, 2, :], bsum[:, 1, :]))
                    go(V.tensor_tensor(wts[:], gl[:, 6], bc(bsum[:, 2, :], E), ALU.mult))
                if part in (1, 2):
                    m = part - 1
                    dve.wait_ge(expert_filled, count(expert_filled, b, X_E1 + 2 * m + 2))
                    dve.wait_ge(h_ready, count(h_ready, b, 1 + m))
                    V.tensor_tensor(h1[:, m, :], px[(X_E1 + 1) % 2][:], sil[:, m, :], ALU.mult).then_inc(h1_ready, 1)
                if part >= 8:
                    if part == 8:
                        dve.wait_ge(base_ready, count(base_ready, b, 1))
                    for t in (part - 8,):
                        dve.wait_ge(expert_filled, count(expert_filled, b, X_DN + t + 1))
                        for e in range(E):
                            i = V.scalar_tensor_tensor(yout[:, t, M0:C], px[(X_DN + t) % 2][:, e * CM:(e + 1) * CM],
                                                       wts[:, t, e:e + 1], yout[:, t, M0:C], ALU.mult, ALU.add)
                            if e < E - 1:
                                step(b, i, back_step)
                            else:
                                i.then_inc(down_read, 1)
                    assert part < FFN_PARTS - 1 or done[back_step] == BACK_STEPS, done

            dve.wait_ge(loaded, 16 * len(ww))
            V.tensor_copy(idb[:], ident[:]).then_inc(consts_ready, 1)
            V.tensor_copy(negb[:], neg32[:].unsqueeze(1).broadcast_to([128, J, 128])).then_inc(consts_ready, 1)
            V.tensor_scalar(negkb[:], tri[:].unsqueeze(1).broadcast_to([128, J, 128]), 1.0, -NEG, ALU.subtract, ALU.mult)
            V.tensor_tensor(wqk[:], ww["w_qk"][:, 0:D], ww["w_qk"][:, D:2 * D], ALU.mult).then_inc(consts_ready, 1)
            V.memset(mxp[:], NEG)
            V.memset(v2[:], 0.0).then_inc(consts_ready, 1)
            dve.wait_ge(consts_ready, N_CONSTS - 1)
            V.memset(v2h[:, :, :, D:D + 1], 1.0).then_inc(consts_ready, 1)
            V.memset(wts[:], 0.0).then_inc(down_read, NT)
            dve.wait_ge(consts_ready, N_CONSTS)
            run(dve, lead, front, attend, back)

        @block.gpsimd
        def _(pool):
            Q = nc.gpsimd

            def masked(b, t):
                for n in range(2):
                    pool.wait_ge(p1_copied, count(p1_copied, b, 2 * t + n + 1))
                    apart(pool)
                    half = p1[:, t % 2, 2 * n + 1]
                    Q.affine_select(out=half, in_=half, compare_op=ALU.is_ge, fill=0.0, base=0,
                                    pattern=[[0, J], [1, 128]], channel_multiplier=-1).then_inc(p1_masked, 1)

            def lead(b, part):
                if part == 4:
                    pool.wait_ge(v_ready, count(v_ready, b, NT))
                    Q.tensor_tensor(cosp, raw, cos_t, ALU.mult).then_inc(cos_ready, 1)
                if part == 6:
                    pool.wait_ge(cos_ready, count(cos_ready, b, 1))
                    pool.wait_ge(sin_ready, count(sin_ready, b, 2))
                    Q.tensor_tensor(qk[:].rearrange("p s t c -> p t s c"), cosp.rearrange("p t (s c) -> p t s c", s=2),
                                    sinp.rearrange("p t (s c) -> p t s c", s=2), ALU.add).then_inc(qk_ready, 1)
                if part in (7, 8):
                    s = part - 7
                    pool.wait_ge(high_ready, count(high_ready, b, s + 1))
                    src = qk[:, s].rearrange("p t (h d) -> p (t h) d", d=D)
                    st = stack[:, s].rearrange("p t h s -> p (t h) s")
                    at = (2 * D, D)[s]
                    Q.tensor_tensor(st[:, :, at:at + D], src, st[:, :, 0:D].bitcast(f32), ALU.subtract)\
                        .then_inc(low_ready, 1)
                if part >= RET:
                    masked(b, part - RET)

            def attend(b, side):
                for part in range(RET):
                    side(part)
                side(RET)
                pool.wait_ge(y_ready, count(y_ready, b, 1))
                pool.wait_ge(out_stored, count(out_stored, b, 0))
                Q.tensor_tensor(yout[:], x1[:], z[:], ALU.add).then_inc(base_ready, 1)
                side(RET + 1)

            def front(b, side):
                masked(b, 2)
                masked(b, 3)

            Q.memset(stack[:].bitcast(f32), 0.0).then_inc(pool_made, 1)
            pool.wait_ge(pool_made, 1)
            Q.memset(stack[:, 1, :, :, SHIFT:SHIFT + 1].bitcast(f32), 1.0).then_inc(consts_ready, 1)
            Q.memset(qx[:].bitcast(f32), 0.0).then_inc(consts_ready, 1)
            Q.memset(kx[:].bitcast(f32), 0.0).then_inc(consts_ready, 1)
            Q.memset(cross[:, 0:128], 0.0).then_inc(consts_ready, 1)
            Q.memset(yout[:], 0.0).then_inc(out_stored, 16)
            nothing = lambda b, part: None
            run(pool, lead, front, attend, nothing)

        @block.sync
        def _(sp):
            out_v = A["out"].rearrange("b (t p) c -> b p t c", p=128)

            def expand_q(b, layer, src, some):
                for j in range(J):
                    sp.dma_start(qx[32 * j:32 * j + 32, some, j, :].bitcast(f32),
                                 src[32 * j:32 * j + 32, some, :].bitcast(f32)).then_inc(qx_ready, 16)

            def expand_k(b, g):
                read, n = stack_read(1, 1, g)
                sp.wait_ge(read, count(read, b, n))
                if g >= 2:
                    apart(sp)
                    sp.wait_ge(ring_filled, count(ring_filled, b, U_AB + PLACE["max", g - 2, NU - 1] + 1))
                for j in range(J):
                    sp.dma_start(kx[32 * j:32 * j + 32, g % 2, j, :].bitcast(f32),
                                 ks[32 * j:32 * j + 32, g, :].bitcast(f32)).then_inc(kx_ready[g % 2], 16)

            def shift(b, g):
                sp.wait_ge(mT_ready, count(mT_ready, b, g + 1))
                apart(sp)
                sp.wait_ge(qx_ready, count(qx_ready, b, 12 * 16))
                for j in range(J):
                    sp.dma_start(qx[32 * j + SHIFT:32 * j + SHIFT + 1, g, j, :].bitcast(f32),
                                 mT[j:j + 1, g % 2, :].bitcast(f32)).then_inc(shift_ready[g % 2], 16)

            def lead(b, part):
                if part == RET:
                    sp.wait_ge(stack_a, count(stack_a, b, 2))
                    sp.wait_ge(stack_b, count(stack_b, b, 2))
                    for end in (G - 1, G):
                        if not first(b):
                            apart(sp)
                            sp.wait_ge(ring_filled, count(ring_filled, b - 1, U_AB + PLACE["exp", end - 1, NU - 1] + 1))
                        expand_q(b, 0, qs1, slice(0, G - 1) if end < G else slice(G - 1, G))

            def front(b, side):
                expand_k(b, 0)
                expand_k(b, 1)
                sp.wait_ge(stack_a, count(stack_a, b, 2 * G))
                sp.wait_ge(stack_b, count(stack_b, b, 2 * G))
                expand_q(b, 1, qs, slice(0, G))
                side(FFN_PARTS - 1)

            def attend(b, side):
                expand_k(b, 2)
                shift(b, 0)
                expand_k(b, 3)
                for g in range(1, G):
                    shift(b, g)
                side(RET)

            def back(b, part):
                if part == FFN_PARTS - 1:
                    sp.wait_ge(down_read, count(down_read, b, NT))
                    sp.dma_start(out_v[b], yout[:]).then_inc(out_stored, 16)

            for name, dst in ww.items():
                sp.dma_start(dst[:], A[name]).then_inc(loaded, 16)
            run(sp, lead, front, attend, back)
            sp.wait_ge(out_stored, count(out_stored, B, 0))


def kernel(**inputs):
    import numpy as _np
    import concourse.bacc as _bacc
    from concourse import mybir as _mybir
    from concourse.bass_utils import run_bass_kernel_spmd as _run

    I = {k: _np.asarray(v) for k, v in inputs.items()}
    a = lambda n: I["L0_attn_" + n]
    w = lambda n: I["L0_ffn_" + n]
    cat = _np.concatenate

    def blocks(m, n=None):
        m = m if n is None else m[:, n:]
        return m.reshape(-1, 128, m.shape[1]).transpose(1, 0, 2).reshape(128, -1)

    rows = lambda v: _np.broadcast_to(v[None, :], (128, v.shape[0]))
    arrays = {
        "x": a("x"),
        "w_qkv1": cat([a("Wq").T, a("Wk").T, a("Wv").T], 1),
        "w_o1": a("Wo").T,
        "w_gn": _np.stack([a("gn_weight"), a("gn_bias")], 1),
        "w_n12": _np.stack([w("n1_w"), w("n2_w")], 1),
        "w_qkv2": cat([w("wq").T, w("wk").T, w("wv").T], 1),
        "w_o2": w("wo").T[:, M0:],
        "w_qk": cat([rows(w("qn_w")), rows(w("kn_w"))], 1),
        "w_gate": w("gate_w").T,
        "w_u0": w("e0_up").T, "w_dn0": blocks(w("e0_down").T, M0),
        "w_g1": w("e1_w1").T, "w_u1": w("e1_w2").T, "w_dn1": blocks(w("e1_down").T, M0),
        "w_l1": w("e2_l1").T, "w_l2": blocks(w("e2_l2").T), "w_l3": blocks(w("e2_l3").T),
        "w_dn2": blocks(w("e2_l4").T, M0),
        "w_d3": w("e3_down").T, "w_u3": w("e3_up").T, "w_dn3": blocks(w("e3_out").T, M0),
    }
    arrays.update(tables())
    nc = _bacc.Bacc("TRN2", target_bir_lowering=False, num_devices=1)
    A, send = {}, {}
    for name, v in arrays.items():
        v = _np.ascontiguousarray(v)
        send[name + "_dram"] = v
        A[name] = nc.dram_tensor(name + "_dram", v.shape, _mybir.dt.from_np(v.dtype), kind="ExternalInput").ap()
    A["out"] = nc.dram_tensor("out_dram", (B, T, C), _mybir.dt.float32, kind="ExternalOutput").ap()
    build(nc, A)
    r = _run(nc, [send], core_ids=[0])
    return r.results[0]["out_dram"]
```

```python
import numpy as np
from contextlib import ExitStack

import concourse.bass as bass
from concourse import mybir

B, T, C = 8, 512, 128
H, D = 16, 8
NT = T // 128
G, J = 4, 4
SW = 32
SHIFT = 3 * D
M0 = 32
CM = C - M0
E = 4
HID = 256
EPS_LN, EPS_RMS = 1e-5, 1.1920929e-07
NEG = -1e30
FMAX = float(np.finfo(np.float32).max)
RSQRT_SEED = 0x5F3759DF
PROJECTION = ("t_id", "w_qkv1")
ROTATION = ("t_cos", "t_sin", "t_state", "t_g128")

U_SC1 = 0
U_N1 = U_SC1 + NT * G
U_QKV2 = U_N1 + NT
U_STK2 = U_QKV2 + NT
U_AB = U_STK2 + 2 * G
MAX_UNITS = [(qt, kt) for qt in range(NT) for kt in range(qt + 1)]
EXP_UNITS = [(kt, qt) for kt in range(NT) for qt in range(kt, NT)]
NU = len(MAX_UNITS)
by = lambda kind, g: [(kind, g, n) for n in range(NU)]
mixed = lambda a, b: [u for two in zip(a, b) for u in two]
AHEAD = 14
MAXIMA = [u for g in range(G) for u in by("max", g)]
EXPS = [u for g in range(G) for u in by("exp", g)]
ORDER = MAXIMA[:NU + AHEAD] + mixed(EXPS, MAXIMA[NU + AHEAD:]) + EXPS[(G - 1) * NU - AHEAD:]
PLACE = {u: i for i, u in enumerate(ORDER)}
MT_AT = {PLACE["max", g, NU - 1] + 3: g for g in range(G)}
WEIGH_AT = {}
for g in range(G):
    for kt in range(NT):
        after = NU * g + EXP_UNITS.index((kt, NT - 1)) + (3, 3, 1, 2)[kt]
        WEIGH_AT.setdefault(PLACE[EXPS[min(after, G * NU - 1)]], []).append((g, kt))
OT_AT = {PLACE["exp", g + 1, 3]: g for g in range(G - 1)}
DOWN = 100
LEAD_AT = (9, 14, 19, 24, 29, 34, 39, 44, 49, 54, 59, 64, 69)
DOWN_AT = (0, 1, 3, 5)
EARLY_DOWN = 2
SIDE_AT = {at: 2 + n for n, at in enumerate(LEAD_AT)}
SIDE_AT.update({at: DOWN + t for t, at in enumerate(DOWN_AT)})
U_N2 = U_AB + len(ORDER)
RING_UNITS = U_N2 + NT
S_ON, S_WO1, S_H, S_K0, S_MT, S_AO, S_WO2, S_XF, S_UNITS = 0, 1, 2, 3, 4, 8, 9, 10, 11
L_XN, L_QKV, L_QT, L_ST, L_STK, L_CROSS, L_UNITS = 0, 1, 5, 6, 9, 17, 18
X_GATE, X_E1, X_L1, X_D3, X_L2, X_U3, X_L3, X_U0, X_DN, X_UNITS = 0, 1, 5, 7, 8, 10, 12, 14, 16, 20

RET = 15
LEAD_PARTS, FFN_PARTS = RET + 2, 8
FFN_AT = {"start": (0,), "scored": (1,), "weighed": (2,), "spread": (3,), "projected": (4, 5), "normed": (6, 7)}
LEAD_EARLY = {"start": -1, "weighed": 0, "projected": 1}
LEAD_STEPS, FRONT_STEPS, TAIL_STEPS, BACK_STEPS, N_CONSTS = 14, 44, 20, 15, 8


def tables():
    f = np.float32
    inv = (f(1.0) / f(10000.0) ** (np.arange(0, D, 2, dtype=f) / f(D))).astype(f)
    ang = (np.arange(T, dtype=f)[:, None] * inv[None, :]).astype(f)
    ang = np.concatenate([ang, ang], -1).astype(np.float64)
    gam = 1.0 - 2.0 ** (-5.0 - np.arange(H, dtype=np.float64))
    sign = np.where(np.arange(D) < D // 2, -1.0, 1.0)
    loc = np.arange(T) % 128
    dq = gam[None, :] ** loc[:, None] / np.sqrt(D)
    dk = gam[None, :] ** (-loc[:, None].astype(np.float64))
    cos, sin = np.cos(ang), np.sin(ang) * sign
    lay = lambda d, a: (d[:, :, None] * a[:, None, :]).reshape(T, C)
    cosd = np.concatenate([lay(dq, cos), lay(dk, cos)], 1).reshape(NT, 128, 2 * C).transpose(1, 0, 2)
    sind = np.concatenate([lay(dq, sin), lay(dk, sin)], 1).reshape(NT, 128, 2 * C).transpose(1, 0, 2)
    g128 = np.repeat(gam ** 128, D)
    same = np.arange(C)[:, None] // D == np.arange(C)[None, :] // D
    r = np.arange(128)
    return {
        "t_cos": np.ascontiguousarray(cosd.reshape(128, -1)).astype(f),
        "t_sin": np.ascontiguousarray(sind.reshape(128, -1)).astype(f),
        "t_state": (same * g128[:, None]).astype(f),
        "t_g128": g128[:, None].astype(f),
        "t_tri": (r[:, None] <= r[None, :]).astype(f),
        "t_neg": np.where(r[None, :] > r[:, None], NEG, 0.0).astype(f),
        "t_id": np.eye(128, dtype=f),
        "t_first": np.tile((np.arange(E)[None, :] < np.arange(E)[:, None]).astype(f).reshape(1, E * E), (128, 1)),
    }


def build(nc, A):
    f32, f32r, bf16, i32 = mybir.dt.float32, mybir.dt.float32r, mybir.dt.bfloat16, mybir.dt.int32
    ALU, ACT, AX = mybir.AluOpType, mybir.ActivationFunctionType, mybir.AxisListType
    ctx = ExitStack()
    with ctx:
        def sb(name, shape, dt=f32):
            return ctx.enter_context(nc.sbuf_tensor(name, shape, dt))

        def pb(name, shape):
            return ctx.enter_context(nc.psum_tensor(name, shape, f32))

        def sem(name):
            return ctx.enter_context(nc.semaphore(name))

        ww = {}
        for name, ap in A.items():
            if name.startswith(("w_", "t_")):
                ww[name] = sb("sb_" + name, list(ap.shape))
        w1, wo1, w2, wo2 = (ww[n] for n in ("w_qkv1", "w_o1", "w_qkv2", "w_o2"))
        ident, tri, neg32 = ww["t_id"], ww["t_tri"], ww["t_neg"]
        cos_t = ww["t_cos"][:].rearrange("p (t c) -> p t c", t=NT)
        sin_t = ww["t_sin"][:].rearrange("p (t c) -> p t c", t=NT)
        idb = sb("idb", [128, 128], bf16)
        negb = sb("negb", [128, J, 128], bf16)
        negkb = sb("negkb", [128, J, 128], bf16)
        wqk = sb("wqk", [128, D])

        x = sb("x", [128, NT, C])
        x_in = sb("x_in", [128, NT, C])
        xn = sb("xn", [128, NT, C])
        nat = sb("nat", [128, NT, C])
        chT = sb("chT", [128, T])
        stats = sb("stats", [128, NT, 6])
        mv = sb("mv", [128, NT, 2])
        mv_in = sb("mv_in", [128, NT, 2])
        rs_v = sb("rs_v", [128, 128])
        rs_i = sb("rs_i", [128, 128], i32)
        rs_y = sb("rs_y", [128, 128])
        rs_t = sb("rs_t", [128, 128])
        qk = sb("qk", [128, 2, NT, C])
        v1 = sb("v1", [128, NT, C])
        v2 = sb("v2", [128, NT, H * (D + 1) + SW])
        v2h = v2[:, :, 0:H * (D + 1)].rearrange("p t (h s) -> p t h s", s=D + 1)
        stack = sb("stack", [128, 2, NT, H, SW], f32r)
        qs1 = sb("qs1", [128, G, T], f32r)
        ks1 = sb("ks1", [128, G, T], f32r)
        qs = sb("qs", [128, G, T], f32r)
        ks = sb("ks", [128, G, T], f32r)
        qx = sb("qx", [128, G, J, T], f32r)
        kx = sb("kx", [128, 2, J, T], f32r)
        state = sb("state", [128, 3, C])
        state_in = sb("state_in", [128, C])
        cross = sb("cross", [128, T])
        p = sb("p", [128, 2, 4, T])
        p1 = p[:].rearrange("p a g (j n) -> p a g j n", j=J)

        def p2(kt):
            return p[:, kt % 2, :, 0:128] if kt == NT - 1 else p[:, kt % 2, :, kt * 128:T]

        oT = sb("oT", [128, 4, T])
        o1 = sb("o1", [128, NT, C])
        sq = oT[:, 0:2, :].rearrange("p a (b c) -> p (a b) c", b=2)
        weighted = oT[:, :, 0:E * CM].rearrange("p t (e c) -> p t e c", e=E)
        rw = oT[:, 2, :].rearrange("p (t c) -> p t c", t=NT)
        red = sb("red", [128, 2, NT, H])
        x1 = sb("x1", [128, NT, C])
        z = sb("z", [128, NT, C])
        mxp = sb("mxp", [128, NT, J, NT])
        mneg = sb("mneg", [128, G, NT, J])
        rcp = sb("rcp", [128, NT, H])
        xfT = sb("xfT", [128, T])
        gl = sb("gl", [128, 8, NT, E])
        mxm = sb("mxm", [128, NT, J])
        bsum = sb("bsum", [128, 3, NT])
        beats = sb("beats", [128, 3, NT, E, E])
        gsum = sb("gsum", [128, 4, NT])
        wts = sb("wts", [128, NT, E])
        hA = sb("hA", [128, 2, T])
        hB = sb("hB", [128, 2, T])
        h0 = sb("h0", [128, 2, T])
        h1 = sb("h1", [128, 2, T])
        h3a = h0[:, 0, :]
        h3 = sb("h3", [128, 2, T])
        sil = hB
        mT = h3[0:J, :, :].bitcast(f32r)
        halved = lambda ap: ap[:].rearrange("p a (b c) -> p (a b) c", b=2)
        raw, cosp, sinp = halved(h1), halved(hA), halved(hB)
        qT = h0[:, 0, :]
        yout = sb("yout", [128, NT, C])

        pr = [pb(f"ring{i}", [128, 512]) for i in range(4)]
        ps = pb("single", [128, 512])
        po = pb("outs", [128, 512])
        px = [pb(f"side{i}", [128, 512]) for i in range(2)]

        waits_carried = {nc.vector: sem("waits_carried_dve"), nc.gpsimd: sem("waits_carried_pool"), nc.sync: sem("waits_carried_sp")}
        gains = {}
        starts = {}

        def counted(name, gain):
            s = sem(name)
            gains[s] = gain
            return s

        projection_loaded = sem("projection_loaded")
        rotation_loaded = sem("rotation_loaded")
        loaded = sem("loaded")
        stack_cleared = sem("stack_cleared")
        pool_made = sem("pool_made")
        consts_ready = sem("consts_ready")
        x_loaded = counted("x_loaded", 16)
        out_stored = counted("out_stored", 16)
        starts[out_stored] = 16
        ring_filled = counted("ring_filled", RING_UNITS)
        single_filled = counted("single_filled", S_UNITS)
        lead_filled = counted("lead_filled", L_UNITS)
        expert_filled = counted("expert_filled", X_UNITS)
        weighed = counted("weighed", NT + G * NT)
        x_kept = counted("x_kept", 1)
        xn_ready = counted("xn_ready", 1)
        xnT_ready = counted("xnT_ready", 1)
        nat_ready = counted("nat_ready", 2)
        chT_ready = counted("chT_ready", 2)
        v_ready = counted("v_ready", 2 * NT)
        sin_ready = counted("sin_ready", 2)
        cos_ready = counted("cos_ready", 1)
        qk_ready = counted("qk_ready", 1)
        high_ready = counted("high_ready", 4)
        low_ready = counted("low_ready", 4)
        qT_ready = counted("qT_ready", 1)
        state_read = counted("state_read", 3)
        state_ready = counted("state_ready", 2)
        cross_ready = counted("cross_ready", 1)
        stack_a = counted("stack_a", 2 * G)
        stack_b = counted("stack_b", 2 * G)
        qx_ready = counted("qx_ready", 12 * 16)
        k0_spread_a = counted("k0_spread_a", 1)
        k0_spread_b = counted("k0_spread_b", 1)
        kx_ready = [counted(f"kx_ready{i}", (1 + i) * J * 16) for i in range(2)]
        shift_ready = [counted(f"shift_ready{i}", 2 * J * 16) for i in range(2)]
        p1_ready = counted("p1_ready", 2 * NT)
        p1_copied = counted("p1_copied", 2 * NT)
        p1_masked = counted("p1_masked", 2 * NT)
        oT_ready = counted("oT_ready", 8)
        o1_copied = counted("o1_copied", NT)
        centred = counted("centred", 1)
        squared = counted("squared", 1)
        x1_ready = counted("x1_ready", 1)
        qkv2_read = counted("qkv2_read", NT)
        k2_ready = counted("k2_ready", 1)
        max_read = counted("max_read", G * NU)
        mneg_ready = counted("mneg_ready", G)
        mT_ready = counted("mT_ready", G)
        exp_done = counted("exp_done", G * NU)
        n2_read = counted("n2_read", NT)
        aoT_ready = counted("aoT_ready", 1)
        y_ready = counted("y_ready", 1)
        ysq_ready = counted("ysq_ready", 1)
        xf_ready = counted("xf_ready", 1)
        xfT_ready = counted("xfT_ready", 1)
        base_ready = counted("base_ready", 1)
        logits_read = counted("logits_read", 1)
        logits_ready = counted("logits_ready", 1)
        gexp_ready = counted("gexp_ready", 1)
        h_ready = counted("h_ready", 13)
        wts_ready = counted("wts_ready", 1)
        h1_ready = counted("h1_ready", 2)
        down_read = counted("down_read", NT)
        sum_step = counted("sum_step", 2 * NT)
        out_ready = counted("out_ready", NT)
        starts[down_read] = NT
        front_step = counted("front_step", FRONT_STEPS)
        lead_step = counted("lead_step", LEAD_STEPS)
        tail_step = counted("tail_step", TAIL_STEPS)
        back_step = counted("back_step", BACK_STEPS)

        def count(s, b, n):
            return b * gains[s] + n + starts.get(s, 0)

        def first(b):
            return isinstance(b, int) and b == 0

        def apart(eng):
            eng.sem_inc(waits_carried[eng], 1)

        def heads(ap):
            return ap.rearrange("p t (h d) -> p (t h) d", d=D)

        def bc(ap, n):
            return ap.unsqueeze(len(ap.shape)).broadcast_to(list(ap.shape) + [n])

        def turn(layer, s):
            return s if layer == 0 else 1 - s

        def stack_read(layer, s, g):
            return (stack_a, stack_b)[g % 2], G * layer + 2 * turn(layer, s) + g // 2 + 1

        ring_read = {}
        for n in range(NT * G):
            ring_read[U_SC1 + n] = ((p1_ready, p1_copied)[n % 2], n // 2 + 1)
        for t in range(NT):
            ring_read[U_N1 + t] = (o1_copied, t + 1)
            ring_read[U_QKV2 + t] = (qkv2_read, t + 1)
            ring_read[U_N2 + t] = (n2_read, t + 1)
        for n in range(2 * G):
            ring_read[U_STK2 + n] = stack_read(1, 1 - n // G, n % G) if n else (k0_spread_b, 1)
        for at, (kind, g, n) in enumerate(ORDER):
            ring_read[U_AB + at] = ({"max": max_read, "exp": exp_done}[kind], NU * g + n + 1)
        single_read = {S_ON: (chT_ready, 1), S_WO1: (x1_ready, 1), S_H: (chT_ready, 2), S_K0: stack_read(1, 1, 0), S_AO: (aoT_ready, 1),
                       S_WO2: (y_ready, 1), S_XF: (xfT_ready, 1)}
        for g in range(G):
            single_read[S_MT + g] = (mT_ready, g + 1)
        lead_read = {L_XN: (xnT_ready, 1), L_QT: (qT_ready, 1), L_CROSS: (cross_ready, 1)}
        for t in range(NT):
            lead_read[L_QKV + t] = (v_ready, t + 1)
        for t in range(NT - 1):
            lead_read[L_ST + t] = (state_read, t + 1)
        for n in range(2 * G):
            lead_read[L_STK + n] = stack_read(0, n // G, n % G)
        expert_read = {X_GATE: (logits_read, 1), X_D3: (h_ready, 5)}
        for m in range(2):
            for u, n in ((X_L1, 3), (X_L2, 6), (X_U3, 8), (X_L3, 10), (X_U0, 12)):
                expert_read[u + m] = (h_ready, n + m)
            expert_read[X_E1 + 2 * m] = (h_ready, 1 + m)
            expert_read[X_E1 + 2 * m + 1] = (h1_ready, m + 1)
        for t in range(NT):
            expert_read[X_DN + t] = (down_read, t + 1)

        def before(b, u, back, units):
            return (b, u - back) if u >= back else (b - 1, u - back + units)

        block = ctx.enter_context(nc.Block())

        def run(eng, lead, front, attend, ffn, down, ready):
            def beside_attention(b, before, after):
                def side(part):
                    if part < DOWN and after:
                        lead(b + 1, part)
                    if part >= DOWN and before and not (eng is nc.tensor and part - DOWN < EARLY_DOWN):
                        down(b - 1, part - DOWN)
                attend(b, side)

            def beside_front(b, before, after):
                def side(place):
                    if after and place in LEAD_EARLY:
                        lead(b + 1, LEAD_EARLY[place])
                    if before:
                        for part in FFN_AT[place]:
                            ffn(b - 1, part)
                    if before and eng is nc.tensor and place == "normed":
                        for t in range(EARLY_DOWN):
                            down(b - 1, t)
                front(b, side)

            for part in range(-1, 5):
                lead(0, part)
            ready()
            for part in range(5, LEAD_PARTS):
                lead(0, part)
            beside_front(0, False, True)
            beside_attention(0, False, True)
            with eng.Fori(1, B - 1) as b:
                beside_front(b, True, True)
                beside_attention(b, True, True)
            beside_front(B - 1, True, False)
            beside_attention(B - 1, True, False)
            for part in range(FFN_PARTS):
                ffn(B - 1, part)
            for t in range(NT):
                down(B - 1, t)

        def beside(at, side):
            if at in SIDE_AT:
                side(SIDE_AT[at])

        @block.tensor
        def _(pe):
            def ring(b, u):
                bb, prev = before(b, u, 4, RING_UNITS)
                if not (isinstance(bb, int) and bb < 0):
                    pe.wait_ge(ring_read[prev][0], count(ring_read[prev][0], bb, ring_read[prev][1]))
                return pr[u % 4]

            def single(b, u):
                bb, prev = before(b, u, 1, S_UNITS)
                if not (isinstance(bb, int) and bb < 0):
                    pe.wait_ge(single_read[prev][0], count(single_read[prev][0], bb, single_read[prev][1]))

            def leading(b, u):
                if u >= 2:
                    pe.wait_ge(lead_read[u - 2][0], count(lead_read[u - 2][0], b, lead_read[u - 2][1]))
                elif not first(b):
                    pe.wait_ge(down_read, count(down_read, b - 2, NT - 1 + u))
                return px[u % 2]

            def expert(b, u):
                if u >= 2:
                    pe.wait_ge(expert_read[u - 2][0], count(expert_read[u - 2][0], b, expert_read[u - 2][1]))
                elif isinstance(b, int) and b == B - 1:
                    pe.wait_ge(down_read, count(down_read, b - 1, NT - 1 + u))
                else:
                    read, n = lead_read[L_UNITS - 2 + u]
                    pe.wait_ge(read, count(read, b + 1, n))
                return px[u % 2]

            def transposed(dst, src):
                for t in range(NT):
                    last = nc.tensor.transpose(dst[:, t * 128:(t + 1) * 128], src(t), ident[:])
                return last

            def stacked(dst, s, g):
                return transposed(dst, lambda t: stack[:, s, t, J * g:J * g + J, :]
                                  .rearrange("p j s -> p (j s)").bitcast(f32))

            def scores(b, t):
                for g in range(G):
                    dst = ring(b, U_SC1 + G * t + g)
                    nc.tensor.matmul(dst[:, :], ks1[:, g, t * 128:(t + 1) * 128],
                                     qx[:, g, :, t * 128:(t + 1) * 128], start=True, stop=True)\
                        .then_inc(ring_filled, 1)

            def weigh_retained(b, t):
                if t or not first(b):
                    pe.wait_ge(oT_ready, count(oT_ready, b, t))
                pe.wait_ge(p1_ready, count(p1_ready, b, 2 * (t + 1)))
                pe.wait_ge(p1_masked, count(p1_masked, b, 2 * (t + 1)))
                for g in range(G):
                    last = nc.tensor.matmul(po[32 * g:32 * g + 32, :], v1[:, t, 32 * g:32 * g + 32],
                                            p1[:, t % 2, g, :, :], start=True, stop=True)
                last.then_inc(weighed, 1)

            def lead(b, part):
                if part == 2:
                    pe.wait_ge(xn_ready, count(xn_ready, b, 1))
                    transposed(leading(b, L_XN), lambda t: xn[:, t, :]).then_inc(lead_filled, 1)
                if part in (3, 4):
                    pe.wait_ge(xnT_ready, count(xnT_ready, b, 1))
                    for t in (0, 1) if part == 3 else (2, 3):
                        dst = leading(b, L_QKV + t)
                        nc.tensor.matmul(dst[:, 0:3 * C], chT[:, t * 128:(t + 1) * 128], w1[:], start=True, stop=True)\
                            .then_inc(lead_filled, 1)
                if part == 7:
                    pe.wait_ge(qk_ready, count(qk_ready, b, 1))
                    transposed(leading(b, L_QT), lambda t: qk[:, 0, t, :]).then_inc(lead_filled, 1)
                if part in (7, 8, 9):
                        t = part - 7
                        dst = leading(b, L_ST + t)
                        nc.tensor.matmul(dst[:, 0:C], qk[:, 1, t, :], v1[:, t, :], start=True, stop=True)\
                            .then_inc(lead_filled, 1)
                if part in (10, 11, 12, 13):
                    s, g0 = (part - 10) // 2, 2 * ((part - 10) % 2)
                    pe.wait_ge(high_ready, count(high_ready, b, s + 1))
                    pe.wait_ge(low_ready, count(low_ready, b, s + 1))
                    for g in (g0, g0 + 1):
                        stacked(leading(b, L_STK + G * s + g), s, g).then_inc(lead_filled, 1)
                if part == 14:
                    dst = leading(b, L_CROSS)
                    pe.wait_ge(qT_ready, count(qT_ready, b, 1))
                    pe.wait_ge(state_ready, count(state_ready, b, 2))
                    for t in range(1, NT):
                        last = nc.tensor.matmul(dst[:, t * 128:(t + 1) * 128], state[:, t - 1, :],
                                                qT[:, t * 128:(t + 1) * 128], start=True, stop=True)
                    last.then_inc(lead_filled, 1)
                if part == RET:
                    pe.wait_ge(stack_a, count(stack_a, b, G))
                    pe.wait_ge(stack_b, count(stack_b, b, G))
                    pe.wait_ge(qx_ready, count(qx_ready, b, 8 * 16))
                    scores(b, 0)
                if part == RET + 1:
                    scores(b, 1)
                    weigh_retained(b, 0)

            def output(b, u, w, n):
                single(b, u)
                for t in range(NT):
                    last = nc.tensor.matmul(ps[:, t * n:(t + 1) * n], chT[:, t * 128:(t + 1) * 128], w[:],
                                            start=True, stop=True)
                last.then_inc(single_filled, 1)

            def front(b, side):
                side("start")
                scores(b, 2)
                weigh_retained(b, 1)
                scores(b, 3)
                weigh_retained(b, 2)
                side("scored")
                weigh_retained(b, 3)
                side("weighed")
                for t in range(NT):
                    pe.wait_ge(oT_ready, count(oT_ready, b, t + 1))
                    transposed(ring(b, U_N1 + t), lambda k: oT[:, t, k * 128:(k + 1) * 128]).then_inc(ring_filled, 1)
                side("spread")
                single(b, S_ON)
                pe.wait_ge(nat_ready, count(nat_ready, b, 1))
                transposed(ps, lambda t: nat[:, t, :]).then_inc(single_filled, 1)
                pe.wait_ge(chT_ready, count(chT_ready, b, 1))
                output(b, S_WO1, wo1, C)
                side("projected")
                single(b, S_H)
                pe.wait_ge(nat_ready, count(nat_ready, b, 2))
                transposed(ps, lambda t: nat[:, t, :]).then_inc(single_filled, 1)
                pe.wait_ge(chT_ready, count(chT_ready, b, 2))
                for t in range(NT):
                    dst = ring(b, U_QKV2 + t)
                    nc.tensor.matmul(dst[:, 0:3 * C], chT[:, t * 128:(t + 1) * 128], w2[:], start=True, stop=True)\
                        .then_inc(ring_filled, 1)
                side("normed")
                for n in range(2 * G):
                    s, g = 1 - n // G, n % G
                    pe.wait_ge(high_ready, count(high_ready, b, 2 + turn(1, s) + 1))
                    pe.wait_ge(low_ready, count(low_ready, b, 2 + turn(1, s) + 1))
                    stacked(ring(b, U_STK2 + n), s, g).then_inc(ring_filled, 1)
                    if n == 0:
                        single(b, S_K0)
                        stacked(ps, s, g).then_inc(single_filled, 1)

            def attend(b, side):
                def weigh(g, kt):
                    if kt == 0:
                        pe.wait_ge(oT_ready, count(oT_ready, b, 4 + g))
                    pe.wait_ge(exp_done, count(exp_done, b, NU * g + EXP_UNITS.index((kt, NT - 1)) + 1))
                    for j in range(J):
                        h = (D + 1) * (J * g + j)
                        last = nc.tensor.matmul(po[32 * j:32 * j + 32, kt * 128:T], v2[:, kt, h:h + SW],
                                                p2(kt)[:, j, :], start=kt == 0, stop=kt == NT - 1,
                                                skip_group_check=True)
                    last.then_inc(weighed, 1)

                pe.wait_ge(v_ready, count(v_ready, b, 2 * NT))
                for at, (kind, g, n) in enumerate(ORDER):
                    if kind == "max":
                        qt, kt = MAX_UNITS[n]
                        if n == 0:
                            read, last_read = stack_read(1, 0, g)
                            pe.wait_ge(read, count(read, b, last_read))
                            if g == 0:
                                pe.wait_ge(k0_spread_a, count(k0_spread_a, b, 1))
                                pe.wait_ge(k0_spread_b, count(k0_spread_b, b, 1))
                            else:
                                pe.wait_ge(kx_ready[g % 2], count(kx_ready[g % 2], b, (1, 1, 2)[g - 1] * J * 16))
                        dst = ring(b, U_AB + at)
                        last = nc.tensor.matmul(dst[:, :], qs[:, g, qt * 128:(qt + 1) * 128],
                                                kx[:, g % 2, :, kt * 128:(kt + 1) * 128], start=True, stop=kt < qt)
                        if kt == qt:
                            last = nc.tensor.matmul(dst[:, :], idb[:], negb[:, :, :], start=False, stop=True)
                        last.then_inc(ring_filled, 1)
                    else:
                        kt, qt = EXP_UNITS[n]
                        if n == 0:
                            if g == 0:
                                pe.wait_ge(qx_ready, count(qx_ready, b, 12 * 16))
                            pe.wait_ge(shift_ready[g % 2], count(shift_ready[g % 2], b, (g // 2 + 1) * J * 16))
                        dst = ring(b, U_AB + at)
                        last = nc.tensor.matmul(dst[:, :], ks[:, g, kt * 128:(kt + 1) * 128],
                                                qx[:, g, :, qt * 128:(qt + 1) * 128], start=True, stop=kt < qt)
                        if kt == qt:
                            last = nc.tensor.matmul(dst[:, :], idb[:], negkb[:, :, :], start=False, stop=True)
                        last.then_inc(ring_filled, 1)
                    if at in MT_AT:
                        gm = MT_AT[at]
                        single(b, S_MT + gm)
                        pe.wait_ge(mneg_ready, count(mneg_ready, b, gm + 1))
                        transposed(ps[0:J, :], lambda t: mneg[:, gm, t, :]).then_inc(single_filled, 1)
                    for g_kt in WEIGH_AT.get(at, []):
                        weigh(*g_kt)
                    beside(at, side)
                for t in range(NT):
                    if t == 0:
                        pe.wait_ge(oT_ready, count(oT_ready, b, 8))
                    transposed(ring(b, U_N2 + t), lambda k: oT[:, k, t * 128:(t + 1) * 128]).then_inc(ring_filled, 1)
                single(b, S_AO)
                pe.wait_ge(n2_read, count(n2_read, b, NT))
                transposed(ps, lambda t: nat[:, t, :]).then_inc(single_filled, 1)
                side(RET)
                pe.wait_ge(aoT_ready, count(aoT_ready, b, 1))
                output(b, S_WO2, wo2, CM)
                side(RET + 1)
                single(b, S_XF)
                pe.wait_ge(xf_ready, count(xf_ready, b, 1))
                transposed(ps, lambda t: nat[:, t, :]).then_inc(single_filled, 1)

            def back(b, part):
                def up(u, w, src, blocks):
                    n = w.shape[-1] // blocks
                    for m in range(n // 128):
                        dst = expert(b, u + m)
                        for k in range(blocks):
                            last = nc.tensor.matmul(dst[:, :], w[:, k * n + m * 128:k * n + (m + 1) * 128],
                                                    src(k), start=k == 0, stop=k == blocks - 1)
                        last.then_inc(expert_filled, 1)

                if part == 0:
                    pe.wait_ge(xfT_ready, count(xfT_ready, b, 1))
                    dst = expert(b, X_GATE)
                    for t in range(NT):
                        last = nc.tensor.matmul(dst[:, t * E:(t + 1) * E], xfT[:, t * 128:(t + 1) * 128], ww["w_gate"][:],
                                                start=True, stop=True)
                    last.then_inc(expert_filled, 1)
                if part in (1, 2):
                    m = part - 1
                    for n, w in enumerate(("w_g1", "w_u1")):
                        dst = expert(b, X_E1 + 2 * m + n)
                        nc.tensor.matmul(dst[:, :], ww[w][:, m * 128:(m + 1) * 128], xfT[:, :], start=True, stop=True)\
                            .then_inc(expert_filled, 1)
                if part == 3:
                    up(X_L1, ww["w_l1"], lambda k: xfT[:, :], 1)
                    up(X_D3, ww["w_d3"], lambda k: xfT[:, :], 1)
                if part == 4:
                    pe.wait_ge(h_ready, count(h_ready, b, 4))
                    up(X_L2, ww["w_l2"], lambda k: hA[:, k, :], 2)
                if part == 5:
                    pe.wait_ge(h_ready, count(h_ready, b, 5))
                    up(X_U3, ww["w_u3"], lambda k: h3a, 1)
                if part == 6:
                    pe.wait_ge(h_ready, count(h_ready, b, 7))
                    up(X_L3, ww["w_l3"], lambda k: hB[:, k, :], 2)
                if part == 7:
                    up(X_U0, ww["w_u0"], lambda k: xfT[:, :], 1)
            def down(b, t):
                pe.wait_ge(h_ready, count(h_ready, b, 13))
                pe.wait_ge(h1_ready, count(h1_ready, b, 2))
                dst = expert(b, X_DN + t)
                for e, (h, w) in enumerate(((h0, "w_dn0"), (h1, "w_dn1"), (hA, "w_dn2"), (h3, "w_dn3"))):
                    for k in range(2):
                        last = nc.tensor.matmul(dst[:, e * CM:(e + 1) * CM], h[:, k, t * 128:(t + 1) * 128],
                                                ww[w][:, k * CM:(k + 1) * CM], start=k == 0, stop=k == 1)
                last.then_inc(expert_filled, 1)

            def ready():
                pe.wait_ge(loaded, 16 * (len(ww) - len(PROJECTION + ROTATION)))
                pe.wait_ge(consts_ready, N_CONSTS)

            pe.wait_ge(projection_loaded, 16 * len(PROJECTION))
            pe.wait_ge(stack_cleared, 1)
            run(pe, lead, front, attend, back, down, ready)

        @block.scalar
        def _(act):
            A_ = nc.scalar.activation
            x_v = A["x"].rearrange("b (t p) c -> b p t c", p=128)

            def high_parts(b, layer, s):
                src = qk[:, s].rearrange("p t (h d) -> p (t h) d", d=D)
                dst = stack[:, s].rearrange("p t h s -> p (t h) s")
                step = (1, 2)[s]
                dst = dst.rearrange("p a (r d) -> p a r d", d=D)[:, :, 0:step + 1:step, :]
                A_(dst, src.unsqueeze(2).broadcast_to([128, NT * H, 2, D]), ACT.Copy).then_inc(high_ready, 1)

            def unmasked(b, t):
                for g in (1, 3):
                    act.wait_ge(ring_filled, count(ring_filled, b, U_SC1 + G * t + g + 1))
                    if g == 1 and (t >= 2 or not first(b)):
                        act.wait_ge(weighed, count(weighed, b, t - 1))
                    A_(p1[:, t % 2, g], pr[(U_SC1 + G * t + g) % 4][:, :].rearrange("p (j n) -> p j n", j=J), ACT.Copy)\
                        .then_inc(p1_copied, 1)

            def lead(b, part):
                if part == -1:
                    if not first(b):
                        act.wait_ge(xn_ready, count(xn_ready, b, 0))
                        act.wait_ge(x_kept, count(x_kept, b, 0))
                    act.dma_start(x_in[:], x_v[b]).then_inc(x_loaded, 16)
                if part == 2:
                    act.wait_ge(lead_filled, count(lead_filled, b, L_XN + 1))
                    A_(chT[:, :], px[L_XN % 2][:, :], ACT.Copy).then_inc(xnT_ready, 1)
                if part in (3, 4):
                    if part == 3 and not first(b):
                        act.wait_ge(down_read, count(down_read, b - 2, NT))
                    for t in (0, 1) if part == 3 else (2, 3):
                        act.wait_ge(lead_filled, count(lead_filled, b, L_QKV + t + 1))
                        src = px[(L_QKV + t) % 2]
                        A_(raw[:, t, :], src[:, 0:2 * C], ACT.Copy)
                        A_(v1[:, t, :], src[:, 2 * C:3 * C], ACT.Copy).then_inc(v_ready, 1)
                if part == 7:
                    act.wait_ge(qk_ready, count(qk_ready, b, 1))
                    high_parts(b, 0, 0)
                    act.wait_ge(lead_filled, count(lead_filled, b, L_QT + 1))
                    A_(qT, px[L_QT % 2][:, :], ACT.Copy).then_inc(qT_ready, 1)
                if part == 8:
                    high_parts(b, 0, 1)
                if part in (10, 11, 12, 13):
                    s, g = (part - 10) // 2, 2 * ((part - 10) % 2)
                    u = L_STK + G * s + g
                    act.wait_ge(lead_filled, count(lead_filled, b, u + 1))
                    A_((qs1, ks1)[s][:, g, :], px[u % 2][:, :], ACT.Copy).then_inc(stack_a, 1)
                if part == 14:
                    act.wait_ge(lead_filled, count(lead_filled, b, L_CROSS + 1))
                    A_(cross[:, 128:T], px[L_CROSS % 2][:, 128:T], ACT.Copy).then_inc(cross_ready, 1)
                if part >= RET:
                    unmasked(b, part - RET)

            def front(b, side):
                side("start")
                unmasked(b, 2)
                unmasked(b, 3)
                side("scored")
                side("weighed")
                for t in range(NT):
                    act.wait_ge(ring_filled, count(ring_filled, b, U_N1 + t + 1))
                    src = pr[(U_N1 + t) % 4][:, :]
                    view = bass.AP(tensor=src.tensor, offset=src.offset, ap=[list(src.ap[0]), [SW, G], [128 + D, J], [1, D]])
                    A_(o1[:, t, :].rearrange("p (g j d) -> p g j d", g=G, j=J), view, ACT.Copy).then_inc(o1_copied, 1)
                act.wait_ge(centred, count(centred, b, 1))
                A_(sq[:, :, 0:C], o1[:, :, :], ACT.Square).then_inc(squared, 1)
                side("spread")
                act.wait_ge(single_filled, count(single_filled, b, S_ON + 1))
                A_(chT[:, :], ps[:, :], ACT.Identity, scale=ww["w_gn"][:, 0:1], bias=ww["w_gn"][:, 1:2])\
                    .then_inc(chT_ready, 1)
                side("projected")
                act.wait_ge(single_filled, count(single_filled, b, S_H + 1))
                A_(chT[:, :], ps[:, :], ACT.Copy, scale=ww["w_n12"][:, 0:1]).then_inc(chT_ready, 1)
                for t in range(NT):
                    act.wait_ge(ring_filled, count(ring_filled, b, U_QKV2 + t + 1))
                    src = pr[(U_QKV2 + t) % 4]
                    A_(sq[:, t, :], src[:, 0:2 * C], ACT.Square)
                    A_(v2h[:, t, :, 0:D], src[:, 2 * C:3 * C].rearrange("p (h d) -> p h d", d=D),
                       ACT.Copy).then_inc(v_ready, 1)
                side("normed")
                act.wait_ge(k2_ready, count(k2_ready, b, 1))
                high_parts(b, 1, 1)
                act.wait_ge(qkv2_read, count(qkv2_read, b, NT))
                high_parts(b, 1, 0)
                act.wait_ge(single_filled, count(single_filled, b, S_K0 + 1))
                for j in (2, 3):
                    i = A_(kx[32 * j:32 * j + 32, 0, j, :], ps[32 * j:32 * j + 32, :], ACT.Copy)
                i.then_inc(k0_spread_a, 1)
                A_(ks[:, 0, :], ps[:, :], ACT.Copy).then_inc(stack_a, 1)
                for n, dst in enumerate((ks, qs)):
                    for g in (0, 2)[1 - n:]:
                        u = U_STK2 + G * n + g
                        act.wait_ge(ring_filled, count(ring_filled, b, u + 1))
                        A_(dst[:, g, :], pr[u % 4][:, :], ACT.Copy).then_inc(stack_a, 1)

            def attend(b, side):
                for at, (kind, g, n) in enumerate(ORDER):
                    if kind == "exp":
                        kt, qt = EXP_UNITS[n]
                        act.wait_ge(ring_filled, count(ring_filled, b, U_AB + at + 1))
                        if qt == kt:
                            act.wait_ge(weighed, count(weighed, b, NT + (NT * g - 1, max(NT * g - 2, 0), NT * g + 1, NT * g)[kt]))
                        A_(p2(kt)[:, :, (qt - kt) * 128:(qt - kt + 1) * 128],
                           pr[(U_AB + at) % 4][:, :].rearrange("p (j n) -> p j n", j=J), ACT.Exp, scale=float(D) ** -0.5)\
                            .then_inc(exp_done, 1)
                    if at in MT_AT:
                        gm = MT_AT[at]
                        act.wait_ge(single_filled, count(single_filled, b, S_MT + gm + 1))
                        if gm == 0:
                            act.wait_ge(down_read, count(down_read, b, 0))
                        if gm >= 2:
                            act.wait_ge(shift_ready[gm % 2], count(shift_ready[gm % 2], b, J * 16))
                        A_(mT[:, gm % 2, :], ps[0:J, :], ACT.Copy).then_inc(mT_ready, 1)
                    beside(at, side)
                act.wait_ge(single_filled, count(single_filled, b, S_AO + 1))
                A_(chT[:, :], ps[:, :], ACT.Copy).then_inc(aoT_ready, 1)
                side(RET)
                act.wait_ge(down_read, count(down_read, b, 0))
                act.wait_ge(y_ready, count(y_ready, b, 1))
                for t in range(NT):
                    i = A_(cosp[:, t, 0:C], z[:, t, :], ACT.Square, accum_out=gsum[:, 0, t:t + 1])
                i.then_inc(ysq_ready, 1)
                act.wait_ge(single_filled, count(single_filled, b, S_XF + 1))
                A_(xfT[:, :], ps[:, :], ACT.Copy, scale=ww["w_n12"][:, 1:2]).then_inc(xfT_ready, 1)
                side(RET + 1)

            def back(b, part):
                def hidden(u, dst, func):
                    act.wait_ge(expert_filled, count(expert_filled, b, u + 1))
                    A_(dst, px[u % 2][:, :], func).then_inc(h_ready, 1)

                if part == 7:
                    act.wait_ge(wts_ready, count(wts_ready, b, 1))
                if part == 0:
                    act.wait_ge(logits_ready, count(logits_ready, b, 1))
                    A_(gl[:, 3], gl[:, 2], ACT.Exp).then_inc(gexp_ready, 1)
                if part in (1, 2):
                    hidden(X_E1 + 2 * (part - 1), sil[:, part - 1, :], ACT.Silu)
                if part == 3:
                    hidden(X_L1, hA[:, 0, :], ACT.Gelu)
                    hidden(X_L1 + 1, hA[:, 1, :], ACT.Gelu)
                    hidden(X_D3, h3a, ACT.Gelu)
                if part == 4:
                    act.wait_ge(h1_ready, count(h1_ready, b, 2))
                    hidden(X_L2, hB[:, 0, :], ACT.Gelu)
                    hidden(X_L2 + 1, hB[:, 1, :], ACT.Gelu)
                if part == 5:
                    hidden(X_U3, h3[:, 0, :], ACT.Gelu)
                    hidden(X_U3 + 1, h3[:, 1, :], ACT.Gelu)
                if part == 6:
                    hidden(X_L3, hA[:, 0, :], ACT.Gelu)
                    hidden(X_L3 + 1, hA[:, 1, :], ACT.Gelu)
                if part == 7:
                    hidden(X_U0, h0[:, 0, :], ACT.Gelu)
                    hidden(X_U0 + 1, h0[:, 1, :], ACT.Gelu)

            def down(b, t):
                act.wait_ge(expert_filled, count(expert_filled, b, X_DN + t + 1))
                for e in range(E):
                    i = A_(weighted[:, t, e, :], px[(X_DN + t) % 2][:, e * CM:(e + 1) * CM], ACT.Copy,
                           scale=wts[:, t, e:e + 1])
                i.then_inc(down_read, 1)

            def ready():
                act.wait_ge(loaded, 16 * (len(ww) - len(PROJECTION + ROTATION)))
                act.wait_ge(consts_ready, N_CONSTS)

            run(act, lead, front, attend, back, down, ready)

        @block.vector
        def _(dve):
            V = nc.vector
            done = {}

            def step(b, ins, s=front_step):
                ins.then_inc(s, 1)
                done[s] = done.get(s, 0) + 1
                dve.wait_ge(s, count(s, b, done[s]))

            def ring(b, u):
                dve.wait_ge(ring_filled, count(ring_filled, b, u + 1))
                return pr[u % 4]

            def rsqrt(b, n, s=front_step):
                v, i, y, t = rs_v[:, 0:n], rs_i[:, 0:n], rs_y[:, 0:n], rs_t[:, 0:n]
                step(b, V.tensor_scalar(i, v.bitcast(i32), 1, None, ALU.logical_shift_right), s)
                step(b, V.tensor_scalar(y.bitcast(i32), i, -1, RSQRT_SEED, ALU.mult, ALU.add), s)
                for _ in range(3):
                    step(b, V.tensor_tensor(t, y, y, ALU.mult), s)
                    step(b, V.scalar_tensor_tensor(t, t, -0.5, v, ALU.mult, ALU.mult), s)
                    step(b, V.scalar_tensor_tensor(y, t, 1.5, y, ALU.add, ALU.mult), s)

            def moments(b, src, dst, s=front_step):
                for t in range(NT):
                    i = V.bn_stats(stats[:, t, :], src[:, t, :])
                step(b, i, s)
                apart(dve)
                for t in range(NT):
                    i = V.bn_aggr(dst[:, t, :], stats[:, t, :])
                step(b, i, s)

            def low_parts(b, layer, s):
                dve.wait_ge(high_ready, count(high_ready, b, 2 * layer + turn(layer, s) + 1))
                src = qk[:, s].rearrange("p t (h d) -> p (t h) d", d=D)
                st = stack[:, s].rearrange("p t h s -> p (t h) s")
                at = (2 * D, D)[s]
                V.tensor_tensor(st[:, :, at:at + D], src, st[:, :, 0:D].bitcast(f32), ALU.subtract)\
                    .then_inc(low_ready, 1)

            def lead(b, part):
                if part == 0:
                    done[lead_step] = 0
                    dve.wait_ge(x_loaded, count(x_loaded, b, 16))
                    moments(b, x_in, mv_in, lead_step)
                if part == 1:
                    step(b, V.tensor_scalar(rs_v[:, 0:NT], mv_in[:, :, 1], EPS_LN, None, ALU.add), lead_step)
                    rsqrt(b, NT, lead_step)
                    if not first(b):
                        dve.wait_ge(xnT_ready, count(xnT_ready, b, 0))
                    for t in range(NT):
                        i = V.tensor_scalar(xn[:, t, :], x_in[:, t, :], mv_in[:, t, 0:1], rs_y[:, t:t + 1],
                                            ALU.subtract, ALU.mult)
                    i.then_inc(xn_ready, 1)
                    assert done[lead_step] == LEAD_STEPS, done
                if part in (4, 5):
                    if part == 4 and first(b):
                        dve.wait_ge(rotation_loaded, 16 * len(ROTATION))
                    m = part - 4
                    dve.wait_ge(v_ready, count(v_ready, b, 2 * m + 2))
                    tt = slice(2 * m, 2 * m + 2)
                    halves = lambda ap, k: ap.rearrange("p t (h d) -> p t h d", d=D)[:, :, :, 4 * k:4 * k + 4]
                    for k in range(2):
                        i = V.tensor_tensor(halves(sinp[:, tt, :], k), halves(raw[:, tt, :], 1 - k),
                                            halves(sin_t[:, tt, :], k), ALU.mult)
                    i.then_inc(sin_ready, 1)
                if part in (7, 8, 9):
                    t = part - 7
                    dve.wait_ge(lead_filled, count(lead_filled, b, L_ST + t + 1))
                    if t == 2:
                        dve.wait_ge(state_ready, count(state_ready, b, 1))
                    dst = state[:, 0, :] if t == 0 else state_in[:, :]
                    V.tensor_tensor(dst, px[(L_ST + t) % 2][:, 0:C], ww["t_state"][:], ALU.mult).then_inc(state_read, 1)
                    if t:
                        dve.wait_ge(state_read, count(state_read, b, t + 1))
                        V.scalar_tensor_tensor(state[:, t, :], state[:, t - 1, :], ww["t_g128"][:, 0:1],
                                               state_in[:, :], ALU.mult, ALU.add).then_inc(state_ready, 1)
                if part in (10, 11, 12, 13):
                    s, g = (part - 10) // 2, 2 * ((part - 10) % 2) + 1
                    u = L_STK + G * s + g
                    dve.wait_ge(lead_filled, count(lead_filled, b, u + 1))
                    V.tensor_copy((qs1, ks1)[s][:, g, :], px[u % 2][:, :]).then_inc(stack_b, 1)
                if part == RET:
                    dve.wait_ge(cross_ready, count(cross_ready, b, 1))
                    masked(b, 0)
                if part == RET + 1:
                    masked(b, 1)
                    add_states(b, 0)

            def masked(b, t):
                for g in (0, 2):
                    src = ring(b, U_SC1 + G * t + g)
                    if g == 0 and (t >= 2 or not first(b)):
                        dve.wait_ge(weighed, count(weighed, b, t - 1))
                    V.tensor_tensor(p1[:, t % 2, g], src[:].rearrange("p (j n) -> p j n", j=J),
                                    tri[:].unsqueeze(1).broadcast_to([128, J, 128]), ALU.mult)\
                        .then_inc(p1_ready, 1)

            def add_states(b, t):
                dve.wait_ge(weighed, count(weighed, b, t + 1))
                V.tensor_tensor(oT[:, t, :].rearrange("p (j n) -> p j n", j=J),
                                po[:].rearrange("p (j n) -> p j n", j=J),
                                cross[:, t * 128:(t + 1) * 128].unsqueeze(1).broadcast_to([128, J, 128]),
                                ALU.add).then_inc(oT_ready, 1)

            def front(b, side):
                done[front_step] = 0
                side("start")
                masked(b, 2)
                add_states(b, 1)
                masked(b, 3)
                add_states(b, 2)
                side("scored")
                add_states(b, 3)
                side("weighed")
                dve.wait_ge(o1_copied, count(o1_copied, b, NT))
                step(b, V.tensor_reduce(red[:, 0].rearrange("p t h -> p (t h)"), heads(o1[:]), AX.X, ALU.add))
                V.scalar_tensor_tensor(heads(o1[:]), bc(red[:, 0].rearrange("p t h -> p (t h)"), D), -1.0 / D,
                                       heads(o1[:]), ALU.mult, ALU.add).then_inc(centred, 1)
                dve.wait_ge(squared, count(squared, b, 1))
                step(b, V.tensor_reduce(red[:, 1], sq[:, :, 0:C].rearrange("p t (h d) -> p t h d", d=D), AX.X, ALU.add))
                step(b, V.tensor_scalar(rs_v[:, 0:NT * H], red[:, 1].rearrange("p t h -> p (t h)"), 1.0 / D, EPS_LN,
                                        ALU.mult, ALU.add))
                rsqrt(b, NT * H)
                V.tensor_tensor(heads(nat[:]), heads(o1[:]), bc(rs_y[:, 0:NT * H], D), ALU.mult).then_inc(nat_ready, 1)
                side("spread")
                if not first(b):
                    dve.wait_ge(base_ready, count(base_ready, b, 0))
                dve.wait_ge(single_filled, count(single_filled, b, S_WO1 + 1))
                dve.wait_ge(x_kept, count(x_kept, b, 1))
                V.tensor_tensor(x1[:], x[:], ps[:].rearrange("p (t c) -> p t c", t=NT), ALU.add).then_inc(x1_ready, 1)
                dve.wait_ge(x1_ready, count(x1_ready, b, 1))
                moments(b, x1, mv)
                step(b, V.tensor_scalar(rs_v[:, 0:NT], mv[:, :, 1], EPS_LN, None, ALU.add))
                step(b, V.scalar_tensor_tensor(rs_v[:, NT:2 * NT], rs_v[:, 0:NT], EPS_RMS, mv[:, :, 1],
                                               ALU.mult, ALU.add))
                rsqrt(b, 2 * NT)
                r1, r12 = rs_y[:, 0:NT], rs_y[:, NT:2 * NT]
                for t in range(NT):
                    i = V.tensor_scalar(nat[:, t, :], x1[:, t, :], mv[:, t, 0:1], r12[:, t:t + 1],
                                        ALU.subtract, ALU.mult)
                i.then_inc(nat_ready, 1)
                for t in range(NT):
                    i = V.tensor_scalar(z[:, t, :], x1[:, t, :], mv[:, t, 0:1], r1[:, t:t + 1],
                                        ALU.subtract, ALU.mult)
                step(b, i)
                side("projected")
                for t in range(NT):
                    dve.wait_ge(v_ready, count(v_ready, b, NT + t + 1))
                    i = V.tensor_reduce(rs_t[:, 2 * H * t:2 * H * (t + 1)], sq[:, t, :].rearrange("p (h d) -> p h d", d=D),
                                        AX.X, ALU.add)
                step(b, i)
                step(b, V.tensor_scalar(rs_v[:, :], rs_t[:, :], 1.0 / D, EPS_RMS, ALU.mult, ALU.add))
                rsqrt(b, 2 * NT * H)
                ry = rs_y[:].rearrange("p (t s h) -> p t s h", t=NT, s=2)
                for t in range(NT):
                    i = V.tensor_tensor(qk[:, 1, t, :].rearrange("p (h d) -> p h d", d=D),
                                        pr[(U_QKV2 + t) % 4][:, C:2 * C].rearrange("p (h d) -> p h d", d=D),
                                        bc(ry[:, t, 1, :], D), ALU.mult)
                i.then_inc(k2_ready, 1)
                step(b, V.tensor_tensor(rw.rearrange("p t (h d) -> p t h d", d=D), bc(ry[:, :, 0, :], D),
                                        wqk[:].unsqueeze(1).unsqueeze(1).broadcast_to([128, NT, H, D]), ALU.mult))
                for t in range(NT):
                    V.tensor_tensor(qk[:, 0, t, :], pr[(U_QKV2 + t) % 4][:, 0:C], rw[:, t, :], ALU.mult)\
                        .then_inc(qkv2_read, 1)
                dve.wait_ge(k2_ready, count(k2_ready, b, 1))
                low_parts(b, 1, 1)
                dve.wait_ge(qkv2_read, count(qkv2_read, b, NT))
                low_parts(b, 1, 0)
                src = ring(b, U_STK2)
                for j in (0, 1):
                    i = V.tensor_copy(kx[32 * j:32 * j + 32, 0, j, :], src[32 * j:32 * j + 32, :])
                i.then_inc(k0_spread_b, 1)
                for n, dst in enumerate((ks, qs)):
                    for g in (1, 3):
                        V.tensor_copy(dst[:, g, :], ring(b, U_STK2 + G * n + g)[:, :]).then_inc(stack_b, 1)
                side("normed")
                assert done[front_step] == FRONT_STEPS, done

            def attend(b, side):
                done[tail_step] = 0
                go = lambda ins: step(b, ins, tail_step)

                def take_output(g):
                    dve.wait_ge(weighed, count(weighed, b, NT + NT * (g + 1)))
                    V.tensor_copy(oT[:, g, :], po[:]).then_inc(oT_ready, 1)

                for at, (kind, g, n) in enumerate(ORDER):
                    if kind == "max":
                        qt, kt = MAX_UNITS[n]
                        V.tensor_reduce(mxp[:, qt, :, kt], ring(b, U_AB + at)[:].rearrange("p (j n) -> p j n", j=J),
                                        AX.X, ALU.max).then_inc(max_read, 1)
                        if n == NU - 1:
                            dve.wait_ge(max_read, count(max_read, b, NU * (g + 1)))
                            go(V.tensor_reduce(mxm[:].rearrange("p t j -> p (t j)"), mxp[:].rearrange("p t j k -> p (t j) k"),
                                               AX.X, ALU.max))
                            V.tensor_scalar(mneg[:, g], mxm[:], -1.0, None, ALU.mult).then_inc(mneg_ready, 1)
                    if OT_AT.get(at) == 0 and not first(b):
                        dve.wait_ge(out_ready, count(out_ready, b, 0))
                    if at in OT_AT:
                        take_output(OT_AT[at])
                    beside(at, side)
                take_output(G - 1)
                for t in range(NT):
                    src = ring(b, U_N2 + t)[:].rearrange("p (h s) -> p h s", s=SW)
                    go(V.reciprocal(rcp[:, t, :], src[:, :, D]))
                    V.tensor_tensor(nat[:, t, :].rearrange("p (h d) -> p h d", d=D), src[:, :, 0:D], bc(rcp[:, t, :], D),
                                    ALU.mult).then_inc(n2_read, 1)
                side(RET)
                dve.wait_ge(single_filled, count(single_filled, b, S_WO2 + 1))
                V.tensor_tensor(z[:, :, M0:C], z[:, :, M0:C], ps[:, 0:NT * CM].rearrange("p (t c) -> p t c", t=NT),
                                ALU.add).then_inc(y_ready, 1)
                dve.wait_ge(ysq_ready, count(ysq_ready, b, 1))
                go(V.tensor_scalar(rs_v[:, 0:NT], gsum[:, 0, :], 1.0 / C, EPS_RMS, ALU.mult, ALU.add))
                rsqrt(b, NT, tail_step)
                for t in range(NT):
                    i = V.tensor_scalar(nat[:, t, :], z[:, t, :], rs_y[:, t:t + 1], None, ALU.mult)
                i.then_inc(xf_ready, 1)
                side(RET + 1)
                assert done[tail_step] == TAIL_STEPS, done

            def back(b, part):
                go = lambda ins: step(b, ins, back_step)
                if part == 0:
                    done[back_step] = 0
                    dve.wait_ge(expert_filled, count(expert_filled, b, X_GATE + 1))
                    logits = px[X_GATE % 2][:, 0:NT * E].rearrange("p (t e) -> p t e", e=E)
                    V.tensor_scalar(gl[:, 0], logits, 0.0, FMAX, ALU.max, ALU.min)
                    V.tensor_scalar(gl[:, 1], logits, 0.0, -FMAX, ALU.min, ALU.max).then_inc(logits_read, 1)
                    dve.wait_ge(logits_read, count(logits_read, b, 1))
                    go(V.tensor_tensor(gl[:, 4], gl[:, 0], gl[:, 1], ALU.add))
                    go(V.tensor_reduce(bsum[:, 0, :], gl[:, 4], AX.X, ALU.max))
                    V.tensor_tensor(gl[:, 2], gl[:, 4], bc(bsum[:, 0, :], E), ALU.subtract).then_inc(logits_ready, 1)
                if part == 3:
                    dve.wait_ge(gexp_ready, count(gexp_ready, b, 1))
                    go(V.tensor_reduce(bsum[:, 1, :], gl[:, 3], AX.X, ALU.add))
                    go(V.reciprocal(bsum[:, 2, :], bsum[:, 1, :]))
                    go(V.tensor_tensor(gl[:, 5], gl[:, 3], bc(bsum[:, 2, :], E), ALU.mult))
                    pf = gl[:, 5].unsqueeze(2).broadcast_to([128, NT, E, E])
                    pe_ = bc(gl[:, 5], E)
                    V.tensor_tensor(beats[:, 0], pf, pe_, ALU.is_gt)
                    go(V.tensor_tensor(beats[:, 1], pf, pe_, ALU.is_ge))
                    go(V.tensor_tensor(beats[:, 2], beats[:, 1], beats[:, 0], ALU.subtract))
                    first = ww["t_first"][:].unsqueeze(1).broadcast_to([128, NT, E * E])
                    flat = lambda k: beats[:, k].rearrange("p t e f -> p t (e f)")
                    go(V.tensor_tensor(flat(1), flat(2), first, ALU.mult))
                    go(V.tensor_tensor(flat(2), flat(0), flat(1), ALU.add))
                    go(V.tensor_reduce(gl[:, 6], beats[:, 2], AX.X, ALU.add))
                    go(V.tensor_scalar(gl[:, 7], gl[:, 6], 1.5, None, ALU.is_lt))
                    go(V.tensor_tensor(gl[:, 6], gl[:, 7], gl[:, 5], ALU.mult))
                    go(V.tensor_reduce(bsum[:, 0, :], gl[:, 6], AX.X, ALU.add))
                    go(V.tensor_scalar(bsum[:, 1, :], bsum[:, 0, :], 1e-8, None, ALU.add))
                    go(V.reciprocal(bsum[:, 2, :], bsum[:, 1, :]))
                    V.tensor_tensor(wts[:], gl[:, 6], bc(bsum[:, 2, :], E), ALU.mult).then_inc(wts_ready, 1)
                    assert done[back_step] == BACK_STEPS, done
                if part in (1, 2):
                    m = part - 1
                    dve.wait_ge(expert_filled, count(expert_filled, b, X_E1 + 2 * m + 2))
                    dve.wait_ge(h_ready, count(h_ready, b, 1 + m))
                    V.tensor_tensor(h1[:, m, :], px[(X_E1 + 1) % 2][:], sil[:, m, :], ALU.mult).then_inc(h1_ready, 1)
            def ready():
                dve.wait_ge(loaded, 16 * (len(ww) - len(PROJECTION + ROTATION)))
                V.tensor_copy(idb[:], ident[:]).then_inc(consts_ready, 1)
                V.tensor_copy(negb[:], neg32[:].unsqueeze(1).broadcast_to([128, J, 128])).then_inc(consts_ready, 1)
                V.tensor_scalar(negkb[:], tri[:].unsqueeze(1).broadcast_to([128, J, 128]), 1.0, -NEG, ALU.subtract, ALU.mult)
                V.tensor_tensor(wqk[:], ww["w_qk"][:, 0:D], ww["w_qk"][:, D:2 * D], ALU.mult).then_inc(consts_ready, 1)
                V.memset(mxp[:], NEG)
                V.memset(v2[:], 0.0).then_inc(consts_ready, 1)
                dve.wait_ge(consts_ready, N_CONSTS - 1)
                V.memset(v2h[:, :, :, D:D + 1], 1.0).then_inc(consts_ready, 1)
                V.memset(wts[:], 0.0).then_inc(down_read, NT)
                dve.wait_ge(consts_ready, N_CONSTS)

            run(dve, lead, front, attend, back, lambda b, t: None, ready)

        @block.gpsimd
        def _(pool):
            Q = nc.gpsimd

            def masked(b, t):
                for n in range(2):
                    pool.wait_ge(p1_copied, count(p1_copied, b, 2 * t + n + 1))
                    apart(pool)
                    half = p1[:, t % 2, 2 * n + 1]
                    Q.affine_select(out=half, in_=half, compare_op=ALU.is_ge, fill=0.0, base=0,
                                    pattern=[[0, J], [1, 128]], channel_multiplier=-1).then_inc(p1_masked, 1)

            def down(b, t):
                pool.wait_ge(down_read, count(down_read, b, t + 1))
                Q.tensor_tensor(weighted[:, t, 0:2, :], weighted[:, t, 0:2, :], weighted[:, t, 2:4, :], ALU.add)\
                    .then_inc(sum_step, 1)
                pool.wait_ge(sum_step, count(sum_step, b, 2 * t + 1))
                Q.tensor_tensor(weighted[:, t, 0, :], weighted[:, t, 0, :], weighted[:, t, 1, :], ALU.add)\
                    .then_inc(sum_step, 1)
                pool.wait_ge(sum_step, count(sum_step, b, 2 * t + 2))
                Q.tensor_tensor(yout[:, t, M0:C], yout[:, t, M0:C], weighted[:, t, 0, :], ALU.add).then_inc(out_ready, 1)

            def lead(b, part):
                if part == 1:
                    pool.wait_ge(x_loaded, count(x_loaded, b, 16))
                    if not first(b):
                        pool.wait_ge(x1_ready, count(x1_ready, b, 0))
                    apart(pool)
                    Q.tensor_copy(x[:], x_in[:]).then_inc(x_kept, 1)
                if part == 4:
                    pool.wait_ge(v_ready, count(v_ready, b, NT))
                    Q.tensor_tensor(cosp, raw, cos_t, ALU.mult).then_inc(cos_ready, 1)
                if part == 6:
                    pool.wait_ge(cos_ready, count(cos_ready, b, 1))
                    pool.wait_ge(sin_ready, count(sin_ready, b, 2))
                    Q.tensor_tensor(qk[:].rearrange("p s t c -> p t s c"), cosp.rearrange("p t (s c) -> p t s c", s=2),
                                    sinp.rearrange("p t (s c) -> p t s c", s=2), ALU.add).then_inc(qk_ready, 1)
                if part in (7, 8):
                    s = part - 7
                    pool.wait_ge(high_ready, count(high_ready, b, s + 1))
                    src = qk[:, s].rearrange("p t (h d) -> p (t h) d", d=D)
                    st = stack[:, s].rearrange("p t h s -> p (t h) s")
                    at = (2 * D, D)[s]
                    Q.tensor_tensor(st[:, :, at:at + D], src, st[:, :, 0:D].bitcast(f32), ALU.subtract)\
                        .then_inc(low_ready, 1)
                if part >= RET:
                    masked(b, part - RET)

            def attend(b, side):
                for t in range(NT):
                    side(DOWN + t)
                for part in range(2, RET):
                    side(part)
                side(RET)
                pool.wait_ge(y_ready, count(y_ready, b, 1))
                pool.wait_ge(out_stored, count(out_stored, b, 0))
                Q.tensor_tensor(yout[:], x1[:], z[:], ALU.add).then_inc(base_ready, 1)
                pool.wait_ge(base_ready, count(base_ready, b, 1))
                side(RET + 1)

            def front(b, side):
                masked(b, 2)
                masked(b, 3)
                for place in FFN_AT:
                    side(place)

            Q.memset(stack[:].bitcast(f32), 0.0).then_inc(pool_made, 1)
            pool.wait_ge(pool_made, 1)
            Q.memset(stack[:, 1, :, :, SHIFT:SHIFT + 1].bitcast(f32), 1.0).then_inc(stack_cleared, 1)
            Q.memset(cross[:, 0:128], 0.0).then_inc(consts_ready, 1)
            Q.memset(yout[:], 0.0).then_inc(out_stored, 16)
            Q.memset(qx[:].bitcast(f32), 0.0).then_inc(consts_ready, 1)
            Q.memset(kx[:].bitcast(f32), 0.0).then_inc(consts_ready, 1)
            pool.wait_ge(rotation_loaded, 16 * len(ROTATION))
            pool.wait_ge(stack_cleared, 1)
            run(pool, lead, front, attend, lambda b, part: None, down, lambda: None)

        @block.sync
        def _(sp):
            out_v = A["out"].rearrange("b (t p) c -> b p t c", p=128)

            def expand_q(b, layer, src, some):
                for j in range(J):
                    sp.dma_start(qx[32 * j:32 * j + 32, some, j, :].bitcast(f32),
                                 src[32 * j:32 * j + 32, some, :].bitcast(f32)).then_inc(qx_ready, 16)

            def expand_k(b, g):
                read, n = stack_read(1, 1, g)
                sp.wait_ge(read, count(read, b, n))
                if g >= 2:
                    apart(sp)
                    sp.wait_ge(ring_filled, count(ring_filled, b, U_AB + PLACE["max", g - 2, NU - 1] + 1))
                for j in range(J):
                    sp.dma_start(kx[32 * j:32 * j + 32, g % 2, j, :].bitcast(f32),
                                 ks[32 * j:32 * j + 32, g, :].bitcast(f32)).then_inc(kx_ready[g % 2], 16)

            def shift(b, g):
                sp.wait_ge(mT_ready, count(mT_ready, b, g + 1))
                apart(sp)
                sp.wait_ge(qx_ready, count(qx_ready, b, 12 * 16))
                for j in range(J):
                    sp.dma_start(qx[32 * j + SHIFT:32 * j + SHIFT + 1, g, j, :].bitcast(f32),
                                 mT[j:j + 1, g % 2, :].bitcast(f32)).then_inc(shift_ready[g % 2], 16)

            def lead(b, part):
                if part == RET:
                    sp.wait_ge(stack_a, count(stack_a, b, 2))
                    sp.wait_ge(stack_b, count(stack_b, b, 2))
                    for end in (G - 1, G):
                        if not first(b):
                            apart(sp)
                            sp.wait_ge(ring_filled, count(ring_filled, b - 1, U_AB + PLACE["exp", end - 1, NU - 1] + 1))
                        expand_q(b, 0, qs1, slice(0, G - 1) if end < G else slice(G - 1, G))

            def front(b, side):
                expand_k(b, 1)
                sp.wait_ge(stack_a, count(stack_a, b, 2 * G))
                sp.wait_ge(stack_b, count(stack_b, b, 2 * G))
                expand_q(b, 1, qs, slice(0, G))

            def attend(b, side):
                side(DOWN + NT - 1)
                expand_k(b, 2)
                shift(b, 0)
                expand_k(b, 3)
                for g in range(1, G):
                    shift(b, g)
                side(RET)

            def down(b, t):
                if t == NT - 1:
                    sp.wait_ge(out_ready, count(out_ready, b, NT))
                    sp.dma_start(out_v[b], yout[:]).then_inc(out_stored, 16)

            for name in PROJECTION:
                sp.dma_start(ww[name][:], A[name]).then_inc(projection_loaded, 16)
            for name in ROTATION:
                sp.dma_start(ww[name][:], A[name]).then_inc(rotation_loaded, 16)
            for name, dst in ww.items():
                if name not in PROJECTION + ROTATION:
                    sp.dma_start(dst[:], A[name]).then_inc(loaded, 16)
            run(sp, lead, front, attend, lambda b, part: None, down, lambda: sp.wait_ge(consts_ready, N_CONSTS))
            sp.wait_ge(out_stored, count(out_stored, B, 0))


def kernel(**inputs):
    import numpy as _np
    import concourse.bacc as _bacc
    from concourse import mybir as _mybir
    from concourse.bass_utils import run_bass_kernel_spmd as _run

    I = {k: _np.asarray(v) for k, v in inputs.items()}
    a = lambda n: I["L0_attn_" + n]
    w = lambda n: I["L0_ffn_" + n]
    cat = _np.concatenate

    def blocks(m, n=None):
        m = m if n is None else m[:, n:]
        return m.reshape(-1, 128, m.shape[1]).transpose(1, 0, 2).reshape(128, -1)

    rows = lambda v: _np.broadcast_to(v[None, :], (128, v.shape[0]))
    arrays = {
        "x": a("x"),
        "w_qkv1": cat([a("Wq").T, a("Wk").T, a("Wv").T], 1),
        "w_o1": a("Wo").T,
        "w_gn": _np.stack([a("gn_weight"), a("gn_bias")], 1),
        "w_n12": _np.stack([w("n1_w"), w("n2_w")], 1),
        "w_qkv2": cat([w("wq").T, w("wk").T, w("wv").T], 1),
        "w_o2": w("wo").T[:, M0:],
        "w_qk": cat([rows(w("qn_w")), rows(w("kn_w"))], 1),
        "w_gate": w("gate_w").T,
        "w_u0": w("e0_up").T, "w_dn0": blocks(w("e0_down").T, M0),
        "w_g1": w("e1_w1").T, "w_u1": w("e1_w2").T, "w_dn1": blocks(w("e1_down").T, M0),
        "w_l1": w("e2_l1").T, "w_l2": blocks(w("e2_l2").T), "w_l3": blocks(w("e2_l3").T),
        "w_dn2": blocks(w("e2_l4").T, M0),
        "w_d3": w("e3_down").T, "w_u3": w("e3_up").T, "w_dn3": blocks(w("e3_out").T, M0),
    }
    arrays.update(tables())
    nc = _bacc.Bacc("TRN2", target_bir_lowering=False, num_devices=1)
    A, send = {}, {}
    for name, v in arrays.items():
        v = _np.ascontiguousarray(v)
        send[name + "_dram"] = v
        A[name] = nc.dram_tensor(name + "_dram", v.shape, _mybir.dt.from_np(v.dtype), kind="ExternalInput").ap()
    A["out"] = nc.dram_tensor("out_dram", (B, T, C), _mybir.dt.float32, kind="ExternalOutput").ap()
    build(nc, A)
    r = _run(nc, [send], core_ids=[0])
    return r.results[0]["out_dram"]
```
